# Optimizing a Trainium2 kernel written in Bass

```python
import numpy as np
import jax
import jax.numpy as jnp

def _softmax(x, axis=-1):
    return jax.nn.softmax(x, axis=axis)

def _gelu(x):
    return jax.nn.gelu(x, approximate=True)

def _silu(x):
    return jax.nn.silu(x)

def _sigmoid(x):
    return jax.nn.sigmoid(x)

def _layernorm(x, axis=-1, eps=1e-05):
    m = jnp.mean(x, axis=axis, keepdims=True)
    v = jnp.var(x, axis=axis, keepdims=True)
    return (x - m) / jnp.sqrt(v + eps)

def _scatter_add(tgt, idx, src, axis=0):
    return tgt.at[idx].add(src)

def _segment_sum(src, seg, n):
    return jax.ops.segment_sum(src, seg, n)
kernel_name = 'mk_recurrent_d2_jaxref_r8_edf77e'

def setup_inputs(seed: int=0):
    np.random.seed(seed)
    _w = jnp.asarray

    def _L0_attn_setup():
        import jax, jax.numpy as jnp
        import numpy as np
        import math
        EMBED = 128
        HEADS = 16
        HEAD_DIM = EMBED // HEADS
        B, N = (2, 256)
        key = jax.random.key(seed)
        ks = jax.random.split(key, 8)
        s = 1.0 / math.sqrt(EMBED)
        Wq = jax.random.uniform(ks[0], (EMBED, EMBED), jnp.float32, -s, s)
        bq = jax.random.uniform(ks[1], (EMBED,), jnp.float32, -s, s)
        Wk = jax.random.uniform(ks[2], (EMBED, EMBED), jnp.float32, -s, s)
        bk = jax.random.uniform(ks[3], (EMBED,), jnp.float32, -s, s)
        Wv = jax.random.uniform(ks[4], (EMBED, EMBED), jnp.float32, -s, s)
        bv = jax.random.uniform(ks[5], (EMBED,), jnp.float32, -s, s)
        Wp = jax.random.normal(ks[6], (HEAD_DIM, HEAD_DIM), jnp.float32)
        x = jax.random.normal(ks[7], (B, N, EMBED), jnp.float32)
        return {'x': x, 'Wq': Wq, 'bq': bq, 'Wk': Wk, 'bk': bk, 'Wv': Wv, 'bv': bv, 'Wp': Wp}
    _L0_attn_in = _L0_attn_setup()

    def _L0_ffn_setup():
        import jax, jax.numpy as jnp
        import numpy as np
        H, F, E_SHARED, E_ROUTED, K = (128, 512, 1, 8, 2)

        def _expert(x, w_up, w_down):
            h = jax.nn.gelu(jnp.einsum('bsh,hf->bsf', x, w_up), approximate=False)
            return jnp.einsum('bsf,fh->bsh', h, w_down)
        key = jax.random.key(seed)
        ks = jax.random.split(key, 6)
        x = jax.random.normal(ks[0], (4, 256, H), dtype=jnp.float32)
        s = 0.02
        shared_up = jax.random.normal(ks[1], (E_SHARED, H, F), dtype=jnp.float32) * s
        shared_down = jax.random.normal(ks[2], (E_SHARED, F, H), dtype=jnp.float32) * s
        routed_up = jax.random.normal(ks[3], (E_ROUTED, H, F), dtype=jnp.float32) * s
        routed_down = jax.random.normal(ks[4], (E_ROUTED, F, H), dtype=jnp.float32) * s
        router_w = jax.random.normal(ks[5], (H, E_ROUTED), dtype=jnp.float32) * s
        return {'x': x, 'shared_up': shared_up, 'shared_down': shared_down, 'routed_up': routed_up, 'routed_down': routed_down, 'router_w': router_w}
    _L0_ffn_in = _L0_ffn_setup()

    def _L1_attn_setup():
        import jax, jax.numpy as jnp
        import numpy as np
        N_HEAD = 16
        LATENT = 32

        def _rotate_half(x):
            xe = x[..., ::2]
            xo = x[..., 1::2]
            return jnp.stack((-xo, xe), axis=-1).reshape(x.shape)

        def _rope_tables(T, latent_dim, dtype):
            inv_freq = 1.0 / 10000.0 ** (jnp.arange(0, latent_dim, 2, dtype=jnp.float32) / latent_dim)
            t = jnp.arange(T, dtype=jnp.float32)
            freqs = jnp.outer(t, inv_freq)
            cos = jnp.repeat(jnp.cos(freqs), 2, axis=-1)[:, :latent_dim]
            sin = jnp.repeat(jnp.sin(freqs), 2, axis=-1)[:, :latent_dim]
            return (cos.astype(dtype), sin.astype(dtype))
        key = jax.random.key(seed)
        ks = jax.random.split(key, 14)
        C = 128
        hd = C // N_HEAD
        L = LATENT
        s = 0.02
        return {'x': jax.random.normal(ks[0], (4, 256, C), jnp.float32), 'c_attn_w': jax.random.normal(ks[1], (3 * C, C), jnp.float32) * s, 'c_attn_b': jnp.zeros((3 * C,), jnp.float32), 'q2l_w': jax.random.normal(ks[2], (L, hd), jnp.float32) * s, 'q2l_b': jnp.zeros((L,), jnp.float32), 'kv2l_w': jax.random.normal(ks[3], (L, hd), jnp.float32) * s, 'kv2l_b': jnp.zeros((L,), jnp.float32), 'l2o_w': jax.random.normal(ks[4], (hd, L), jnp.float32) * s, 'l2o_b': jnp.zeros((hd,), jnp.float32), 'wqk_w': jax.random.normal(ks[5], (L, L), jnp.float32) * s, 'wqk_b': jnp.zeros((L,), jnp.float32), 'cproj_w': jax.random.normal(ks[6], (C, C), jnp.float32) * s, 'cproj_b': jnp.zeros((C,), jnp.float32)}
    _L1_attn_in = _L1_attn_setup()

    def _L1_ffn_setup():
        import jax, jax.numpy as jnp
        import numpy as np
        B, S, H = (2, 256, 128)
        F = 512
        E = 8
        TOP_K = 2
        SHARED_SCALE = 0.1
        EPS = 1e-09

        def _moe_forward(x3, Wg, W1, b1, W2, b2, Ws1, bs1, Ws2, bs2):
            b, s, h = x3.shape
            x = x3.reshape(-1, h)
            T = x.shape[0]
            logits = x @ Wg
            probs = jax.nn.softmax(logits, axis=-1)
            vals, idx = jax.lax.top_k(probs, TOP_K)
            weights = vals / (jnp.sum(vals, axis=-1, keepdims=True) + EPS)
            cw = jnp.zeros((T, E), dtype=x.dtype).at[jnp.arange(T)[:, None], idx].set(weights)
            hpre = jnp.einsum('th,ehf->tef', x, W1) + b1
            act = jax.nn.silu(hpre)
            y = jnp.einsum('tef,efh->teh', act, W2) + b2
            out = jnp.einsum('te,teh->th', cw, y)
            shared = jax.nn.silu(x @ Ws1 + bs1) @ Ws2 + bs2
            out = out + SHARED_SCALE * shared
            return out.reshape(b, s, h)
        key = jax.random.key(seed)
        ks = jax.random.split(key, 10)
        sc = 0.02
        return {'hidden_states': jax.random.normal(ks[0], (B, S, H), dtype=jnp.float32), 'Wg': jax.random.normal(ks[1], (H, E), dtype=jnp.float32) * sc, 'W1': jax.random.normal(ks[2], (E, H, F), dtype=jnp.float32) * sc, 'b1': jnp.zeros((E, F), dtype=jnp.float32), 'W2': jax.random.normal(ks[3], (E, F, H), dtype=jnp.float32) * sc, 'b2': jnp.zeros((E, H), dtype=jnp.float32), 'Ws1': jax.random.normal(ks[4], (H, F), dtype=jnp.float32) * sc, 'bs1': jnp.zeros((F,), dtype=jnp.float32), 'Ws2': jax.random.normal(ks[5], (F, H), dtype=jnp.float32) * sc, 'bs2': jnp.zeros((H,), dtype=jnp.float32)}
    _L1_ffn_in = _L1_ffn_setup()
    _d = {'L0_attn_x': _L0_attn_in['x'], 'L0_attn_Wq': _L0_attn_in['Wq'], 'L0_attn_bq': _L0_attn_in['bq'], 'L0_attn_Wk': _L0_attn_in['Wk'], 'L0_attn_bk': _L0_attn_in['bk'], 'L0_attn_Wv': _L0_attn_in['Wv'], 'L0_attn_bv': _L0_attn_in['bv'], 'L0_attn_Wp': _L0_attn_in['Wp'], 'L0_ffn_shared_up': _L0_ffn_in['shared_up'], 'L0_ffn_shared_down': _L0_ffn_in['shared_down'], 'L0_ffn_routed_up': _L0_ffn_in['routed_up'], 'L0_ffn_routed_down': _L0_ffn_in['routed_down'], 'L0_ffn_router_w': _L0_ffn_in['router_w'], 'L1_attn_c_attn_w': _L1_attn_in['c_attn_w'], 'L1_attn_c_attn_b': _L1_attn_in['c_attn_b'], 'L1_attn_q2l_w': _L1_attn_in['q2l_w'], 'L1_attn_q2l_b': _L1_attn_in['q2l_b'], 'L1_attn_kv2l_w': _L1_attn_in['kv2l_w'], 'L1_attn_kv2l_b': _L1_attn_in['kv2l_b'], 'L1_attn_l2o_w': _L1_attn_in['l2o_w'], 'L1_attn_l2o_b': _L1_attn_in['l2o_b'], 'L1_attn_wqk_w': _L1_attn_in['wqk_w'], 'L1_attn_wqk_b': _L1_attn_in['wqk_b'], 'L1_attn_cproj_w': _L1_attn_in['cproj_w'], 'L1_attn_cproj_b': _L1_attn_in['cproj_b'], 'L1_ffn_Wg': _L1_ffn_in['Wg'], 'L1_ffn_W1': _L1_ffn_in['W1'], 'L1_ffn_b1': _L1_ffn_in['b1'], 'L1_ffn_W2': _L1_ffn_in['W2'], 'L1_ffn_b2': _L1_ffn_in['b2'], 'L1_ffn_Ws1': _L1_ffn_in['Ws1'], 'L1_ffn_bs1': _L1_ffn_in['bs1'], 'L1_ffn_Ws2': _L1_ffn_in['Ws2'], 'L1_ffn_bs2': _L1_ffn_in['bs2']}
    _x0 = _d['L0_attn_x']
    _d['L0_attn_x'] = jax.random.normal(jax.random.fold_in(jax.random.key(seed), 1), (16, 512, 128), dtype=_x0.dtype)
    del _x0
    return _d

def reference(L0_attn_x, L0_attn_Wq, L0_attn_bq, L0_attn_Wk, L0_attn_bk, L0_attn_Wv, L0_attn_bv, L0_attn_Wp, L0_ffn_shared_up, L0_ffn_shared_down, L0_ffn_routed_up, L0_ffn_routed_down, L0_ffn_router_w, L1_attn_c_attn_w, L1_attn_c_attn_b, L1_attn_q2l_w, L1_attn_q2l_b, L1_attn_kv2l_w, L1_attn_kv2l_b, L1_attn_l2o_w, L1_attn_l2o_b, L1_attn_wqk_w, L1_attn_wqk_b, L1_attn_cproj_w, L1_attn_cproj_b, L1_ffn_Wg, L1_ffn_W1, L1_ffn_b1, L1_ffn_W2, L1_ffn_b2, L1_ffn_Ws1, L1_ffn_bs1, L1_ffn_Ws2, L1_ffn_bs2):

    def _L0_attn_ref(x, Wq, bq, Wk, bk, Wv, bv, Wp):
        import jax, jax.numpy as jnp
        import numpy as np
        import math
        EMBED = 128
        HEADS = 16
        HEAD_DIM = EMBED // HEADS
        B, N = (2, 256)
        Bb, Nn, E = x.shape
        H, D = (HEADS, HEAD_DIM)
        q = (x @ Wq + bq).reshape(Bb, Nn, H, D)
        k = (x @ Wk + bk).reshape(Bb, Nn, H, D)
        v = (x @ Wv + bv).reshape(Bb, Nn, H, D)
        q = jnp.einsum('bnhe,ei->bnhi', q, Wp)
        k = jnp.einsum('bnhe,ei->bnhi', k, Wp)
        scores = jnp.einsum('bnhi,bmhi->bnhm', q, k) / math.sqrt(D)
        attn = jax.nn.softmax(scores, axis=-1)
        out = jnp.einsum('bnhm,bmhe->bnhe', attn, v).reshape(Bb, Nn, E)
        return out

    def _L0_ffn_ref(x, shared_up, shared_down, routed_up, routed_down, router_w):
        import jax, jax.numpy as jnp
        import numpy as np
        H, F, E_SHARED, E_ROUTED, K = (128, 512, 1, 8, 2)

        def _expert(x, w_up, w_down):
            h = jax.nn.gelu(jnp.einsum('bsh,hf->bsf', x, w_up), approximate=False)
            return jnp.einsum('bsf,fh->bsh', h, w_down)
        shared_out = jnp.zeros_like(x)
        for i in range(E_SHARED):
            shared_out = shared_out + _expert(x, shared_up[i], shared_down[i])
        probs = jax.nn.softmax(jnp.einsum('bsh,he->bse', x, router_w), axis=-1)
        top_k_prob, top_k_idx = jax.lax.top_k(probs, K)
        onehot = jax.nn.one_hot(top_k_idx, E_ROUTED, dtype=x.dtype)
        gates = jnp.einsum('bsk,bske->bse', top_k_prob, onehot)
        routed_out = jnp.zeros_like(x)
        for e in range(E_ROUTED):
            y = _expert(x, routed_up[e], routed_down[e])
            routed_out = routed_out + gates[..., e:e + 1] * y
        return shared_out + routed_out + x

    def _L1_attn_ref(x, c_attn_w, c_attn_b, q2l_w, q2l_b, kv2l_w, kv2l_b, l2o_w, l2o_b, wqk_w, wqk_b, cproj_w, cproj_b):
        import jax, jax.numpy as jnp
        import numpy as np
        N_HEAD = 16
        LATENT = 32

        def _rotate_half(x):
            xe = x[..., ::2]
            xo = x[..., 1::2]
            return jnp.stack((-xo, xe), axis=-1).reshape(x.shape)

        def _rope_tables(T, latent_dim, dtype):
            inv_freq = 1.0 / 10000.0 ** (jnp.arange(0, latent_dim, 2, dtype=jnp.float32) / latent_dim)
            t = jnp.arange(T, dtype=jnp.float32)
            freqs = jnp.outer(t, inv_freq)
            cos = jnp.repeat(jnp.cos(freqs), 2, axis=-1)[:, :latent_dim]
            sin = jnp.repeat(jnp.sin(freqs), 2, axis=-1)[:, :latent_dim]
            return (cos.astype(dtype), sin.astype(dtype))
        B, T, C = x.shape
        H = N_HEAD
        hd = C // H
        L = q2l_w.shape[0]
        qkv = x @ c_attn_w.T + c_attn_b
        q, k, v = jnp.split(qkv, 3, axis=2)

        def heads(t):
            return t.reshape(B, T, H, hd).transpose(0, 2, 1, 3)
        q, k, v = (heads(q), heads(k), heads(v))
        q_lat = q @ q2l_w.T + q2l_b
        k_lat = k @ kv2l_w.T + kv2l_b
        v_lat = v @ kv2l_w.T + kv2l_b
        cos, sin = _rope_tables(T, L, x.dtype)
        cos = cos[None, None]
        sin = sin[None, None]
        q_lat = q_lat * cos + _rotate_half(q_lat) * sin
        k_lat = k_lat * cos + _rotate_half(k_lat) * sin
        q_for_k = q_lat @ wqk_w.T + wqk_b
        att = jnp.einsum('bhql,bhkl->bhqk', q_for_k, k_lat) * L ** (-0.5)
        causal = jnp.tril(jnp.ones((T, T), dtype=bool))
        att = jnp.where(causal[None, None], att, -jnp.inf)
        att = jax.nn.softmax(att, axis=-1)
        y_lat = jnp.einsum('bhqk,bhkl->bhql', att, v_lat)
        y = y_lat @ l2o_w.T + l2o_b
        y = y.transpose(0, 2, 1, 3).reshape(B, T, C)
        return y @ cproj_w.T + cproj_b

    def _L1_ffn_ref(hidden_states, Wg, W1, b1, W2, b2, Ws1, bs1, Ws2, bs2):
        import jax, jax.numpy as jnp
        import numpy as np
        B, S, H = (2, 256, 128)
        F = 512
        E = 8
        TOP_K = 2
        SHARED_SCALE = 0.1
        EPS = 1e-09

        def _moe_forward(x3, Wg, W1, b1, W2, b2, Ws1, bs1, Ws2, bs2):
            b, s, h = x3.shape
            x = x3.reshape(-1, h)
            T = x.shape[0]
            logits = x @ Wg
            probs = jax.nn.softmax(logits, axis=-1)
            vals, idx = jax.lax.top_k(probs, TOP_K)
            weights = vals / (jnp.sum(vals, axis=-1, keepdims=True) + EPS)
            cw = jnp.zeros((T, E), dtype=x.dtype).at[jnp.arange(T)[:, None], idx].set(weights)
            hpre = jnp.einsum('th,ehf->tef', x, W1) + b1
            act = jax.nn.silu(hpre)
            y = jnp.einsum('tef,efh->teh', act, W2) + b2
            out = jnp.einsum('te,teh->th', cw, y)
            shared = jax.nn.silu(x @ Ws1 + bs1) @ Ws2 + bs2
            out = out + SHARED_SCALE * shared
            return out.reshape(b, s, h)
        return _moe_forward(hidden_states, Wg, W1, b1, W2, b2, Ws1, bs1, Ws2, bs2)
    x = L0_attn_x
    xn = _layernorm(x, axis=-1)
    s = _L0_attn_ref(xn, L0_attn_Wq, L0_attn_bq, L0_attn_Wk, L0_attn_bk, L0_attn_Wv, L0_attn_bv, L0_attn_Wp)
    g = _silu(_L0_ffn_ref(xn, L0_ffn_shared_up, L0_ffn_shared_down, L0_ffn_routed_up, L0_ffn_routed_down, L0_ffn_router_w))
    x = x + s * g
    xn = _layernorm(x, axis=-1)
    s = _L1_attn_ref(xn, L1_attn_c_attn_w, L1_attn_c_attn_b, L1_attn_q2l_w, L1_attn_q2l_b, L1_attn_kv2l_w, L1_attn_kv2l_b, L1_attn_l2o_w, L1_attn_l2o_b, L1_attn_wqk_w, L1_attn_wqk_b, L1_attn_cproj_w, L1_attn_cproj_b)
    g = _silu(_L1_ffn_ref(xn, L1_ffn_Wg, L1_ffn_W1, L1_ffn_b1, L1_ffn_W2, L1_ffn_b2, L1_ffn_Ws1, L1_ffn_bs1, L1_ffn_Ws2, L1_ffn_bs2))
    x = x + s * g
    return x

_drawn_inputs = setup_inputs


def setup_inputs(seed=0):
    import zlib

    import numpy as np

    out = dict(_drawn_inputs(seed))
    spreads = {'L1_attn_c_attn_b': (0.0, 0.8),
     'L1_attn_q2l_b': (0.0, 0.8),
     'L1_attn_kv2l_b': (0.0, 0.8),
     'L1_attn_l2o_b': (0.0, 0.8),
     'L1_attn_wqk_b': (0.0, 0.8),
     'L1_attn_cproj_b': (0.0, 0.8),
     'L1_ffn_b1': (0.0, 0.8),
     'L1_ffn_b2': (0.0, 0.8),
     'L1_ffn_bs1': (0.0, 0.8),
     'L1_ffn_bs2': (0.0, 2.0)}
    factors = {'L0_attn_bk': 64.0,
     'L0_ffn_shared_up': 5.599,
     'L0_ffn_shared_down': 5.485,
     'L0_ffn_routed_up': 8.0,
     'L0_ffn_routed_down': 8.0,
     'L0_ffn_router_w': 8.0,
     'L1_attn_c_attn_w': 8.0,
     'L1_attn_q2l_w': 8.0,
     'L1_attn_kv2l_w': 8.0,
     'L1_attn_l2o_w': 8.0,
     'L1_attn_wqk_w': 8.0,
     'L1_attn_cproj_w': 8.0,
     'L1_ffn_Wg': 8.0,
     'L1_ffn_W1': 8.0,
     'L1_ffn_W2': 8.0,
     'L1_ffn_Ws1': 8.0,
     'L1_ffn_Ws2': 8.0}
    for name, (base, spread) in spreads.items():
        noise = np.random.default_rng([zlib.crc32(name.encode()), seed]).standard_normal(out[name].shape)
        drawn = base * np.exp(spread * noise) if base else spread * noise
        out[name] = jnp.asarray(drawn.astype(out[name].dtype))
    for name, factor in factors.items():
        out[name] = (out[name] * factor).astype(out[name].dtype)
    return out
```

```python
from contextlib import ExitStack

import numpy as np

import concourse.bass as bass
from concourse import mybir

F32 = mybir.dt.float32
F32R = mybir.dt.float32r
BF16 = mybir.dt.bfloat16
I32 = mybir.dt.int32
ALU = mybir.AluOpType
ACT = mybir.ActivationFunctionType
AX = mybir.AxisListType

P = 128
BATCH, SEQ = 16, 512
TOKENS = BATCH * SEQ
TILES = TOKENS // P
TPB = SEQ // P
HEADS, HD = 16, 8
GH = 4
GROUPS = HEADS // GH
VC = HD + 1
LAT = 32
E, F = 8, 512
FB = F // P
SLOTS = 256
HALVES = SLOTS // P
ROUTED = (2 * TOKENS + E * (SLOTS - 1)) // SLOTS
ROUTED += ROUTED % 2
SHARED = TOKENS // SLOTS
ETILES = ROUTED + SHARED
ROWS = ETILES * SLOTS
SHARED_ROW = ROUTED * SLOTS
M_ROW = 96
EPS = 1e-5
MASKED = -1e30


def wait(eng, sem, value):
    if not isinstance(value, int) or value > 0:
        eng.wait_ge(sem, value)


def carried(eng, first, *waits):
    for _, v in waits:
        if not isinstance(v, int):
            eng.compute_val(v)
    eng.wait_ge(*first)
    for sem, v in waits:
        eng.wait_ge(sem, v)


def inside(value, count):
    return not isinstance(value, int) or 0 <= value < count


def loop(eng, count, body):
    body(0)
    with eng.Fori(1, count - 1) as i:
        body(i)
    body(count - 1)


class Layer:

    def __init__(self, nc, semaphores):
        self.nc, self.semaphores = nc, semaphores

    def semaphore(self, name):
        if name not in self.semaphores:
            self.semaphores[name] = self.nc.alloc_semaphore(name)
        return self.semaphores[name]


    def queue_semaphore(self, name):
        return self.nc.alloc_semaphore(f"{name}_{self.index}")


def clear(nc, semaphores):
    every = list(semaphores.values())
    with nc.Block() as block:
        @block.sync
        def _(sp):
            for s in every[0::4]:
                sp.sem_clear(s)

        @block.gpsimd
        def _(pool):
            for s in every[1::4]:
                pool.sem_clear(s)

        @block.scalar
        def _(act):
            for s in every[2::4]:
                act.sem_clear(s)

        @block.vector
        def _(dve):
            for s in every[3::4]:
                dve.sem_clear(s)


def alloc(nc, ctx):
    def sb(name, shape, dt=F32):
        return ctx.enter_context(nc.sbuf_tensor(name, shape, dt))

    def psum(name, banks=1):
        return ctx.enter_context(nc.psum_tensor(name, [P, banks * SEQ], F32))

    def sem(name):
        return nc.alloc_semaphore(name)

    return sb, psum, sem


def load_constants(nc, d, w):
    with ExitStack() as ctx:
        sb, psum, sem = alloc(nc, ctx)
        loaded, folded, copied, ready = sem("w_loaded"), sem("w_folded"), sem("w_copied"), sem("w_ready")
        masks_zero = sem("w_masks_zero")
        ps = [psum(f"w_ps{i}") for i in range(2)]
        t = {}
        for name in ("wqT", "wkT", "wpx", "cq", "ck", "cv", "mask8", "mask32x32", "rot", "wqkx"):
            t[name] = sb("t_" + name, [P, P])
        for name in ("q2lx", "kv2lx", "mask32"):
            t[name] = sb("t_" + name, [P, HEADS * LAT])
        for name in ("kv2lrep", "l2orep"):
            t[name] = sb("t_" + name, [LAT, P])
        for name in ("bq", "bk", "cqb", "ckb", "cvb", "q2lbx", "kv2lbx", "l2obx"):
            t[name] = sb("t_" + name, [P, 1])
        kv2lb = sb("t_kv2lb", [LAT, 1])
        cprojb = sb("t_cprojb", [1, P])
        bd = {n: sb("bd_" + n, [P, P]) for n in ("wp", "v")}
        for n in ("q", "k"):
            bd[n] = sb("bd_" + n, [P, HEADS * LAT])

        loads = [(t[n], d[n]) for n in t] + [(kv2lb, d["kv2lb"]), (cprojb, d["cprojb"])]
        loads += [(w[n], d[n]) for n in ("ident", "tri", "cos", "sin", "wv0", "bv0", "wr0", "wr1",
                                         "bqk", "cprojT")]
        folds = []

        def fold(m, n, products, evacuate):
            folds.append((m, n, products, evacuate))

        def copy_to(out):
            return lambda eng, p: [eng.tensor_copy(out, p)]

        fold(P, P, [(t["wqT"], bd["wp"])], copy_to(w["wq0"][:, :]))
        fold(P, P, [(t["wkT"], bd["wp"])], copy_to(w["wk0"][:, :]))
        fold(P, 1, [(bd["wp"], t["bq"])], copy_to(w["bq0"][:, :]))
        fold(P, 1, [(bd["wp"], t["bk"])], copy_to(w["bk0"][:, :]))
        for s, c, x, lb in (("q", "cq", "cqb", "q2lbx"), ("k", "ck", "ckb", "kv2lbx")):
            def both(eng, p, s=s):
                turned = w["wb" + s][:, :].rearrange("p (j two) -> p j two", two=2)
                plain = p.rearrange("p (j two) -> p j two", two=2)
                return [eng.tensor_copy(w["wa" + s][:, :], p),
                        eng.tensor_scalar(turned[:, :, 0], plain[:, :, 1], -1.0, None, ALU.mult),
                        eng.tensor_copy(turned[:, :, 1], plain[:, :, 0])]
            fold(P, HEADS * LAT, [(t[c], bd[s])], both)
            for g in range(GROUPS):
                def bias(eng, p, s=s, g=g, lb=lb):
                    return [eng.tensor_tensor(w["ba" + s][:, g:g + 1], p, t[lb][:, :], ALU.add)]
                fold(P, 1, [(bd[s][:, g * P:(g + 1) * P], t[x])], bias)
            fold(P, GROUPS, [(t["rot"], w["ba" + s])], copy_to(w["bb" + s][:, :]))
        fold(P, P, [(t["kv2lrep"], t["l2orep"])],
             lambda eng, p: [eng.tensor_tensor(bd["v"][:, :], p, t["mask8"][:, :], ALU.mult)])
        fold(P, P, [(t["cv"], bd["v"])], copy_to(w["wv1"][:, :]))
        fold(1, P, [(t["cvb"], bd["v"]), (kv2lb, t["l2orep"])], copy_to(w["bv1"][:, :]))
        fold(1, P, [(t["l2obx"], w["cprojT"])],
             lambda eng, p: [eng.tensor_tensor(w["bs1"][:, :], p, cprojb[:, :], ALU.add)])
        MASKS = 6

        with nc.Block() as block:
            @block.sync
            def _(sp):
                for out, src in loads:
                    sp.dma_start(out[:, :], src).then_inc(loaded, 16)

            @block.vector
            def _(dve):
                dve.memset(w["ones"][:, :], 1.0)
                dve.memset(w["eps"][:, :], EPS)
                dve.wait_ge(loaded, 16 * len(loads))
                dve.tensor_copy(w["ident_bf"][:, :], w["ident"][:, :]).then_inc(ready, 1)
                dve.tensor_tensor(bd["wp"][:, :], t["wpx"][:, :], t["mask8"][:, :], ALU.mult).then_inc(ready, 1)
                dve.tensor_tensor(bd["q"][:, :], t["q2lx"][:, :], t["mask32"][:, :], ALU.mult).then_inc(ready, 1)
                dve.tensor_tensor(bd["k"][:, :], t["kv2lx"][:, :], t["mask32"][:, :], ALU.mult).then_inc(ready, 1)
                dve.tensor_tensor(w["wqk"][:, :], t["wqkx"][:, :], t["mask32x32"][:, :], ALU.mult).then_inc(ready, 1)
                dve.memset(w["zeros"][:, :], 0.0).then_inc(ready, 1)
                for i, (m, n, _, evacuate) in enumerate(folds):
                    dve.wait_ge(folded, i + 1)
                    evacuate(dve, ps[i % 2][0:m, 0:n])[-1].then_inc(copied, 1)

            @block.tensor
            def _(pe):
                pe.wait_ge(ready, MASKS)
                for i, (m, n, products, _) in enumerate(folds):
                    wait(pe, copied, i)
                    for j, (a, b) in enumerate(products):
                        mm = pe.matmul(ps[i % 2][0:m, 0:n], a[:, :], b[:, :],
                                       start=(j == 0), stop=(j == len(products) - 1))
                    mm.then_inc(folded, 1)

            @block.gpsimd
            def _(pool):
                pool.memset(w["mask_q"][:, :], 0.0).then_inc(masks_zero, 1)
                pool.memset(w["mask_k"][:, :], 0.0).then_inc(masks_zero, 1)
                pool.wait_ge(masks_zero, 2)
                pool.affine_select(out=w["mask_q"][:, :], in_=w["mask_q"][:, :], compare_op=ALU.is_ge,
                                   fill=MASKED, base=0, pattern=[[-1, P]], channel_multiplier=1)
                pool.affine_select(out=w["mask_k"][:, :], in_=w["mask_k"][:, :], compare_op=ALU.is_ge,
                                   fill=MASKED, base=0, pattern=[[1, P]], channel_multiplier=-1)


def prepare(nc, L, d, w):
    l = L.index
    jobs = 2 if l == 0 else 2 * GROUPS
    with ExitStack() as ctx:
        sb, psum, sem = alloc(nc, ctx)
        S = lambda name: L.semaphore(f"a_{name}")
        x = sb(f"a{l}_x", [P, 2, TPB, P])
        stats = sb(f"a{l}_stats", [P, 2, TPB, 6])
        mean_var = sb(f"a{l}_mv", [P, 2, TPB, 2])
        sd = sb(f"a{l}_sd", [P, 2, TPB])
        rstd = sb(f"a{l}_rstd", [P, 2, TPB])
        xn = sb(f"a{l}_xn", [P, 2, TPB, P])
        xT = sb(f"a{l}_xT", [P, 2, SEQ])
        v = sb(f"a{l}_v", [P, 2, TPB, HEADS, VC])
        parts = sb(f"a{l}_parts", [P, 2, 2, SEQ], F32R)
        roped = sb(f"a{l}_roped", [P, 2, 3, SEQ])
        ps_x = psum(f"a{l}_ps_x")
        ps_r = psum(f"a{l}_ps_r")[:, 0:TPB * E].rearrange("p (t e) -> p t e", e=E)
        ps_v = psum(f"a{l}_ps_v")[:, :].rearrange("p (t n) -> p t n", n=P)
        ps_j = [[psum(f"a{l}_ps_j{i}{k}") for k in range(2)] for i in range(2)]
        ps_q = psum(f"a{l}_ps_q")

        zeroed = S("zeroed")
        x_in = [S(f"x_in{s}") for s in range(2)]
        xn_out = [S(f"xn_out{s}") for s in range(2)]
        v_out = [S(f"v_out{s}") for s in range(2)]
        parts_out = [S(f"parts_out{s}") for s in range(2)]
        var_done, sd_done, normed, stat = S("var"), S("sd"), S("normed"), S("stat")
        turned, xT_done = S("turned"), S("xT")
        routed, logits_done = S("routed"), S("logits")
        v_mm, v_done, v_ones = S("v_mm"), S("v_done"), S("v_ones")
        proj, mixed, summed = S("proj"), S("mixed"), S("summed")
        q_mm, hi_done, lo_done = S("q_mm"), S("hi"), S("lo")
        lo_pool = S("lo_pool")
        sem_chain = S("chain")

        x_view = L.x_in.rearrange("(b t p) n -> b p t n", t=TPB, p=P)
        xn_view = L.slots_in[SHARED_ROW:ROWS, :].rearrange("(b t p) n -> b p t n", t=TPB, p=P)
        v_view = L.v.rearrange("(b p) n -> b p n", p=P)
        z_view = L.slots_in[0:SHARED_ROW, :].rearrange("(z p r) n -> z p (r n)", p=P, r=16)

        def bias_of(j):
            return (w["bq0"], w["bk0"])[j][:, 0:1] if l == 0 else w["bqk"][:, 0:1]

        with nc.Block() as block:
            @block.sync
            def _(sp):
                for z in range(SHARED_ROW // (16 * P)):
                    sp.dma_start(z_view[z], w["zeros"][:, :]).then_inc(zeroed, 16)

                def load(bb, s):
                    b = 2 * bb + s
                    wait(sp, normed, TPB * (b - 1))
                    sp.dma_start(x[:, s], x_view[bass.ds(b, 1)].rearrange("o p t n -> (o p) t n")
                                 ).then_inc(x_in[s], 16)

                def body(bb):
                    for s in range(2):
                        b = 2 * bb + s
                        if isinstance(bb, int) and b == 0:
                            load(0, 0)
                            load(0, 1)
                        sp.wait_ge(normed, TPB * (b + 1))
                        sp.dma_start(xn_view[bass.ds(b, 1)].rearrange("o p t n -> (o p) t n"), xn[:, s]
                                     ).then_inc(xn_out[s], 16)
                        if not isinstance(bb, int) or bb < BATCH // 2 - 1:
                            load(bb + 1, s)
                        for j in range(jobs):
                            n = jobs * b + j
                            sp.wait_ge(hi_done, n + 1)
                            if l == 0 or j % 2 == 0:
                                sp.wait_ge(lo_done, (jobs * b + j if l == 0 else (jobs * b + j) // 2) + 1)
                            else:
                                sp.wait_ge(lo_pool, (jobs * b + j) // 2 + 1)
                            dst = (L.q, L.k)[j % 2][:, (j // 2) * P:(j // 2 + 1) * P, bass.ds(b * SEQ, SEQ)]
                            sp.dma_start(dst.rearrange("r f t -> f r t"), parts[:, j % 2].bitcast(F32)
                                         ).then_inc(parts_out[j % 2], 16)
                        sp.wait_ge(v_done, b + 1)
                        sp.dma_start(v_view[bass.ds(b, 1)].rearrange("o p n -> (o p) n"),
                                     v[:, s].rearrange("p t h c -> p (t h c)")).then_inc(v_out[s], 16)

                loop(sp, BATCH // 2, body)
                sp.wait_ge(zeroed, 16 * (SHARED_ROW // (16 * P)))
                for s in range(2):
                    sp.wait_ge(xn_out[s], 16 * (BATCH // 2))
                    sp.wait_ge(v_out[s], 16 * (BATCH // 2))
                    sp.wait_ge(parts_out[s], 16 * BATCH * jobs // 2)

            @block.vector
            def _(dve):
                dve.memset(v[:, :, :, :, HD:VC], 1.0).then_inc(v_ones, 1)

                def norm(bb, s):
                    b = 2 * bb + s
                    dve.wait_ge(x_in[s], 16 * (bb + 1))
                    for t in range(TPB):
                        dve.bn_stats(stats[:, s, t, :], x[:, s, t, :]).then_inc(stat, 1)
                    carried(dve, (stat, 1), (stat, TPB * (b + 1)))
                    for t in range(TPB):
                        dve.bn_aggr(mean_var[:, s, t, :], stats[:, s, t, :]).then_inc(var_done, 1)
                    dve.wait_ge(sd_done, b + 1)
                    dve.reciprocal(rstd[:, s, :], sd[:, s, :]).then_inc(sem_chain, 1)
                    dve.wait_ge(sem_chain, b + 1)
                    wait(dve, xn_out[s], 16 * bb)
                    wait(dve, turned, b - 1)
                    for t in range(TPB):
                        dve.tensor_scalar(xn[:, s, t, :], x[:, s, t, :], mean_var[:, s, t, 0:1],
                                          rstd[:, s, t:t + 1], ALU.subtract, ALU.mult).then_inc(normed, 1)

                def body(bb):
                    for s in range(2):
                        b = 2 * bb + s
                        if isinstance(bb, int) and bb == 0 and s == 0:
                            norm(0, 0)
                        if not (isinstance(bb, int) and b == BATCH - 1):
                            norm(bb + s, 1 - s)
                        dve.wait_ge(routed, b + 1)
                        dve.tensor_copy(w["logits"][:, bass.ds(b * TPB, TPB), :], ps_r[:, :, :]
                                        ).then_inc(logits_done, 1)
                        for j in range(jobs):
                            n = jobs * b + j
                            if l == 0:
                                dve.wait_ge(hi_done, n + 1)
                                dve.scalar_tensor_tensor(parts[:, j, 1, :], ps_j[j][0][:, :], bias_of(j),
                                                         parts[:, j, 0, :], ALU.add, ALU.subtract
                                                         ).then_inc(lo_done, 1)
                                continue
                            g, which = j // 2, "qk"[j % 2]
                            dve.wait_ge(proj, n + 1)
                            wait(dve, summed, n - 1)
                            dve.scalar_tensor_tensor(roped[:, j % 2, 0, :], ps_j[j % 2][0][:, :],
                                                     w["ba" + which][:, g:g + 1], w["cos"][:, :],
                                                     ALU.add, ALU.mult).then_inc(mixed, 1)
                            dve.scalar_tensor_tensor(roped[:, j % 2, 1, :], ps_j[j % 2][1][:, :],
                                                     w["bb" + which][:, g:g + 1], w["sin"][:, :],
                                                     ALU.add, ALU.mult).then_inc(mixed, 1)
                            if j % 2 == 1:
                                dve.wait_ge(hi_done, n)
                                dve.scalar_tensor_tensor(parts[:, 0, 1, :], ps_q[:, :], bias_of(j),
                                                         parts[:, 0, 0, :], ALU.add, ALU.subtract
                                                         ).then_inc(lo_done, 1)

                loop(dve, BATCH // 2, body)

            @block.gpsimd
            def _(pool):
                if l == 0:
                    return

                def body(b):
                    for j in range(jobs):
                        n = jobs * b + j
                        pool.wait_ge(mixed, 2 * n + 2)
                        if j % 2 == 0:
                            wait(pool, q_mm, (jobs // 2) * b + j // 2)
                        else:
                            wait(pool, lo_pool, (jobs // 2) * b + j // 2)
                        pool.tensor_tensor(roped[:, j % 2, 2, :], roped[:, j % 2, 0, :],
                                           roped[:, j % 2, 1, :], ALU.add).then_inc(summed, 1)
                        if j % 2 == 1:
                            pool.wait_ge(hi_done, n + 1)
                            pool.wait_ge(summed, n + 1)
                            pool.tensor_tensor(parts[:, 1, 1, :], roped[:, 1, 2, :], parts[:, 1, 0, :],
                                               ALU.subtract).then_inc(lo_pool, 1)

                loop(pool, BATCH, body)

            @block.scalar
            def _(act):
                def sqrt(b, s):
                    act.wait_ge(var_done, TPB * (b + 1))
                    act.activation(sd[:, s, :], mean_var[:, s, :, 1], ACT.Sqrt, bias=w["eps"][:, 0:1]
                                   ).then_inc(sd_done, 1)

                def body(bb):
                    for s in range(2):
                        b = 2 * bb + s
                        if isinstance(bb, int) and bb == 0 and s == 0:
                            sqrt(0, 0)
                        act.wait_ge(turned, b + 1)
                        wait(act, proj, jobs * (b - 1))
                        act.activation(xT[:, s, :], ps_x[:, :], ACT.Copy).then_inc(xT_done, 1)
                        if not (isinstance(bb, int) and b == BATCH - 1):
                            sqrt(b + 1, 1 - s)
                        act.wait_ge(v_mm, b + 1)
                        act.wait_ge(v_ones, 1)
                        wait(act, v_out[s], 16 * bb)
                        act.activation(v[:, s, :, :, 0:HD],
                                       ps_v[:, :, :].rearrange("p t (h c) -> p t h c", h=HEADS),
                                       ACT.Copy).then_inc(v_done, 1)
                        for j in range(jobs):
                            n = jobs * b + j
                            half = (jobs // 2) * b + j // 2
                            wait(act, parts_out[j % 2], 16 * half)
                            if l == 0:
                                act.wait_ge(proj, n + 1)
                                src = ps_j[j][0]
                            elif j % 2 == 0:
                                act.wait_ge(q_mm, half + 1)
                                src = ps_q
                            else:
                                act.wait_ge(summed, n + 1)
                            if l == 1 and j % 2 == 1:
                                act.activation(parts[:, 1, 0, :], roped[:, 1, 2, :], ACT.Copy
                                               ).then_inc(hi_done, 1)
                            else:
                                act.activation(parts[:, j % 2, 0, :], src[:, :], ACT.Identity,
                                               bias=bias_of(j)).then_inc(hi_done, 1)

                loop(act, BATCH // 2, body)

            @block.tensor
            def _(pe):
                def turn(b, s):
                    pe.wait_ge(normed, TPB * (b + 1))
                    wait(pe, xT_done, b)
                    for t in range(TPB):
                        mm = pe.transpose(ps_x[:, t * P:(t + 1) * P], xn[:, s, t, :], w["ident"][:, :])
                    mm.then_inc(turned, 1)

                def body(bb):
                    for s in range(2):
                        b = 2 * bb + s
                        if isinstance(bb, int) and bb == 0 and s == 0:
                            turn(0, 0)
                        pe.wait_ge(xT_done, b + 1)
                        wait(pe, logits_done, b)
                        for t in range(TPB):
                            mm = pe.matmul(ps_r[:, t, :], xT[:, s, t * P:(t + 1) * P], L.wr[:, :],
                                           start=True, stop=True)
                        mm.then_inc(routed, 1)
                        wait(pe, v_done, b)
                        for t in range(TPB):
                            pe.matmul(ps_v[:, t, :], xT[:, s, t * P:(t + 1) * P], L.wv[:, :],
                                      start=True, stop=False)
                            mm = pe.matmul(ps_v[:, t, :], w["ones"][0:1, :], L.bv[:, :],
                                           start=False, stop=True)
                        mm.then_inc(v_mm, 1)

                        def to_latent_q(j):
                            k = (jobs // 2) * b + j // 2
                            pe.wait_ge(summed, jobs * b + j + 1)
                            wait(pe, lo_done, k)
                            pe.matmul(ps_q[:, :], w["wqk"][:, :], roped[:, 0, 2, :],
                                      start=True, stop=True).then_inc(q_mm, 1)

                        for j in range(jobs):
                            n = jobs * b + j
                            if l == 0:
                                wait(pe, lo_done, n - 1)
                                pe.matmul(ps_j[j][0][:, :], (w["wq0"], w["wk0"])[j][:, :], xT[:, s, :],
                                          start=True, stop=True).then_inc(proj, 1)
                                continue
                            which, g = "qk"[j % 2], j // 2
                            wait(pe, mixed, 2 * (n - 1))
                            for k, form in enumerate("ab"):
                                mm = pe.matmul(ps_j[j % 2][k][:, :],
                                               w["w" + form + which][:, g * P:(g + 1) * P], xT[:, s, :],
                                               start=True, stop=True)
                            mm.then_inc(proj, 1)
                            if j % 2 == 1:
                                to_latent_q(j - 1)
                        if not (isinstance(bb, int) and b == BATCH - 1):
                            turn(b + 1, 1 - s)

                loop(pe, BATCH // 2, body)


def dispatch(nc, L, w):
    l = L.index
    TE = [P, TILES, E]
    with ExitStack() as ctx:
        sb, psum, sem = alloc(nc, ctx)
        S = lambda name: L.semaphore(f"b_{name}")
        big = {n: sb(f"b{l}_{n}", TE) for n in ("ex", "pick", "oh1", "oh2", "oh", "total", "sum0", "sum1", "pos")}
        small = {n: sb(f"b{l}_{n}", [P, TILES]) for n in ("top", "all", "first", "p1", "p2")}
        iota_e = sb(f"b{l}_iota_e", [P, E])
        iota_c = sb(f"b{l}_iota_c", [P, E, TOKENS // SLOTS])
        iota_t = sb(f"b{l}_iota_t", [P, ETILES, E])
        over = sb(f"b{l}_over", [P, E, TOKENS // SLOTS])
        before = sb(f"b{l}_before", [P, ETILES, E])
        tiles = sb(f"b{l}_tiles", [P, 4, E])
        ps_in, ps_all = psum(f"b{l}_ps_in"), psum(f"b{l}_ps_all")
        rows = sb(f"b{l}_rows", [P, 2, P])
        index = sb(f"b{l}_index", [P, 2, 2], I32)
        chain, iotas, shifted, exps = S("chain"), S("iotas"), S("shifted"), S("exps")
        onehot, counted, placed = S("onehot"), S("counted"), S("placed")
        row_in = [S(f"row_in{s}") for s in range(2)]
        row_out = [L.queue_semaphore(f"row_out{s}") for s in range(2)]
        index_done = S("index")

        def over_e(x):
            return x[:, :].unsqueeze(2).to_broadcast(TE)

        def over_t(x):
            return x.unsqueeze(1).to_broadcast(TE)

        xn_view = L.slots_in[SHARED_ROW:ROWS, :].rearrange("(t p) n -> t p n", p=P)

        with nc.Block() as block:
            @block.gpsimd
            def _(pool):
                pool.iota(iota_e[:, :], pattern=[[1, E]], base=-E, channel_multiplier=0,
                          allow_small_or_imprecise_dtypes=True).then_inc(iotas, 1)
                pool.iota(iota_c[:, :, :], pattern=[[0, E], [SLOTS, TOKENS // SLOTS]], base=0,
                          channel_multiplier=0, allow_small_or_imprecise_dtypes=True).then_inc(iotas, 1)
                pool.iota(iota_t[:, :, :], pattern=[[1, ETILES], [0, E]], base=0,
                          channel_multiplier=0, allow_small_or_imprecise_dtypes=True).then_inc(iotas, 1)
                pool.wait_ge(placed, 1)

                def body(tt):
                    for s in range(2):
                        t = 2 * tt + s
                        wait(pool, row_out[s], 32 * tt)
                        for k in range(2):
                            pool.tensor_copy(index[:, s, k:k + 1], w["slot"][:, k, bass.ds(t, 1)]
                                             ).then_inc(index_done, 1)
                        carried(pool, (placed, 1), (index_done, 2 * t + 2), (row_in[s], 16 * (tt + 1)))
                        for k in range(2):
                            pool.indirect_dma_start(
                                L.slots_in, bass.IndirectOffsetOnAxis(ap=index[:, s, k:k + 1], axis=0),
                                rows[:, s, :], None).then_inc(row_out[s], 16)

                loop(pool, TILES // 2, body)
                for s in range(2):
                    pool.wait_ge(row_out[s], 16 * TILES)

            @block.sync
            def _(sp):
                def body(tt):
                    for s in range(2):
                        wait(sp, row_out[s], 32 * tt)
                        sp.dma_start(rows[:, s, :], xn_view[bass.ds(2 * tt + s, 1)].rearrange("o p n -> (o p) n")
                                     ).then_inc(row_in[s], 16)

                loop(sp, TILES // 2, body)

            @block.scalar
            def _(act):
                act.wait_ge(shifted, 1)
                act.activation(big["ex"][:, :, :], big["ex"][:, :, :], ACT.Exp).then_inc(exps, 1)

            @block.tensor
            def _(pe):
                pe.wait_ge(onehot, 1)
                flat = big["oh"][:, :, :].rearrange("p t e -> p (t e)")
                pe.matmul(ps_in[:, :], w["tri"][:, :], flat, start=True, stop=True)
                pe.matmul(ps_all[:, :], w["ones"][:, :], flat, start=True, stop=True).then_inc(counted, 1)

            @block.vector
            def _(dve):
                done = [0]

                def step(ins):
                    done[0] += 1
                    ins.then_inc(chain, 1)
                    dve.wait_ge(chain, done[0])

                ex, pick, pos = big["ex"], big["pick"], big["pos"]
                step(dve.tensor_reduce(small["top"][:, :], w["logits"][:, :, :], AX.X, ALU.max))
                dve.tensor_tensor(ex[:, :, :], w["logits"][:, :, :], over_e(small["top"]), ALU.subtract
                                  ).then_inc(shifted, 1)
                dve.wait_ge(exps, 1)
                dve.wait_ge(iotas, 3)
                step(dve.tensor_reduce(small["all"][:, :], ex[:, :, :], AX.X, ALU.add))
                step(dve.reciprocal(small["all"][:, :], small["all"][:, :]))
                for k, (oh, p) in enumerate(((big["oh1"], small["p1"]), (big["oh2"], small["p2"]))):
                    step(dve.tensor_reduce(small["top"][:, :], ex[:, :, :], AX.X, ALU.max))
                    step(dve.tensor_tensor(pick[:, :, :], ex[:, :, :], over_e(small["top"]), ALU.is_equal))
                    step(dve.tensor_tensor(pick[:, :, :], pick[:, :, :], over_t(iota_e[:, :]), ALU.mult))
                    step(dve.tensor_reduce(small["first"][:, :], pick[:, :, :], AX.X, ALU.min))
                    step(dve.tensor_tensor(oh[:, :, :], over_t(iota_e[:, :]), over_e(small["first"]), ALU.is_equal))
                    step(dve.tensor_tensor(p[:, :], small["top"][:, :], small["all"][:, :], ALU.mult))
                    if k == 0:
                        step(dve.scalar_tensor_tensor(ex[:, :, :], oh[:, :, :], -2.0, ex[:, :, :],
                                                      ALU.mult, ALU.add))
                dve.tensor_tensor(big["oh"][:, :, :], big["oh1"][:, :, :], big["oh2"][:, :, :], ALU.add
                                  ).then_inc(onehot, 1)
                if l == 0:
                    step(dve.tensor_copy(w["gate"][:, 0, :], small["p1"][:, :]))
                    step(dve.tensor_copy(w["gate"][:, 1, :], small["p2"][:, :]))
                else:
                    step(dve.tensor_tensor(small["first"][:, :], small["p1"][:, :], small["p2"][:, :], ALU.add))
                    step(dve.tensor_scalar(small["first"][:, :], small["first"][:, :], 1e-9, None, ALU.add))
                    step(dve.reciprocal(small["first"][:, :], small["first"][:, :]))
                    step(dve.tensor_tensor(w["gate"][:, 0, :], small["p1"][:, :], small["first"][:, :], ALU.mult))
                    step(dve.tensor_tensor(w["gate"][:, 1, :], small["p2"][:, :], small["first"][:, :], ALU.mult))
                dve.wait_ge(counted, 1)
                flat = lambda x: x[:, :, :].rearrange("p t e -> p (t e)")
                dve.tensor_copy(flat(big["total"]), ps_all[:, :])
                step(dve.tensor_copy(flat(big["sum0"]), ps_all[:, :]))
                a, b = big["sum0"], big["sum1"]
                reach = 1
                while reach < TILES:
                    dve.tensor_copy(b[:, 0:reach, :], a[:, 0:reach, :])
                    step(dve.tensor_tensor(b[:, reach:TILES, :], a[:, reach:TILES, :],
                                           a[:, 0:TILES - reach, :], ALU.add))
                    a, b = b, a
                    reach *= 2
                counts = a[:, TILES - 1, :]
                step(dve.tensor_tensor(over[:, :, :], counts.unsqueeze(2).to_broadcast([P, E, TOKENS // SLOTS]),
                                       iota_c[:, :, :], ALU.is_gt))
                step(dve.tensor_reduce(tiles[:, 0, :], over[:, :, :], AX.X, ALU.add))
                step(dve.tensor_copy(tiles[:, 1, :], tiles[:, 0, :]))
                e, f, reach = 1, 2, 1
                while reach < E:
                    dve.tensor_copy(tiles[:, f, 0:reach], tiles[:, e, 0:reach])
                    step(dve.tensor_tensor(tiles[:, f, reach:E], tiles[:, e, reach:E],
                                           tiles[:, e, 0:E - reach], ALU.add))
                    e, f, reach = f, e, 2 * reach
                step(dve.tensor_tensor(before[:, :, :], tiles[:, e, :].unsqueeze(1).to_broadcast([P, ETILES, E]),
                                       iota_t[:, :, :], ALU.is_le))
                step(dve.tensor_reduce(w["tile_f"][:, :], before[:, :, :], AX.X, ALU.add))
                step(dve.tensor_copy(w["tile_expert"][:, :], w["tile_f"][:, :]))
                step(dve.tensor_tensor(tiles[:, 3, :], tiles[:, e, :], tiles[:, 0, :], ALU.subtract))
                step(dve.tensor_scalar(tiles[:, 3, :], tiles[:, 3, :], float(SLOTS), None, ALU.mult))
                step(dve.tensor_tensor(pos[:, :, :], a[:, :, :], big["total"][:, :, :], ALU.subtract))
                step(dve.tensor_tensor(pos[:, :, :], pos[:, :, :], over_t(tiles[:, 3, :]), ALU.add))
                step(dve.tensor_tensor(flat(pos), flat(pos), ps_in[:, :], ALU.add))
                for k, oh in enumerate((big["oh1"], big["oh2"])):
                    step(dve.tensor_tensor(pick[:, :, :], oh[:, :, :], pos[:, :, :], ALU.mult))
                    step(dve.tensor_reduce(small["first"][:, :], pick[:, :, :], AX.X, ALU.add))
                    step(dve.tensor_copy(w["slot"][:, k, :], small["first"][:, :]))
                dve.tensor_copy(small["first"][:, :], small["first"][:, :]).then_inc(placed, 1)


def experts(nc, L, w):
    l = L.index
    with ExitStack() as ctx:
        sb, psum, sem = alloc(nc, ctx)
        S = lambda name: L.semaphore(f"c_{name}")
        up = sb(f"c{l}_up", [P, 2, F + FB])
        down = sb(f"c{l}_down", [P, 2, FB, P])
        b2 = sb(f"c{l}_b2", [1, 2, P])
        rows = sb(f"c{l}_rows", [P, 2, HALVES, P])
        xT = sb(f"c{l}_xT", [P, 2, SLOTS])
        hT = sb(f"c{l}_hT", [P, 2, FB, SLOTS])
        y = sb(f"c{l}_y", [P, 2, HALVES, P])
        ps_x = psum(f"c{l}_ps_x")
        ps_h = [psum(f"c{l}_ps_h{s}", 2) for s in range(2)]
        ps_y = [psum(f"c{l}_ps_y{s}") for s in range(2)]
        rows_in = [S(f"rows_in{s}") for s in range(2)]
        weights_in = [S(f"weights_in{s}") for s in range(2)]
        y_out = [S(f"y_out{s}") for s in range(2)]
        turned, xT_done, h_mm, h_done, y_mm, y_done = (
            S("turned"), S("xT"), S("h_mm"), S("h"), S("y_mm"), S("y"))
        WEIGHT_DMAS = 2 if l == 0 else 3
        H_STEPS = 1 if l == 0 else FB

        in_view = L.slots_in.rearrange("(t a p) n -> t p a n", a=HALVES, p=P)
        out_view = L.slots_out.rearrange("(t a p) n -> t p a n", a=HALVES, p=P)

        def steps(eng, body):
            pass

        with nc.Block() as block:
            @block.sync
            def _(sp):
                def body(tt):
                    for s in range(2):
                        t = 2 * tt + s
                        expert = sp.value_load(w["tile_expert"][0:1, bass.ds(t, 1)], min_val=0, max_val=E)
                        wait(sp, turned, t - 1)
                        sp.dma_start(rows[:, s], in_view[bass.ds(t, 1)].rearrange("o p a n -> (o p) a n")
                                     ).then_inc(rows_in[s], 16)
                        wait(sp, y_mm, t - 1)
                        sp.dma_start(up[:, s, 0:L.up_width], L.w1[bass.ds(expert, 1)].rearrange("o p n -> (o p) n")
                                     ).then_inc(weights_in[s], 16)
                        sp.dma_start(down[:, s], L.w2[bass.ds(expert, 1)].rearrange(
                            "o (p j) n -> (o p) j n", j=FB)).then_inc(weights_in[s], 16)
                        if l == 1:
                            sp.dma_start(b2[:, s, :], L.b2[bass.ds(expert, 1), :]).then_inc(weights_in[s], 16)

                loop(sp, ETILES // 2, body)

            @block.tensor
            def _(pe):
                def turn(tt, s):
                    t = 2 * tt + s
                    pe.wait_ge(rows_in[s], 16 * (tt + 1))
                    wait(pe, xT_done, t)
                    for a in range(HALVES):
                        mm = pe.transpose(ps_x[:, a * P:(a + 1) * P], rows[:, s, a, :], w["ident"][:, :])
                    mm.then_inc(turned, 1)

                def go_up(tt, s):
                    t = 2 * tt + s
                    pe.wait_ge(xT_done, t + 1)
                    pe.wait_ge(weights_in[s], 16 * WEIGHT_DMAS * (tt + 1))
                    wait(pe, h_done, H_STEPS * (t - 1))
                    for j in range(FB):
                        mm = pe.matmul(ps_h[s][:, j * SLOTS:(j + 1) * SLOTS], up[:, s, j:F:FB], xT[:, s, :],
                                       start=True, stop=True)
                    mm.then_inc(h_mm, 1)

                def go_down(tt, s):
                    t = 2 * tt + s
                    pe.wait_ge(h_done, H_STEPS * (t + 1))
                    wait(pe, y_done, t - 1)
                    for a in range(HALVES):
                        out = ps_y[s][:, a * P:(a + 1) * P]
                        for j in range(FB):
                            mm = pe.matmul(out, hT[:, s, j, a * P:(a + 1) * P], down[:, s, j, :],
                                           start=(j == 0), stop=(l == 0 and j == FB - 1))
                        if l == 1:
                            mm = pe.matmul(out, w["ones"][0:1, :], b2[:, s, :], start=False, stop=True)
                    mm.then_inc(y_mm, 1)

                def body(tt):
                    static = isinstance(tt, int)
                    for s in range(2):
                        if static and tt == 0 and s == 0:
                            turn(0, 0)
                        if not (static and tt == ETILES // 2 - 1 and s == 1):
                            turn(tt + s, 1 - s)
                        go_up(tt, s)
                        if not (static and tt == 0 and s == 0):
                            go_down(tt - 1 + s, 1 - s)
                    if static and tt == ETILES // 2 - 1:
                        go_down(tt, 1)

                loop(pe, ETILES // 2, body)

            @block.scalar
            def _(act):
                def store(tt, s):
                    act.wait_ge(y_done, 2 * tt + s + 1)
                    act.dma_start(out_view[bass.ds(2 * tt + s, 1)].rearrange("o p a n -> (o p) a n"),
                                  y[:, s]).then_inc(y_out[s], 16)

                def body(tt):
                    for s in range(2):
                        t = 2 * tt + s
                        act.wait_ge(h_mm, t + 1)
                        wait(act, y_mm, t - 1)
                        if l == 0:
                            act.activation(hT[:, s].rearrange("p j n -> p (j n)"), ps_h[s][:, :], ACT.Gelu
                                           ).then_inc(h_done, 1)
                        else:
                            act.wait_ge(weights_in[s], 16 * WEIGHT_DMAS * (tt + 1))
                            for j in range(FB):
                                act.activation(hT[:, s, j, :], ps_h[s][:, j * SLOTS:(j + 1) * SLOTS], ACT.Silu,
                                               bias=up[:, s, F + j:F + j + 1]).then_inc(h_done, 1)
                        if not (isinstance(t, int) and t == 0):
                            store(tt - 1 + s, 1 - s)

                loop(act, ETILES // 2, body)
                store(ETILES // 2 - 1, 1)
                for s in range(2):
                    act.wait_ge(y_out[s], 16 * (ETILES // 2))

            @block.vector
            def _(dve):
                def turn(tt, s):
                    t = 2 * tt + s
                    dve.wait_ge(turned, t + 1)
                    wait(dve, h_mm, t - 1)
                    dve.tensor_copy(xT[:, s, :], ps_x[:, 0:SLOTS]).then_inc(xT_done, 1)

                def leave(tt, s):
                    t = 2 * tt + s
                    dve.wait_ge(y_mm, t + 1)
                    wait(dve, y_out[s], 16 * tt)
                    dve.tensor_copy(y[:, s].rearrange("p a n -> p (a n)"), ps_y[s][:, 0:SLOTS]
                                    ).then_inc(y_done, 1)

                def body(tt):
                    static = isinstance(tt, int)
                    for s in range(2):
                        if static and tt == 0 and s == 0:
                            turn(0, 0)
                        if not (static and tt == ETILES // 2 - 1 and s == 1):
                            turn(tt + s, 1 - s)
                        if not (static and tt == 0 and s == 0):
                            leave(tt - 1 + s, 1 - s)
                    if static and tt == ETILES // 2 - 1:
                        leave(tt, 1)

                loop(dve, ETILES // 2, body)


def combine(nc, L, w):
    l = L.index
    with ExitStack() as ctx:
        sb, psum, sem = alloc(nc, ctx)
        S = lambda name: L.semaphore(f"e_{name}")
        N = 4
        x, xn, s_in, shared = (sb(f"e{l}_{n}", [P, N, P]) for n in ("x", "xn", "s", "shared"))
        picked = sb(f"e{l}_picked", [P, N, 2, P])
        ffn, silu, out = (sb(f"e{l}_{n}", [P, 2, P]) for n in ("ffn", "silu", "out"))
        sT = sb(f"e{l}_sT", [P, 2, P])
        index = sb(f"e{l}_index", [P, N, 2], I32)
        ps_t = [psum(f"e{l}_ps_t{i}") for i in range(2)]
        ps_s = [psum(f"e{l}_ps_s{i}") for i in range(2)]
        tile_in = [S(f"tile_in{i}") for i in range(N)]
        picked_in = [L.queue_semaphore(f"picked_in{i}") for i in range(N)]
        out_out = [S(f"out_out{i}") for i in range(2)]
        index_done, summed, gated, stored = S("index"), S("summed"), S("gated"), S("stored")
        partial, product = S("partial"), S("product")
        turned, sT_done, s_mm = S("turned"), S("sT"), S("s_mm")
        LOADS = 4 if l == 0 else 3
        view = lambda a: a.rearrange("(t p) n -> t p n", p=P)
        x_v, s_v, o_v = view(L.x_in), view(L.s), view(L.x_out)
        xn_v = view(L.slots_in[SHARED_ROW:ROWS, :])
        sh_v = view(L.slots_out[SHARED_ROW:ROWS, :])

        with nc.Block() as block:
            @block.sync
            def _(sp):
                def body(tt):
                    for i in range(N):
                        t = N * tt + i
                        wait(sp, stored, t - N + 1)
                        if l == 1:
                            wait(sp, turned, t - N + 1)
                        one = lambda v: v[bass.ds(t, 1)].rearrange("o p n -> (o p) n")
                        sp.dma_start(x[:, i], one(x_v)).then_inc(tile_in[i], 16)
                        sp.dma_start(s_in[:, i], one(s_v)).then_inc(tile_in[i], 16)
                        sp.dma_start(shared[:, i], one(sh_v)).then_inc(tile_in[i], 16)
                        if l == 0:
                            sp.dma_start(xn[:, i], one(xn_v)).then_inc(tile_in[i], 16)

                loop(sp, TILES // N, body)

            @block.gpsimd
            def _(pool):
                def body(tt):
                    for i in range(N):
                        t = N * tt + i
                        wait(pool, stored, t - N + 1)
                        for k in range(2):
                            pool.tensor_copy(index[:, i, k:k + 1], w["slot"][:, k, bass.ds(t, 1)]
                                             ).then_inc(index_done, 1)
                        carried(pool, (index_done, 2), (index_done, 2 * t + 2))
                        for k in range(2):
                            pool.indirect_dma_start(
                                picked[:, i, k, :], None, L.slots_out,
                                bass.IndirectOffsetOnAxis(ap=index[:, i, k:k + 1], axis=0)
                                ).then_inc(picked_in[i], 16)

                loop(pool, TILES // N, body)

            @block.scalar
            def _(act):
                def body(tt):
                    for i in range(N):
                        t = N * tt + i
                        act.wait_ge(summed, t + 1)
                        act.activation(silu[:, i % 2], ffn[:, i % 2], ACT.Silu).then_inc(gated, 1)
                        act.wait_ge(stored, t + 1)
                        act.dma_start(o_v[bass.ds(t, 1)].rearrange("o p n -> (o p) n"), out[:, i % 2]
                                      ).then_inc(out_out[i % 2], 16)

                loop(act, TILES // N, body)
                for i in range(2):
                    act.wait_ge(out_out[i], 16 * TILES // 2)

            @block.tensor
            def _(pe):
                if l == 0:
                    return

                def body(tt):
                    for i in range(N):
                        t = N * tt + i
                        pe.wait_ge(tile_in[i], 16 * LOADS * (tt + 1))
                        wait(pe, sT_done, t - 1)
                        pe.transpose(ps_t[i % 2][:, 0:P], s_in[:, i], w["ident"][:, :]).then_inc(turned, 1)
                        pe.wait_ge(sT_done, t + 1)
                        wait(pe, stored, t - 1)
                        pe.matmul(ps_s[i % 2][:, 0:P], sT[:, i % 2], w["cprojT"][:, :], start=True, stop=False)
                        pe.matmul(ps_s[i % 2][:, 0:P], w["ones"][0:1, :], w["bs1"][:, :],
                                  start=False, stop=True).then_inc(s_mm, 1)

                loop(pe, TILES // N, body)

            @block.vector
            def _(dve):
                def add_up(tt, i):
                    t = N * tt + i
                    dve.wait_ge(tile_in[i], 16 * LOADS * (tt + 1))
                    dve.wait_ge(picked_in[i], 32 * (tt + 1))
                    gate = [w["gate"][:, k, bass.ds(t, 1)] for k in range(2)]
                    acc = ffn[:, i % 2]
                    wait(dve, gated, t - 1)
                    if l == 0:
                        dve.tensor_tensor(acc, shared[:, i], xn[:, i], ALU.add).then_inc(partial, 1)
                    else:
                        dve.tensor_scalar(acc, shared[:, i], 0.1, None, ALU.mult).then_inc(partial, 1)
                    dve.wait_ge(partial, 2 * t + 1)
                    dve.scalar_tensor_tensor(acc, picked[:, i, 0], gate[0], acc, ALU.mult, ALU.add
                                             ).then_inc(partial, 1)
                    dve.wait_ge(partial, 2 * t + 2)
                    dve.scalar_tensor_tensor(acc, picked[:, i, 1], gate[1], acc, ALU.mult, ALU.add
                                             ).then_inc(summed, 1)
                    if l == 1:
                        dve.wait_ge(turned, t + 1)
                        wait(dve, s_mm, t - 1)
                        dve.tensor_copy(sT[:, i % 2], ps_t[i % 2][:, 0:P]).then_inc(sT_done, 1)

                def finish(tt, i):
                    t = N * tt + i
                    dve.wait_ge(gated, t + 1)
                    wait(dve, out_out[i % 2], 16 * ((N // 2) * tt + i // 2))
                    s = s_in[:, i]
                    if l == 1:
                        dve.wait_ge(s_mm, t + 1)
                        s = ps_s[i % 2][:, 0:P]
                    dve.tensor_tensor(out[:, i % 2], s, silu[:, i % 2], ALU.mult).then_inc(product, 1)
                    dve.wait_ge(product, t + 1)
                    dve.tensor_tensor(out[:, i % 2], out[:, i % 2], x[:, i], ALU.add).then_inc(stored, 1)

                def body(tt):
                    for i in range(N):
                        if isinstance(tt, int) and tt == 0 and i == 0:
                            add_up(0, 0)
                        if not (isinstance(tt, int) and tt == TILES // N - 1 and i == N - 1):
                            add_up(tt + (i + 1) // N, (i + 1) % N)
                        finish(tt, i)

                loop(dve, TILES // N, body)


def attend(nc, L, w):
    l = L.index
    LEAD = 7
    UNITS = BATCH * GROUPS
    STEPS = UNITS * TPB
    PER_BATCH = GROUPS * TPB
    PARTS = L.products
    ROW = L.head_rows
    causal = l == 1
    with ExitStack() as ctx:
        sb, psum, sem = alloc(nc, ctx)
        S = lambda name: L.semaphore(f"d_{name}")
        q = [sb(f"d{l}_q{g}", [P, GH, SEQ], F32R) for g in range(GROUPS)]
        k = [sb(f"d{l}_k{g}", [P, GH, SEQ], F32R) for g in range(GROUPS)]
        v = sb(f"d{l}_v", [P, GROUPS, TPB, GH, VC])
        probs = sb(f"d{l}_probs", [P, 2, GH, SEQ])
        maxima = sb(f"d{l}_maxima", [P, GH, TPB])
        m_parts = sb(f"d{l}_m_parts", [P, 2, GH, TPB])
        mT = sb(f"d{l}_mT", [2 * GH * TPB, 2, P])
        o = sb(f"d{l}_o", [P, SEQ])
        inv = sb(f"d{l}_inv", [P, TPB, GH])
        out = sb(f"d{l}_out", [P, TPB, P])
        ps_s = [psum(f"d{l}_ps_s{i}", 2) for i in range(2)]
        ps_m = [psum(f"d{l}_ps_m{i}") for i in range(2)]
        ps_o = psum(f"d{l}_ps_o")
        ps_t = psum(f"d{l}_ps_t")

        qk_in = [S(f"qk_in{g}") for g in range(GROUPS)]
        m_in = [S(f"m_in{g}") for g in range(GROUPS)]
        out_out = S("out_out")
        cleared, m_mm, m_read, m_max, m_hi, m_split = (
            S("cleared"), S("m_mm"), S("m_read"), S("m_max"), S("m_hi"), S("m_split"))
        m_turned, mT_done = S("m_turned"), S("mT")
        s_mm, exps, pv, o_copied, o_turned, o_inv, o_done = (
            S("s_mm"), S("exps"), S("pv"), S("o_copied"), S("o_turned"), S("o_inv"), S("o_done"))
        minus_one, o_zero = S("minus_one"), S("o_zero")
        LOADS = 2 * len(PARTS) + 1

        out_view = L.s.rearrange("(b t p) n -> b p t n", t=TPB, p=P)
        v_view = L.v.rearrange("(b p) (t h c) -> b p t h c", p=P, t=TPB, h=HEADS)

        def at(b, offset):
            turns, rest = divmod(offset, PER_BATCH)
            b = b + turns
            return b, rest // TPB, rest % TPB, PER_BATCH * b + rest, GROUPS * b + rest // TPB

        def all_steps(eng, step):
            for n in range(-LEAD, 0):
                step(0, n)
            def body(b):
                for n in range(PER_BATCH):
                    step(b, n)
            loop(eng, BATCH, body)
            for n in range(TPB):
                step(BATCH, n)

        def width(qb):
            return (qb + 1) * P if causal else SEQ

        def first(kb):
            return kb * P if causal else 0

        with nc.Block() as block:
            @block.sync
            def _(sp):
                def load(b, g):
                    u = GROUPS * b + g
                    wait(sp, pv, TPB * (u - GROUPS + 1))
                    tokens = bass.ds(b * SEQ, SEQ)
                    for i, pair in enumerate(PARTS):
                        for dst, src, part in ((q, L.q, pair[0]), (k, L.k, pair[1])):
                            rows = src[part, g * GH * ROW:(g + 1) * GH * ROW, tokens]
                            sp.dma_start(dst[g][i * ROW:(i + 1) * ROW, :, :].bitcast(F32),
                                         rows.rearrange("(h r) t -> r h t", h=GH)).then_inc(qk_in[g], 16)
                    sp.dma_start(v[:, g], v_view[bass.ds(b, 1), :, :, g * GH:(g + 1) * GH, :].rearrange(
                        "o p t h c -> (o p) t (h c)")).then_inc(qk_in[g], 16)

                def step(b, offset):
                    _, _, kb, _, u = at(b, offset)
                    if kb == 1 and inside(at(b, offset + 3 * TPB)[4], UNITS) and not (
                            isinstance(u, int) and u < 0):
                        load(*at(b, offset + 3 * TPB)[0:2])
                    if kb == 2 and inside(u + 1, UNITS):
                        nb, ng, _, _, nu = at(b, offset + TPB)
                        sp.wait_ge(mT_done, nu + 1)
                        for part in range(2):
                            rows = mT[part * GH * TPB:(part + 1) * GH * TPB, ng % 2, :]
                            dst = q[ng][M_ROW + part:M_ROW + part + 1, :, :].bitcast(F32)
                            sp.dma_start(dst.rearrange("o h (t n) -> o (h t) n", n=P), rows
                                           ).then_inc(m_in[ng], 16)
                    if kb == TPB - 1:
                        ob, og, _, _, ou = at(b, offset - TPB)
                        if og == GROUPS - 1 and inside(ou, UNITS):
                            sp.wait_ge(o_done, ou + 1)
                            sp.dma_start(out_view[bass.ds(ob, 1)].rearrange("o p t n -> (o p) t n"),
                                           out[:, :, :]).then_inc(out_out, 16)

                sp.wait_ge(cleared, 2 * GROUPS)
                for g in range(3):
                    load(0, g)
                all_steps(sp, step)
                sp.wait_ge(out_out, 16 * BATCH)

            @block.gpsimd
            def _(pool):
                for g in range(GROUPS):
                    pool.memset(q[g][:, :, :].bitcast(F32), 0.0).then_inc(cleared, 1)
                    pool.memset(k[g][:, :, :].bitcast(F32), 0.0).then_inc(cleared, 1)
                pool.wait_ge(cleared, 2 * GROUPS)
                for g in range(GROUPS):
                    pool.memset(k[g][M_ROW:M_ROW + 2, :, :].bitcast(F32), -1.0).then_inc(minus_one, 1)

            @block.scalar
            def _(act):
                def step(b, offset):
                    _, _, kb, n, u = at(b, offset)
                    for pair in range(2):
                        if inside(n, STEPS):
                            act.wait_ge(s_mm, 2 * n + pair + 1)
                            wait(act, pv, n - 1)
                            wide = SEQ - first(kb)
                            act.activation(
                                probs[:, offset % 2, 2 * pair:2 * pair + 2, 0:wide],
                                ps_s[pair][:, :].rearrange("p (h n) -> p h n", h=2)[:, :, 0:wide],
                                ACT.Exp, scale=L.scale).then_inc(exps, 1)
                        if pair == 0 and kb == 1 and inside(u - 1, UNITS):
                            act.wait_ge(pv, TPB * u)
                            wait(act, o_turned, u - 1)
                            act.activation(o[:, :], ps_o[:, :], ACT.Copy).then_inc(o_copied, 1)

                all_steps(act, step)

            @block.vector
            def _(dve):
                dve.memset(ps_o[:, :], 0.0).then_inc(o_zero, 1)

                def step(b, offset):
                    _, g, kb, n, u = at(b, offset)
                    mb, mg, qb, m, mu = at(b, offset + LEAD)
                    for h in range(GH):
                        if inside(m, STEPS):
                            dve.wait_ge(m_mm, GH * m + h + 1)
                            if qb == 0 and h == 0:
                                wait(dve, m_split, mu)
                            dve.tensor_reduce(maxima[:, h, qb:qb + 1], ps_m[h % 2][:, 0:width(qb)],
                                              AX.X, ALU.max).then_inc(m_read, 1)
                        if h == 1 and kb == 2 and inside(u + 1, UNITS):
                            _, ng, _, _, nu = at(b, offset + TPB)
                            dve.wait_ge(m_turned, nu + 1)
                            before = at(b, offset - TPB)
                            if inside(before[4], UNITS):
                                dve.wait_ge(m_in[before[1]], 32 * (before[0] + 1))
                            dve.tensor_copy(mT[:, ng % 2, :], ps_t[0:2 * GH * TPB, 0:P]).then_inc(mT_done, 1)
                        if h == 1 and kb == 3 and inside(u - 1, UNITS):
                            ob, og, _, _, ou = at(b, offset - TPB)
                            dve.wait_ge(o_turned, ou + 1)
                            if og == 0:
                                wait(dve, out_out, 16 * ob)
                            ov = ps_t[:, :].rearrange("p (t h c) -> p t h c", t=TPB, h=GH)
                            dve.reciprocal(inv[:, :, :], ov[:, :, :, HD]).then_inc(o_inv, 1)
                            dve.wait_ge(o_inv, ou + 1)
                            for t in range(TPB):
                                ins = dve.tensor_tensor(
                                    out[:, t, og * GH * HD:(og + 1) * GH * HD].rearrange("p (h c) -> p h c", h=GH),
                                    ov[:, t, :, 0:HD],
                                    inv[:, t, :].unsqueeze(2).to_broadcast([P, GH, HD]), ALU.mult)
                            ins.then_inc(o_done, 1)
                    if qb == TPB - 1 and inside(m, STEPS):
                        dve.wait_ge(m_read, GH * (m + 1))
                        wait(dve, m_turned, mu)
                        dve.tensor_copy(m_parts[:, 0].bitcast(F32R), maxima[:, :, :]).then_inc(m_hi, 1)
                        dve.wait_ge(m_hi, mu + 1)
                        dve.tensor_tensor(m_parts[:, 1].bitcast(F32R), maxima[:, :, :], m_parts[:, 0],
                                          ALU.subtract).then_inc(m_split, 1)

                all_steps(dve, step)

            @block.tensor
            def _(pe):
                pe.wait_ge(minus_one, GROUPS)
                pe.wait_ge(o_zero, 1)

                def scores(b, offset):
                    _, g, kb, n, u = at(b, offset)
                    if kb == 0:
                        pe.wait_ge(m_in[g], 32 * (at(b, offset)[0] + 1))
                    for pair in range(2):
                        wait(pe, exps, 2 * n + pair - 1)
                        for i in range(2):
                            h = 2 * pair + i
                            out_ps = ps_s[pair][:, i * SEQ:(i + 1) * SEQ - first(kb)]
                            mm = pe.matmul(out_ps, k[g][0:M_ROW + 2, h, kb * P:(kb + 1) * P],
                                           q[g][0:M_ROW + 2, h, first(kb):SEQ], start=True, stop=not causal)
                            if causal:
                                mm = pe.matmul(out_ps[:, 0:P], w["ident_bf"][:, :], w["mask_k"][:, :],
                                               start=False, stop=True)
                        mm.then_inc(s_mm, 1)

                def for_maxima(b, offset):
                    mb, g, qb, m, mu = at(b, offset)
                    if qb == 0:
                        pe.wait_ge(qk_in[g], 16 * LOADS * (mb + 1))
                    for h in range(GH):
                        wait(pe, m_read, GH * m + h - 1)
                        wide = width(qb)
                        mm = pe.matmul(ps_m[h % 2][:, 0:wide], q[g][0:M_ROW, h, qb * P:(qb + 1) * P],
                                       k[g][0:M_ROW, h, 0:wide], start=True, stop=not causal)
                        if causal:
                            mm = pe.matmul(ps_m[h % 2][:, qb * P:wide], w["ident_bf"][:, :], w["mask_q"][:, :],
                                           start=False, stop=True)
                        mm.then_inc(m_mm, 1)

                def with_v(b, offset):
                    _, g, kb, n, u = at(b, offset)
                    pe.wait_ge(exps, 2 * n + 2)
                    if kb == 0:
                        wait(pe, o_copied, u)
                    for h in range(GH):
                        mm = pe.matmul(ps_o[32 * h:32 * h + VC, first(kb):SEQ], v[:, g, kb, h, :],
                                       probs[:, offset % 2, h, 0:SEQ - first(kb)],
                                       start=(kb == 0), stop=(kb == TPB - 1), tile_position=(0, 32 * h))
                    mm.then_inc(pv, 1)

                def step(b, offset):
                    _, g, kb, n, u = at(b, offset)
                    if inside(n, STEPS):
                        scores(b, offset)
                    if inside(at(b, offset + LEAD)[3], STEPS):
                        for_maxima(b, offset + LEAD)
                    if inside(at(b, offset - 1)[3], STEPS):
                        with_v(b, offset - 1)
                    if kb == 1 and inside(u + 1, UNITS):
                        nu = at(b, offset + TPB)[4]
                        pe.wait_ge(m_split, nu + 1)
                        wait(pe, o_done, nu - 2)
                        pe.transpose(ps_t[0:2 * GH * TPB, 0:P], m_parts[:, :, :, :].rearrange("p a h t -> p (a h t)"),
                                     w["ident"][:, :]).then_inc(m_turned, 1)
                    if kb == 2 and inside(u - 1, UNITS):
                        pe.wait_ge(o_copied, u)
                        wait(pe, o_done, u - 1)
                        wait(pe, mT_done, min(u + 2, UNITS) if isinstance(u, int) else u + 2)
                        for t in range(TPB):
                            mm = pe.transpose(ps_t[:, t * P:(t + 1) * P], o[:, t * P:(t + 1) * P], w["ident"][:, :])
                        mm.then_inc(o_turned, 1)

                all_steps(pe, step)


def build(nc, d, out):
    with ExitStack() as ctx:
        sb, _, _ = alloc(nc, ctx)
        w = {n: sb(n, [P, P]) for n in ("ident", "tri", "wq0", "wk0", "wv0", "wv1", "wqk", "cprojT", "ones")}
        for n in ("wr0", "wr1"):
            w[n] = sb(n, [P, E])
        for n in ("bq0", "bk0", "bqk", "eps"):
            w[n] = sb(n, [P, 1])
        for n in ("bv0", "bv1", "bs1"):
            w[n] = sb(n, [1, P])
        for n in ("waq", "wbq", "wak", "wbk", "cos", "sin"):
            w[n] = sb(n, [P, HEADS * LAT])
        for n in ("baq", "bbq", "bak", "bbk"):
            w[n] = sb(n, [P, GROUPS])
        for n in ("ident_bf", "mask_q", "mask_k"):
            w[n] = sb(n, [P, P], BF16)
        w["zeros"] = sb("zeros", [P, 16 * P])
        w["logits"] = sb("logits", [P, TILES, E])
        w["gate"] = sb("gate", [P, 2, TILES])
        w["slot"] = sb("slot", [P, 2, TILES], I32)
        w["tile_f"] = sb("tile_f", [P, ETILES])
        w["tile_expert"] = sb("tile_expert", [P, ETILES], I32)

        def scratch(name, shape):
            return nc.dram_tensor(name, shape, F32, kind="Internal").ap()

        layers, semaphores = [], {}
        for l in range(2):
            L = Layer(nc, semaphores)
            L.index = l
            rows = (HD, LAT)[l]
            L.head_rows = rows
            L.products = [(0, 0), (0, 1), (1, 0)] + [(1, 1)] * (l == 0)
            L.scale = float(rows) ** -0.5
            L.q, L.k = (scratch(f"{n}{l}", [2, HEADS * rows, TOKENS]) for n in "qk")
            L.v = scratch(f"v{l}", [BATCH * P, TPB * HEADS * VC])
            L.slots_in, L.slots_out = scratch(f"slots_in{l}", [ROWS, P]), scratch(f"slots_out{l}", [ROWS, P])
            L.s = scratch(f"s{l}", [TOKENS, P])
            L.x_in = d["x"] if l == 0 else layers[0].x_out
            L.x_out = scratch("x1", [TOKENS, P]) if l == 0 else out
            L.wr, L.wv, L.bv = w[f"wr{l}"], w[f"wv{l}"], w[f"bv{l}"]
            L.w1, L.w2, L.b2, L.up_width = d[f"up{l}"], d[f"down{l}"], d["b2"], (F, F + FB)[l]
            layers.append(L)

        load_constants(nc, d, w)
        for L in layers:
            if L.index > 0:
                clear(nc, semaphores)
            prepare(nc, L, d, w)
            dispatch(nc, L, w)
            experts(nc, L, w)
            attend(nc, L, w)
            combine(nc, L, w)


def layout(i):
    a = {n: np.ascontiguousarray(x) for n, x in i.items()}
    col = lambda x: x.reshape(-1, 1)
    row = lambda x: x.reshape(1, -1)
    d = {"x": a["L0_attn_x"].reshape(TOKENS, P)}
    d["wqT"], d["wkT"], d["wv0"] = a["L0_attn_Wq"].T, a["L0_attn_Wk"].T, a["L0_attn_Wv"]
    d["bq"], d["bk"], d["bv0"] = col(a["L0_attn_bq"]), col(a["L0_attn_bk"]), row(a["L0_attn_bv"])
    d["wpx"] = np.tile(a["L0_attn_Wp"], (HEADS, HEADS))
    d["wr0"], d["wr1"] = a["L0_ffn_router_w"], a["L1_ffn_Wg"]
    d["up0"] = np.concatenate([a["L0_ffn_routed_up"], a["L0_ffn_shared_up"]])
    d["down0"] = np.concatenate([a["L0_ffn_routed_down"], a["L0_ffn_shared_down"]])
    d["cq"], d["ck"], d["cv"] = a["L1_attn_c_attn_w"].reshape(3, P, P)
    d["cqb"], d["ckb"], d["cvb"] = a["L1_attn_c_attn_b"].reshape(3, P, 1)
    d["q2lx"] = np.tile(a["L1_attn_q2l_w"].T, (HEADS, HEADS))
    d["kv2lx"] = np.tile(a["L1_attn_kv2l_w"].T, (HEADS, HEADS))
    d["q2lbx"], d["kv2lbx"] = col(np.tile(a["L1_attn_q2l_b"], GH)), col(np.tile(a["L1_attn_kv2l_b"], GH))
    d["kv2lrep"] = np.tile(a["L1_attn_kv2l_w"], (1, HEADS))
    d["kv2lb"] = col(a["L1_attn_kv2l_b"])
    d["l2orep"] = np.tile(a["L1_attn_l2o_w"].T, (1, HEADS))
    d["l2obx"] = col(np.tile(a["L1_attn_l2o_b"], HEADS))
    d["wqkx"] = np.tile(a["L1_attn_wqk_w"].T, (GH, GH))
    d["bqk"] = col(np.tile(a["L1_attn_wqk_b"], GH))
    d["cprojT"], d["cprojb"] = a["L1_attn_cproj_w"].T, row(a["L1_attn_cproj_b"])
    b1 = np.concatenate([a["L1_ffn_b1"], row(a["L1_ffn_bs1"])]).reshape(E + 1, P, FB)
    d["up1"] = np.concatenate([np.concatenate([a["L1_ffn_W1"], a["L1_ffn_Ws1"][None]]), b1], axis=2)
    d["down1"] = np.concatenate([a["L1_ffn_W2"], a["L1_ffn_Ws2"][None]])
    d["b2"] = np.concatenate([a["L1_ffn_b2"], row(a["L1_ffn_bs2"])])

    n = np.arange(P)
    d["ident"] = np.eye(P)
    d["tri"] = n[:, None] < n[None, :]
    d["mask8"] = n[:, None] // HD == n[None, :] // HD
    d["mask32"] = n[:, None] // HD == np.arange(HEADS * LAT)[None, :] // LAT
    d["mask32x32"] = n[:, None] // LAT == n[None, :] // LAT
    d["rot"] = (n[:, None] == n[None, :] - 1) * (n[None, :] % 2) * 1.0 - (n[:, None] == n[None, :] + 1) * (1 - n[None, :] % 2)
    steps = np.arange(0, LAT, 2, dtype=np.float32) / np.float32(LAT)
    freq = np.float32(1.0) / np.power(np.float32(10000.0), steps)
    angle = np.repeat(np.outer(np.arange(SEQ, dtype=np.float32), freq), 2, axis=1).T
    d["cos"], d["sin"] = np.tile(np.cos(angle), (GH, 1)), np.tile(np.sin(angle), (GH, 1))
    return {name: np.ascontiguousarray(x, dtype=np.float32) for name, x in d.items()}


def kernel(**inputs):
    import concourse.bacc as bacc
    from concourse.bass_utils import run_bass_kernel_spmd

    nc = bacc.Bacc("TRN2", target_bir_lowering=False, num_devices=1)
    arrays = {f"in_{name}": x for name, x in layout(inputs).items()}
    d = {name: nc.dram_tensor(name, x.shape, F32, kind="ExternalInput").ap() for name, x in arrays.items()}
    out = nc.dram_tensor("out", [TOKENS, P], F32, kind="ExternalOutput").ap()
    build(nc, {name.removeprefix("in_"): ap for name, ap in d.items()}, out)
    r = run_bass_kernel_spmd(nc, [arrays], core_ids=[0])
    return r.results[0]["out"].reshape(BATCH, SEQ, P)
```

```python
from contextlib import ExitStack

import numpy as np

import concourse.bass as bass
from concourse import mybir

F32 = mybir.dt.float32
F32R = mybir.dt.float32r
BF16 = mybir.dt.bfloat16
I32 = mybir.dt.int32
ALU = mybir.AluOpType
ACT = mybir.ActivationFunctionType
AX = mybir.AxisListType

P = 128
BATCH, SEQ = 16, 512
TOKENS = BATCH * SEQ
TILES = TOKENS // P
TPB = SEQ // P
HEADS, HD = 16, 8
GH = 4
GROUPS = HEADS // GH
VC = HD + 1
LAT = 32
E, F = 8, 512
FB = F // P
SLOTS = 256
HALVES = SLOTS // P
ROUTED = (2 * TOKENS + E * (SLOTS - 1)) // SLOTS
ROUTED += ROUTED % 2
SHARED = TOKENS // SLOTS
ETILES = ROUTED + SHARED
ROWS = ETILES * SLOTS
SHARED_ROW = ROUTED * SLOTS
M_ROW = 96
EPS = 1e-5
MASKED = -1e30


def wait(eng, sem, value):
    if not isinstance(value, int) or value > 0:
        eng.wait_ge(sem, value)


def carried(eng, first, *waits):
    for _, v in waits:
        if not isinstance(v, int):
            eng.compute_val(v)
    eng.wait_ge(*first)
    for sem, v in waits:
        eng.wait_ge(sem, v)


def inside(value, count):
    return not isinstance(value, int) or 0 <= value < count


def loop(eng, count, body):
    body(0)
    with eng.Fori(1, count - 1) as i:
        body(i)
    body(count - 1)


class Layer:

    def __init__(self, nc, semaphores):
        self.nc, self.semaphores = nc, semaphores

    def semaphore(self, name):
        if name not in self.semaphores:
            self.semaphores[name] = self.nc.alloc_semaphore(name)
        return self.semaphores[name]


    def queue_semaphore(self, name):
        return self.nc.alloc_semaphore(f"{name}_{self.index}")


def clear(nc, semaphores):
    every = list(semaphores.values())
    with nc.Block() as block:
        @block.sync
        def _(sp):
            for s in every[0::4]:
                sp.sem_clear(s)

        @block.gpsimd
        def _(pool):
            for s in every[1::4]:
                pool.sem_clear(s)

        @block.scalar
        def _(act):
            for s in every[2::4]:
                act.sem_clear(s)

        @block.vector
        def _(dve):
            for s in every[3::4]:
                dve.sem_clear(s)


def alloc(nc, ctx):
    def sb(name, shape, dt=F32):
        return ctx.enter_context(nc.sbuf_tensor(name, shape, dt))

    def psum(name, banks=1):
        return ctx.enter_context(nc.psum_tensor(name, [P, banks * SEQ], F32))

    def sem(name):
        return nc.alloc_semaphore(name)

    return sb, psum, sem


def load_constants(nc, d, w):
    with ExitStack() as ctx:
        sb, psum, sem = alloc(nc, ctx)
        loaded, folded, copied, ready = sem("w_loaded"), sem("w_folded"), sem("w_copied"), sem("w_ready")
        masks_zero = sem("w_masks_zero")
        ps = [psum(f"w_ps{i}") for i in range(2)]
        t = {}
        for name in ("wqT", "wkT", "wpx", "cq", "ck", "cv", "mask8", "mask32x32", "rot", "wqkx"):
            t[name] = sb("t_" + name, [P, P])
        for name in ("q2lx", "kv2lx", "mask32"):
            t[name] = sb("t_" + name, [P, HEADS * LAT])
        for name in ("kv2lrep", "l2orep"):
            t[name] = sb("t_" + name, [LAT, P])
        for name in ("bq", "bk", "cqb", "ckb", "cvb", "q2lbx", "kv2lbx", "l2obx"):
            t[name] = sb("t_" + name, [P, 1])
        kv2lb = sb("t_kv2lb", [LAT, 1])
        cprojb = sb("t_cprojb", [1, P])
        bd = {n: sb("bd_" + n, [P, P]) for n in ("wp", "v")}
        for n in ("q", "k"):
            bd[n] = sb("bd_" + n, [P, HEADS * LAT])

        loads = [(t[n], d[n]) for n in t] + [(kv2lb, d["kv2lb"]), (cprojb, d["cprojb"])]
        loads += [(w[n], d[n]) for n in ("ident", "tri", "cos", "sin", "wv0", "bv0", "wr0", "wr1",
                                         "bqk", "cprojT")]
        folds = []

        def fold(m, n, products, evacuate):
            folds.append((m, n, products, evacuate))

        def copy_to(out):
            return lambda eng, p: [eng.tensor_copy(out, p)]

        fold(P, P, [(t["wqT"], bd["wp"])], copy_to(w["wq0"][:, :]))
        fold(P, P, [(t["wkT"], bd["wp"])], copy_to(w["wk0"][:, :]))
        fold(P, 1, [(bd["wp"], t["bq"])], copy_to(w["bq0"][:, :]))
        fold(P, 1, [(bd["wp"], t["bk"])], copy_to(w["bk0"][:, :]))
        for s, c, x, lb in (("q", "cq", "cqb", "q2lbx"), ("k", "ck", "ckb", "kv2lbx")):
            def both(eng, p, s=s):
                turned = w["wb" + s][:, :].rearrange("p (j two) -> p j two", two=2)
                plain = p.rearrange("p (j two) -> p j two", two=2)
                return [eng.tensor_copy(w["wa" + s][:, :], p),
                        eng.tensor_scalar(turned[:, :, 0], plain[:, :, 1], -1.0, None, ALU.mult),
                        eng.tensor_copy(turned[:, :, 1], plain[:, :, 0])]
            fold(P, HEADS * LAT, [(t[c], bd[s])], both)
            for g in range(GROUPS):
                def bias(eng, p, s=s, g=g, lb=lb):
                    return [eng.tensor_tensor(w["ba" + s][:, g:g + 1], p, t[lb][:, :], ALU.add)]
                fold(P, 1, [(bd[s][:, g * P:(g + 1) * P], t[x])], bias)
            fold(P, GROUPS, [(t["rot"], w["ba" + s])], copy_to(w["bb" + s][:, :]))
        fold(P, P, [(t["kv2lrep"], t["l2orep"])],
             lambda eng, p: [eng.tensor_tensor(bd["v"][:, :], p, t["mask8"][:, :], ALU.mult)])
        fold(P, P, [(t["cv"], bd["v"])], copy_to(w["wv1"][:, :]))
        fold(1, P, [(t["cvb"], bd["v"]), (kv2lb, t["l2orep"])], copy_to(w["bv1"][:, :]))
        fold(1, P, [(t["l2obx"], w["cprojT"])],
             lambda eng, p: [eng.tensor_tensor(w["bs1"][:, :], p, cprojb[:, :], ALU.add)])
        MASKS = 6

        with nc.Block() as block:
            @block.sync
            def _(sp):
                for out, src in loads:
                    sp.dma_start(out[:, :], src).then_inc(loaded, 16)

            @block.vector
            def _(dve):
                dve.memset(w["ones"][:, :], 1.0)
                dve.memset(w["eps"][:, :], EPS)
                dve.wait_ge(loaded, 16 * len(loads))
                dve.tensor_copy(w["ident_bf"][:, :], w["ident"][:, :]).then_inc(ready, 1)
                dve.tensor_tensor(bd["wp"][:, :], t["wpx"][:, :], t["mask8"][:, :], ALU.mult).then_inc(ready, 1)
                dve.tensor_tensor(bd["q"][:, :], t["q2lx"][:, :], t["mask32"][:, :], ALU.mult).then_inc(ready, 1)
                dve.tensor_tensor(bd["k"][:, :], t["kv2lx"][:, :], t["mask32"][:, :], ALU.mult).then_inc(ready, 1)
                dve.tensor_tensor(w["wqk"][:, :], t["wqkx"][:, :], t["mask32x32"][:, :], ALU.mult).then_inc(ready, 1)
                dve.memset(w["zeros"][:, :], 0.0).then_inc(ready, 1)
                for i, (m, n, _, evacuate) in enumerate(folds):
                    dve.wait_ge(folded, i + 1)
                    evacuate(dve, ps[i % 2][0:m, 0:n])[-1].then_inc(copied, 1)

            @block.tensor
            def _(pe):
                pe.wait_ge(ready, MASKS)
                for i, (m, n, products, _) in enumerate(folds):
                    wait(pe, copied, i)
                    for j, (a, b) in enumerate(products):
                        mm = pe.matmul(ps[i % 2][0:m, 0:n], a[:, :], b[:, :],
                                       start=(j == 0), stop=(j == len(products) - 1))
                    mm.then_inc(folded, 1)

            @block.gpsimd
            def _(pool):
                pool.memset(w["mask_q"][:, :], 0.0).then_inc(masks_zero, 1)
                pool.memset(w["mask_k"][:, :], 0.0).then_inc(masks_zero, 1)
                pool.wait_ge(masks_zero, 2)
                pool.affine_select(out=w["mask_q"][:, :], in_=w["mask_q"][:, :], compare_op=ALU.is_ge,
                                   fill=MASKED, base=0, pattern=[[-1, P]], channel_multiplier=1)
                pool.affine_select(out=w["mask_k"][:, :], in_=w["mask_k"][:, :], compare_op=ALU.is_ge,
                                   fill=MASKED, base=0, pattern=[[1, P]], channel_multiplier=-1)


def prepare(nc, L, d, w):
    l = L.index
    jobs = 2 if l == 0 else 2 * GROUPS
    with ExitStack() as ctx:
        sb, psum, sem = alloc(nc, ctx)
        S = lambda name: L.semaphore(f"a_{name}")
        x = sb(f"a{l}_x", [P, 2, TPB, P])
        stats = sb(f"a{l}_stats", [P, 2, TPB, 6])
        mean_var = sb(f"a{l}_mv", [P, 2, TPB, 2])
        sd = sb(f"a{l}_sd", [P, 2, TPB])
        rstd = sb(f"a{l}_rstd", [P, 2, TPB])
        xn = sb(f"a{l}_xn", [P, 2, TPB, P])
        xT = sb(f"a{l}_xT", [P, 2, SEQ])
        v = sb(f"a{l}_v", [P, 2, TPB, HEADS, VC])
        parts = sb(f"a{l}_parts", [P, 2, 2, SEQ], F32R)
        roped = sb(f"a{l}_roped", [P, 2, 3, SEQ])
        ps_x = psum(f"a{l}_ps_x")
        ps_r = psum(f"a{l}_ps_r")[:, 0:TPB * E].rearrange("p (t e) -> p t e", e=E)
        ps_v = psum(f"a{l}_ps_v")[:, :].rearrange("p (t n) -> p t n", n=P)
        ps_j = [[psum(f"a{l}_ps_j{i}{k}") for k in range(2)] for i in range(2)]
        ps_q = psum(f"a{l}_ps_q")

        zeroed = S("zeroed")
        x_in = [S(f"x_in{s}") for s in range(2)]
        xn_out = [S(f"xn_out{s}") for s in range(2)]
        v_out = [S(f"v_out{s}") for s in range(2)]
        parts_out = [S(f"parts_out{s}") for s in range(2)]
        var_done, sd_done, normed, stat = S("var"), S("sd"), S("normed"), S("stat")
        turned, xT_done = S("turned"), S("xT")
        routed, logits_done = S("routed"), S("logits")
        v_mm, v_done, v_ones = S("v_mm"), S("v_done"), S("v_ones")
        proj, mixed, summed = S("proj"), S("mixed"), S("summed")
        q_mm, hi_done, lo_done = S("q_mm"), S("hi"), S("lo")
        lo_pool = S("lo_pool")
        sem_chain = S("chain")

        x_view = L.x_in.rearrange("(b t p) n -> b p t n", t=TPB, p=P)
        xn_view = L.slots_in[SHARED_ROW:ROWS, :].rearrange("(b t p) n -> b p t n", t=TPB, p=P)
        v_view = L.v.rearrange("(b p) n -> b p n", p=P)
        z_view = L.slots_in[0:SHARED_ROW, :].rearrange("(z p r) n -> z p (r n)", p=P, r=16)

        def bias_of(j):
            return (w["bq0"], w["bk0"])[j][:, 0:1] if l == 0 else w["bqk"][:, 0:1]

        with nc.Block() as block:
            @block.sync
            def _(sp):
                for z in range(SHARED_ROW // (16 * P)):
                    sp.dma_start(z_view[z], w["zeros"][:, :]).then_inc(zeroed, 16)

                def load(bb, s):
                    b = 2 * bb + s
                    wait(sp, normed, TPB * (b - 1))
                    sp.dma_start(x[:, s], x_view[bass.ds(b, 1)].rearrange("o p t n -> (o p) t n")
                                 ).then_inc(x_in[s], 16)

                def body(bb):
                    for s in range(2):
                        b = 2 * bb + s
                        if isinstance(bb, int) and b == 0:
                            load(0, 0)
                            load(0, 1)
                        sp.wait_ge(normed, TPB * (b + 1))
                        sp.dma_start(xn_view[bass.ds(b, 1)].rearrange("o p t n -> (o p) t n"), xn[:, s]
                                     ).then_inc(xn_out[s], 16)
                        if not isinstance(bb, int) or bb < BATCH // 2 - 1:
                            load(bb + 1, s)
                        for j in range(jobs):
                            n = jobs * b + j
                            sp.wait_ge(hi_done, n + 1)
                            if l == 0 or j % 2 == 0:
                                sp.wait_ge(lo_done, (jobs * b + j if l == 0 else (jobs * b + j) // 2) + 1)
                            else:
                                sp.wait_ge(lo_pool, (jobs * b + j) // 2 + 1)
                            dst = (L.q, L.k)[j % 2][:, (j // 2) * P:(j // 2 + 1) * P, bass.ds(b * SEQ, SEQ)]
                            sp.dma_start(dst.rearrange("r f t -> f r t"), parts[:, j % 2].bitcast(F32)
                                         ).then_inc(parts_out[j % 2], 16)
                        sp.wait_ge(v_done, b + 1)
                        sp.dma_start(v_view[bass.ds(b, 1)].rearrange("o p n -> (o p) n"),
                                     v[:, s].rearrange("p t h c -> p (t h c)")).then_inc(v_out[s], 16)

                loop(sp, BATCH // 2, body)
                sp.wait_ge(zeroed, 16 * (SHARED_ROW // (16 * P)))
                for s in range(2):
                    sp.wait_ge(xn_out[s], 16 * (BATCH // 2))
                    sp.wait_ge(v_out[s], 16 * (BATCH // 2))
                    sp.wait_ge(parts_out[s], 16 * BATCH * jobs // 2)

            @block.vector
            def _(dve):
                dve.memset(v[:, :, :, :, HD:VC], 1.0).then_inc(v_ones, 1)

                def norm(bb, s):
                    b = 2 * bb + s
                    dve.wait_ge(x_in[s], 16 * (bb + 1))
                    for t in range(TPB):
                        dve.bn_stats(stats[:, s, t, :], x[:, s, t, :]).then_inc(stat, 1)
                    carried(dve, (stat, 1), (stat, TPB * (b + 1)))
                    for t in range(TPB):
                        dve.bn_aggr(mean_var[:, s, t, :], stats[:, s, t, :]).then_inc(var_done, 1)
                    dve.wait_ge(sd_done, b + 1)
                    dve.reciprocal(rstd[:, s, :], sd[:, s, :]).then_inc(sem_chain, 1)
                    dve.wait_ge(sem_chain, b + 1)
                    wait(dve, xn_out[s], 16 * bb)
                    wait(dve, turned, b - 1)
                    for t in range(TPB):
                        dve.tensor_scalar(xn[:, s, t, :], x[:, s, t, :], mean_var[:, s, t, 0:1],
                                          rstd[:, s, t:t + 1], ALU.subtract, ALU.mult).then_inc(normed, 1)

                def body(bb):
                    for s in range(2):
                        b = 2 * bb + s
                        if isinstance(bb, int) and bb == 0 and s == 0:
                            norm(0, 0)
                        if not (isinstance(bb, int) and b == BATCH - 1):
                            norm(bb + s, 1 - s)
                        dve.wait_ge(routed, b + 1)
                        dve.tensor_copy(w["logits"][:, bass.ds(b * TPB, TPB), :], ps_r[:, :, :]
                                        ).then_inc(logits_done, 1)
                        for j in range(jobs):
                            n = jobs * b + j
                            if l == 0:
                                dve.wait_ge(hi_done, n + 1)
                                dve.scalar_tensor_tensor(parts[:, j, 1, :], ps_j[j][0][:, :], bias_of(j),
                                                         parts[:, j, 0, :], ALU.add, ALU.subtract
                                                         ).then_inc(lo_done, 1)
                                continue
                            g, which = j // 2, "qk"[j % 2]
                            dve.wait_ge(proj, n + 1)
                            wait(dve, summed, n - 1)
                            dve.scalar_tensor_tensor(roped[:, j % 2, 0, :], ps_j[j % 2][0][:, :],
                                                     w["ba" + which][:, g:g + 1], w["cos"][:, :],
                                                     ALU.add, ALU.mult).then_inc(mixed, 1)
                            dve.scalar_tensor_tensor(roped[:, j % 2, 1, :], ps_j[j % 2][1][:, :],
                                                     w["bb" + which][:, g:g + 1], w["sin"][:, :],
                                                     ALU.add, ALU.mult).then_inc(mixed, 1)
                            if j % 2 == 1:
                                dve.wait_ge(hi_done, n)
                                dve.scalar_tensor_tensor(parts[:, 0, 1, :], ps_q[:, :], bias_of(j),
                                                         parts[:, 0, 0, :], ALU.add, ALU.subtract
                                                         ).then_inc(lo_done, 1)

                loop(dve, BATCH // 2, body)

            @block.gpsimd
            def _(pool):
                if l == 0:
                    return

                def body(b):
                    for j in range(jobs):
                        n = jobs * b + j
                        pool.wait_ge(mixed, 2 * n + 2)
                        if j % 2 == 0:
                            wait(pool, q_mm, (jobs // 2) * b + j // 2)
                        else:
                            wait(pool, lo_pool, (jobs // 2) * b + j // 2)
                        pool.tensor_tensor(roped[:, j % 2, 2, :], roped[:, j % 2, 0, :],
                                           roped[:, j % 2, 1, :], ALU.add).then_inc(summed, 1)
                        if j % 2 == 1:
                            pool.wait_ge(hi_done, n + 1)
                            pool.wait_ge(summed, n + 1)
                            pool.tensor_tensor(parts[:, 1, 1, :], roped[:, 1, 2, :], parts[:, 1, 0, :],
                                               ALU.subtract).then_inc(lo_pool, 1)

                loop(pool, BATCH, body)

            @block.scalar
            def _(act):
                def sqrt(b, s):
                    act.wait_ge(var_done, TPB * (b + 1))
                    act.activation(sd[:, s, :], mean_var[:, s, :, 1], ACT.Sqrt, bias=w["eps"][:, 0:1]
                                   ).then_inc(sd_done, 1)

                def body(bb):
                    for s in range(2):
                        b = 2 * bb + s
                        if isinstance(bb, int) and bb == 0 and s == 0:
                            sqrt(0, 0)
                        act.wait_ge(turned, b + 1)
                        wait(act, proj, jobs * (b - 1))
                        act.activation(xT[:, s, :], ps_x[:, :], ACT.Copy).then_inc(xT_done, 1)
                        if not (isinstance(bb, int) and b == BATCH - 1):
                            sqrt(b + 1, 1 - s)
                        act.wait_ge(v_mm, b + 1)
                        act.wait_ge(v_ones, 1)
                        wait(act, v_out[s], 16 * bb)
                        act.activation(v[:, s, :, :, 0:HD],
                                       ps_v[:, :, :].rearrange("p t (h c) -> p t h c", h=HEADS),
                                       ACT.Copy).then_inc(v_done, 1)
                        for j in range(jobs):
                            n = jobs * b + j
                            half = (jobs // 2) * b + j // 2
                            wait(act, parts_out[j % 2], 16 * half)
                            if l == 0:
                                act.wait_ge(proj, n + 1)
                                src = ps_j[j][0]
                            elif j % 2 == 0:
                                act.wait_ge(q_mm, half + 1)
                                src = ps_q
                            else:
                                act.wait_ge(summed, n + 1)
                            if l == 1 and j % 2 == 1:
                                act.activation(parts[:, 1, 0, :], roped[:, 1, 2, :], ACT.Copy
                                               ).then_inc(hi_done, 1)
                            else:
                                act.activation(parts[:, j % 2, 0, :], src[:, :], ACT.Identity,
                                               bias=bias_of(j)).then_inc(hi_done, 1)

                loop(act, BATCH // 2, body)

            @block.tensor
            def _(pe):
                def turn(b, s):
                    pe.wait_ge(normed, TPB * (b + 1))
                    wait(pe, xT_done, b)
                    for t in range(TPB):
                        mm = pe.transpose(ps_x[:, t * P:(t + 1) * P], xn[:, s, t, :], w["ident"][:, :])
                    mm.then_inc(turned, 1)

                def body(bb):
                    for s in range(2):
                        b = 2 * bb + s
                        if isinstance(bb, int) and bb == 0 and s == 0:
                            turn(0, 0)
                        pe.wait_ge(xT_done, b + 1)
                        wait(pe, logits_done, b)
                        for t in range(TPB):
                            mm = pe.matmul(ps_r[:, t, :], xT[:, s, t * P:(t + 1) * P], L.wr[:, :],
                                           start=True, stop=True)
                        mm.then_inc(routed, 1)
                        wait(pe, v_done, b)
                        for t in range(TPB):
                            pe.matmul(ps_v[:, t, :], xT[:, s, t * P:(t + 1) * P], L.wv[:, :],
                                      start=True, stop=False)
                            mm = pe.matmul(ps_v[:, t, :], w["ones"][0:1, :], L.bv[:, :],
                                           start=False, stop=True)
                        mm.then_inc(v_mm, 1)

                        def to_latent_q(j):
                            k = (jobs // 2) * b + j // 2
                            pe.wait_ge(summed, jobs * b + j + 1)
                            wait(pe, lo_done, k)
                            pe.matmul(ps_q[:, :], w["wqk"][:, :], roped[:, 0, 2, :],
                                      start=True, stop=True).then_inc(q_mm, 1)

                        for j in range(jobs):
                            n = jobs * b + j
                            if l == 0:
                                wait(pe, lo_done, n - 1)
                                pe.matmul(ps_j[j][0][:, :], (w["wq0"], w["wk0"])[j][:, :], xT[:, s, :],
                                          start=True, stop=True).then_inc(proj, 1)
                                continue
                            which, g = "qk"[j % 2], j // 2
                            wait(pe, mixed, 2 * (n - 1))
                            for k, form in enumerate("ab"):
                                mm = pe.matmul(ps_j[j % 2][k][:, :],
                                               w["w" + form + which][:, g * P:(g + 1) * P], xT[:, s, :],
                                               start=True, stop=True)
                            mm.then_inc(proj, 1)
                            if j % 2 == 1:
                                to_latent_q(j - 1)
                        if not (isinstance(bb, int) and b == BATCH - 1):
                            turn(b + 1, 1 - s)

                loop(pe, BATCH // 2, body)


def dispatch(nc, L, w):
    l = L.index
    TE = [P, TILES, E]
    with ExitStack() as ctx:
        sb, psum, sem = alloc(nc, ctx)
        S = lambda name: L.semaphore(f"b_{name}")
        big = {n: sb(f"b{l}_{n}", TE) for n in ("ex", "pick", "oh1", "oh2", "oh", "total", "sum0", "sum1", "pos")}
        small = {n: sb(f"b{l}_{n}", [P, TILES]) for n in ("top", "all", "first", "p1", "p2")}
        iota_e = sb(f"b{l}_iota_e", [P, E])
        iota_c = sb(f"b{l}_iota_c", [P, E, TOKENS // SLOTS])
        iota_t = sb(f"b{l}_iota_t", [P, ETILES, E])
        over = sb(f"b{l}_over", [P, E, TOKENS // SLOTS])
        before = sb(f"b{l}_before", [P, ETILES, E])
        tiles = sb(f"b{l}_tiles", [P, 4, E])
        ps_in, ps_all = psum(f"b{l}_ps_in"), psum(f"b{l}_ps_all")
        chain, iotas, shifted, exps = S("chain"), S("iotas"), S("shifted"), S("exps")
        onehot, counted = S("onehot"), S("counted")

        def over_e(x):
            return x[:, :].unsqueeze(2).to_broadcast(TE)

        def over_t(x):
            return x.unsqueeze(1).to_broadcast(TE)

        with nc.Block() as block:
            @block.gpsimd
            def _(pool):
                pool.iota(iota_e[:, :], pattern=[[1, E]], base=-E, channel_multiplier=0,
                          allow_small_or_imprecise_dtypes=True).then_inc(iotas, 1)
                pool.iota(iota_c[:, :, :], pattern=[[0, E], [SLOTS, TOKENS // SLOTS]], base=0,
                          channel_multiplier=0, allow_small_or_imprecise_dtypes=True).then_inc(iotas, 1)
                pool.iota(iota_t[:, :, :], pattern=[[1, ETILES], [0, E]], base=0,
                          channel_multiplier=0, allow_small_or_imprecise_dtypes=True).then_inc(iotas, 1)

            @block.scalar
            def _(act):
                act.wait_ge(shifted, 1)
                act.activation(big["ex"][:, :, :], big["ex"][:, :, :], ACT.Exp).then_inc(exps, 1)

            @block.tensor
            def _(pe):
                pe.wait_ge(onehot, 1)
                flat = big["oh"][:, :, :].rearrange("p t e -> p (t e)")
                pe.matmul(ps_in[:, :], w["tri"][:, :], flat, start=True, stop=True)
                pe.matmul(ps_all[:, :], w["ones"][:, :], flat, start=True, stop=True).then_inc(counted, 1)

            @block.vector
            def _(dve):
                done = [0]

                def step(ins):
                    done[0] += 1
                    ins.then_inc(chain, 1)
                    dve.wait_ge(chain, done[0])

                ex, pick, pos = big["ex"], big["pick"], big["pos"]
                step(dve.tensor_reduce(small["top"][:, :], w["logits"][:, :, :], AX.X, ALU.max))
                dve.tensor_tensor(ex[:, :, :], w["logits"][:, :, :], over_e(small["top"]), ALU.subtract
                                  ).then_inc(shifted, 1)
                dve.wait_ge(exps, 1)
                dve.wait_ge(iotas, 3)
                step(dve.tensor_reduce(small["all"][:, :], ex[:, :, :], AX.X, ALU.add))
                step(dve.reciprocal(small["all"][:, :], small["all"][:, :]))
                for k, (oh, p) in enumerate(((big["oh1"], small["p1"]), (big["oh2"], small["p2"]))):
                    step(dve.tensor_reduce(small["top"][:, :], ex[:, :, :], AX.X, ALU.max))
                    step(dve.tensor_tensor(pick[:, :, :], ex[:, :, :], over_e(small["top"]), ALU.is_equal))
                    step(dve.tensor_tensor(pick[:, :, :], pick[:, :, :], over_t(iota_e[:, :]), ALU.mult))
                    step(dve.tensor_reduce(small["first"][:, :], pick[:, :, :], AX.X, ALU.min))
                    step(dve.tensor_tensor(oh[:, :, :], over_t(iota_e[:, :]), over_e(small["first"]), ALU.is_equal))
                    step(dve.tensor_tensor(p[:, :], small["top"][:, :], small["all"][:, :], ALU.mult))
                    if k == 0:
                        step(dve.scalar_tensor_tensor(ex[:, :, :], oh[:, :, :], -2.0, ex[:, :, :],
                                                      ALU.mult, ALU.add))
                dve.tensor_tensor(big["oh"][:, :, :], big["oh1"][:, :, :], big["oh2"][:, :, :], ALU.add
                                  ).then_inc(onehot, 1)
                if l == 0:
                    step(dve.tensor_copy(w["gate"][:, 0, :], small["p1"][:, :]))
                    step(dve.tensor_copy(w["gate"][:, 1, :], small["p2"][:, :]))
                else:
                    step(dve.tensor_tensor(small["first"][:, :], small["p1"][:, :], small["p2"][:, :], ALU.add))
                    step(dve.tensor_scalar(small["first"][:, :], small["first"][:, :], 1e-9, None, ALU.add))
                    step(dve.reciprocal(small["first"][:, :], small["first"][:, :]))
                    step(dve.tensor_tensor(w["gate"][:, 0, :], small["p1"][:, :], small["first"][:, :], ALU.mult))
                    step(dve.tensor_tensor(w["gate"][:, 1, :], small["p2"][:, :], small["first"][:, :], ALU.mult))
                dve.wait_ge(counted, 1)
                flat = lambda x: x[:, :, :].rearrange("p t e -> p (t e)")
                dve.tensor_copy(flat(big["total"]), ps_all[:, :])
                step(dve.tensor_copy(flat(big["sum0"]), ps_all[:, :]))
                a, b = big["sum0"], big["sum1"]
                reach = 1
                while reach < TILES:
                    dve.tensor_copy(b[:, 0:reach, :], a[:, 0:reach, :])
                    step(dve.tensor_tensor(b[:, reach:TILES, :], a[:, reach:TILES, :],
                                           a[:, 0:TILES - reach, :], ALU.add))
                    a, b = b, a
                    reach *= 2
                counts = a[:, TILES - 1, :]
                step(dve.tensor_tensor(over[:, :, :], counts.unsqueeze(2).to_broadcast([P, E, TOKENS // SLOTS]),
                                       iota_c[:, :, :], ALU.is_gt))
                step(dve.tensor_reduce(tiles[:, 0, :], over[:, :, :], AX.X, ALU.add))
                step(dve.tensor_copy(tiles[:, 1, :], tiles[:, 0, :]))
                e, f, reach = 1, 2, 1
                while reach < E:
                    dve.tensor_copy(tiles[:, f, 0:reach], tiles[:, e, 0:reach])
                    step(dve.tensor_tensor(tiles[:, f, reach:E], tiles[:, e, reach:E],
                                           tiles[:, e, 0:E - reach], ALU.add))
                    e, f, reach = f, e, 2 * reach
                step(dve.tensor_tensor(before[:, :, :], tiles[:, e, :].unsqueeze(1).to_broadcast([P, ETILES, E]),
                                       iota_t[:, :, :], ALU.is_le))
                step(dve.tensor_reduce(w["tile_f"][:, :], before[:, :, :], AX.X, ALU.add))
                step(dve.tensor_copy(w["tile_expert"][:, :], w["tile_f"][:, :]))
                step(dve.tensor_tensor(tiles[:, 3, :], tiles[:, e, :], tiles[:, 0, :], ALU.subtract))
                step(dve.tensor_scalar(tiles[:, 3, :], tiles[:, 3, :], float(SLOTS), None, ALU.mult))
                step(dve.tensor_tensor(pos[:, :, :], a[:, :, :], big["total"][:, :, :], ALU.subtract))
                step(dve.tensor_tensor(pos[:, :, :], pos[:, :, :], over_t(tiles[:, 3, :]), ALU.add))
                step(dve.tensor_tensor(flat(pos), flat(pos), ps_in[:, :], ALU.add))
                for k, oh in enumerate((big["oh1"], big["oh2"])):
                    step(dve.tensor_tensor(pick[:, :, :], oh[:, :, :], pos[:, :, :], ALU.mult))
                    step(dve.tensor_reduce(small["first"][:, :], pick[:, :, :], AX.X, ALU.add))
                    step(dve.tensor_copy(w["slot"][:, k, :], small["first"][:, :]))


def experts(nc, L, w):
    l = L.index
    N = 4
    with ExitStack() as ctx:
        sb, psum, sem = alloc(nc, ctx)
        S = lambda name: L.semaphore(f"c_{name}")
        up = sb(f"c{l}_up", [P, N, F + FB])
        down = sb(f"c{l}_down", [P, N, FB, P])
        b2 = sb(f"c{l}_b2", [1, N, P])
        rows = sb(f"c{l}_rows", [P, N, HALVES, P])
        xT = sb(f"c{l}_xT", [P, 2, SLOTS])
        hT = sb(f"c{l}_hT", [P, 2, FB, SLOTS])
        y = sb(f"c{l}_y", [P, 2, HALVES, P])
        ps_x = psum(f"c{l}_ps_x")
        ps_h = [psum(f"c{l}_ps_h{s}", 2) for s in range(2)]
        ps_y = [psum(f"c{l}_ps_y{s}") for s in range(2)]
        rows_in = [S(f"rows_in{i}") for i in range(N)]
        weights_in = [S(f"weights_in{i}") for i in range(N)]
        y_out = [S(f"y_out{s}") for s in range(2)]
        turned, xT_done, h_mm, h_done, y_mm, y_done = (
            S("turned"), S("xT"), S("h_mm"), S("h"), S("y_mm"), S("y"))
        WEIGHT_DMAS = 2 if l == 0 else 3
        H_STEPS = 1 if l == 0 else FB

        in_view = L.slots_in.rearrange("(t a p) n -> t p a n", a=HALVES, p=P)
        out_view = L.slots_out.rearrange("(t a p) n -> t p a n", a=HALVES, p=P)

        TURNS = ETILES // N

        def follow(tt, i, by):
            return tt + (i + by) // N, (i + by) % N

        def each_tile(eng, step):
            def body(tt):
                for i in range(N):
                    step(tt, i)
            loop(eng, TURNS, body)

        with nc.Block() as block:
            @block.sync
            def _(sp):
                def step(tt, i):
                    t = N * tt + i
                    expert = sp.value_load(w["tile_expert"][0:1, bass.ds(t, 1)], min_val=0, max_val=E)
                    wait(sp, turned, t - N + 1)
                    sp.dma_start(rows[:, i], in_view[bass.ds(t, 1)].rearrange("o p a n -> (o p) a n")
                                 ).then_inc(rows_in[i], 16)
                    wait(sp, y_mm, t - N + 1)
                    sp.dma_start(up[:, i, 0:L.up_width], L.w1[bass.ds(expert, 1)].rearrange("o p n -> (o p) n")
                                 ).then_inc(weights_in[i], 16)
                    sp.dma_start(down[:, i], L.w2[bass.ds(expert, 1)].rearrange(
                        "o (p j) n -> (o p) j n", j=FB)).then_inc(weights_in[i], 16)
                    if l == 1:
                        sp.dma_start(b2[:, i, :], L.b2[bass.ds(expert, 1), :]).then_inc(weights_in[i], 16)

                each_tile(sp, step)

            @block.tensor
            def _(pe):
                def turn(tt, i):
                    t = N * tt + i
                    pe.wait_ge(rows_in[i], 16 * (tt + 1))
                    wait(pe, xT_done, t)
                    for a in range(HALVES):
                        mm = pe.transpose(ps_x[:, a * P:(a + 1) * P], rows[:, i, a, :], w["ident"][:, :])
                    mm.then_inc(turned, 1)

                def go_up(tt, i):
                    t, s = N * tt + i, i % 2
                    pe.wait_ge(xT_done, t + 1)
                    pe.wait_ge(weights_in[i], 16 * WEIGHT_DMAS * (tt + 1))
                    wait(pe, h_done, H_STEPS * (t - 1))
                    for j in range(FB):
                        mm = pe.matmul(ps_h[s][:, j * SLOTS:(j + 1) * SLOTS], up[:, i, j:F:FB], xT[:, s, :],
                                       start=True, stop=True)
                    mm.then_inc(h_mm, 1)

                def go_down(tt, i):
                    t, s = N * tt + i, i % 2
                    pe.wait_ge(h_done, H_STEPS * (t + 1))
                    wait(pe, y_done, t - 1)
                    for a in range(HALVES):
                        out = ps_y[s][:, a * P:(a + 1) * P]
                        for j in range(FB):
                            mm = pe.matmul(out, hT[:, s, j, a * P:(a + 1) * P], down[:, i, j, :],
                                           start=(j == 0), stop=(l == 0 and j == FB - 1))
                        if l == 1:
                            mm = pe.matmul(out, w["ones"][0:1, :], b2[:, i, :], start=False, stop=True)
                    mm.then_inc(y_mm, 1)

                def step(tt, i):
                    nt, ni = follow(tt, i, 1)
                    if inside(N * nt + ni, ETILES):
                        turn(nt, ni)
                    go_up(tt, i)
                    before = follow(tt, i, -1)
                    if inside(N * before[0] + before[1], ETILES):
                        go_down(*before)

                turn(0, 0)
                each_tile(pe, step)
                go_down(TURNS - 1, N - 1)

            @block.scalar
            def _(act):
                def store(tt, i):
                    act.wait_ge(y_done, N * tt + i + 1)
                    act.dma_start(out_view[bass.ds(N * tt + i, 1)].rearrange("o p a n -> (o p) a n"),
                                  y[:, i % 2]).then_inc(y_out[i % 2], 16)

                def step(tt, i):
                    t, s = N * tt + i, i % 2
                    act.wait_ge(h_mm, t + 1)
                    wait(act, y_mm, t - 1)
                    if l == 0:
                        act.activation(hT[:, s].rearrange("p j n -> p (j n)"), ps_h[s][:, :], ACT.Gelu
                                       ).then_inc(h_done, 1)
                    else:
                        act.wait_ge(weights_in[i], 16 * WEIGHT_DMAS * (tt + 1))
                        for j in range(FB):
                            act.activation(hT[:, s, j, :], ps_h[s][:, j * SLOTS:(j + 1) * SLOTS], ACT.Silu,
                                           bias=up[:, i, F + j:F + j + 1]).then_inc(h_done, 1)
                    before = follow(tt, i, -1)
                    if inside(N * before[0] + before[1], ETILES):
                        store(*before)

                each_tile(act, step)
                store(TURNS - 1, N - 1)
                for s in range(2):
                    act.wait_ge(y_out[s], 16 * (ETILES // 2))

            @block.vector
            def _(dve):
                def turn(tt, i):
                    t = N * tt + i
                    dve.wait_ge(turned, t + 1)
                    wait(dve, h_mm, t - 1)
                    dve.tensor_copy(xT[:, i % 2, :], ps_x[:, 0:SLOTS]).then_inc(xT_done, 1)

                def leave(tt, i):
                    t, s = N * tt + i, i % 2
                    dve.wait_ge(y_mm, t + 1)
                    wait(dve, y_out[s], 16 * ((N // 2) * tt + i // 2))
                    dve.tensor_copy(y[:, s].rearrange("p a n -> p (a n)"), ps_y[s][:, 0:SLOTS]
                                    ).then_inc(y_done, 1)

                def step(tt, i):
                    nt, ni = follow(tt, i, 1)
                    if inside(N * nt + ni, ETILES):
                        turn(nt, ni)
                    before = follow(tt, i, -1)
                    if inside(N * before[0] + before[1], ETILES):
                        leave(*before)

                turn(0, 0)
                each_tile(dve, step)
                leave(TURNS - 1, N - 1)


def combine(nc, L, w):
    l = L.index
    with ExitStack() as ctx:
        sb, psum, sem = alloc(nc, ctx)
        S = lambda name: L.semaphore(f"e_{name}")
        N = 4
        x, xn, s_in, shared = (sb(f"e{l}_{n}", [P, N, P]) for n in ("x", "xn", "s", "shared"))
        picked = sb(f"e{l}_picked", [P, N, 2, P])
        ffn, silu, out = (sb(f"e{l}_{n}", [P, 2, P]) for n in ("ffn", "silu", "out"))
        sT = sb(f"e{l}_sT", [P, 2, P])
        index = sb(f"e{l}_index", [P, N, 2], I32)
        ps_t = [psum(f"e{l}_ps_t{i}") for i in range(2)]
        ps_s = [psum(f"e{l}_ps_s{i}") for i in range(2)]
        tile_in = [S(f"tile_in{i}") for i in range(N)]
        picked_in = [L.queue_semaphore(f"picked_in{i}") for i in range(N)]
        out_out = [S(f"out_out{i}") for i in range(2)]
        index_done, summed, gated, stored = S("index"), S("summed"), S("gated"), S("stored")
        partial, product = S("partial"), S("product")
        turned, sT_done, s_mm = S("turned"), S("sT"), S("s_mm")
        LOADS = 4 if l == 0 else 3
        view = lambda a: a.rearrange("(t p) n -> t p n", p=P)
        x_v, s_v, o_v = view(L.x_in), view(L.s), view(L.x_out)
        xn_v = view(L.slots_in[SHARED_ROW:ROWS, :])
        sh_v = view(L.slots_out[SHARED_ROW:ROWS, :])

        with nc.Block() as block:
            @block.sync
            def _(sp):
                def body(tt):
                    for i in range(N):
                        t = N * tt + i
                        wait(sp, stored, t - N + 1)
                        if l == 1:
                            wait(sp, turned, t - N + 1)
                        one = lambda v: v[bass.ds(t, 1)].rearrange("o p n -> (o p) n")
                        sp.dma_start(x[:, i], one(x_v)).then_inc(tile_in[i], 16)
                        sp.dma_start(s_in[:, i], one(s_v)).then_inc(tile_in[i], 16)
                        sp.dma_start(shared[:, i], one(sh_v)).then_inc(tile_in[i], 16)
                        if l == 0:
                            sp.dma_start(xn[:, i], one(xn_v)).then_inc(tile_in[i], 16)

                loop(sp, TILES // N, body)

            @block.gpsimd
            def _(pool):
                def body(tt):
                    for i in range(N):
                        t = N * tt + i
                        wait(pool, stored, t - N + 1)
                        for k in range(2):
                            pool.tensor_copy(index[:, i, k:k + 1], w["slot"][:, k, bass.ds(t, 1)]
                                             ).then_inc(index_done, 1)
                        carried(pool, (index_done, 2), (index_done, 2 * t + 2))
                        for k in range(2):
                            pool.indirect_dma_start(
                                picked[:, i, k, :], None, L.slots_out,
                                bass.IndirectOffsetOnAxis(ap=index[:, i, k:k + 1], axis=0)
                                ).then_inc(picked_in[i], 16)

                loop(pool, TILES // N, body)

            @block.scalar
            def _(act):
                def body(tt):
                    for i in range(N):
                        t = N * tt + i
                        act.wait_ge(summed, t + 1)
                        act.activation(silu[:, i % 2], ffn[:, i % 2], ACT.Silu).then_inc(gated, 1)
                        act.wait_ge(stored, t + 1)
                        act.dma_start(o_v[bass.ds(t, 1)].rearrange("o p n -> (o p) n"), out[:, i % 2]
                                      ).then_inc(out_out[i % 2], 16)

                loop(act, TILES // N, body)
                for i in range(2):
                    act.wait_ge(out_out[i], 16 * TILES // 2)

            @block.tensor
            def _(pe):
                if l == 0:
                    return

                def body(tt):
                    for i in range(N):
                        t = N * tt + i
                        pe.wait_ge(tile_in[i], 16 * LOADS * (tt + 1))
                        wait(pe, sT_done, t - 1)
                        pe.transpose(ps_t[i % 2][:, 0:P], s_in[:, i], w["ident"][:, :]).then_inc(turned, 1)
                        pe.wait_ge(sT_done, t + 1)
                        wait(pe, stored, t - 1)
                        pe.matmul(ps_s[i % 2][:, 0:P], sT[:, i % 2], w["cprojT"][:, :], start=True, stop=False)
                        pe.matmul(ps_s[i % 2][:, 0:P], w["ones"][0:1, :], w["bs1"][:, :],
                                  start=False, stop=True).then_inc(s_mm, 1)

                loop(pe, TILES // N, body)

            @block.vector
            def _(dve):
                def add_up(tt, i):
                    t = N * tt + i
                    dve.wait_ge(tile_in[i], 16 * LOADS * (tt + 1))
                    dve.wait_ge(picked_in[i], 32 * (tt + 1))
                    gate = [w["gate"][:, k, bass.ds(t, 1)] for k in range(2)]
                    acc = ffn[:, i % 2]
                    wait(dve, gated, t - 1)
                    if l == 0:
                        dve.tensor_tensor(acc, shared[:, i], xn[:, i], ALU.add).then_inc(partial, 1)
                    else:
                        dve.tensor_scalar(acc, shared[:, i], 0.1, None, ALU.mult).then_inc(partial, 1)
                    dve.wait_ge(partial, 2 * t + 1)
                    dve.scalar_tensor_tensor(acc, picked[:, i, 0], gate[0], acc, ALU.mult, ALU.add
                                             ).then_inc(partial, 1)
                    dve.wait_ge(partial, 2 * t + 2)
                    dve.scalar_tensor_tensor(acc, picked[:, i, 1], gate[1], acc, ALU.mult, ALU.add
                                             ).then_inc(summed, 1)
                    if l == 1:
                        dve.wait_ge(turned, t + 1)
                        wait(dve, s_mm, t - 1)
                        dve.tensor_copy(sT[:, i % 2], ps_t[i % 2][:, 0:P]).then_inc(sT_done, 1)

                def finish(tt, i):
                    t = N * tt + i
                    dve.wait_ge(gated, t + 1)
                    wait(dve, out_out[i % 2], 16 * ((N // 2) * tt + i // 2))
                    s = s_in[:, i]
                    if l == 1:
                        dve.wait_ge(s_mm, t + 1)
                        s = ps_s[i % 2][:, 0:P]
                    dve.tensor_tensor(out[:, i % 2], s, silu[:, i % 2], ALU.mult).then_inc(product, 1)
                    dve.wait_ge(product, t + 1)
                    dve.tensor_tensor(out[:, i % 2], out[:, i % 2], x[:, i], ALU.add).then_inc(stored, 1)

                def body(tt):
                    for i in range(N):
                        if isinstance(tt, int) and tt == 0 and i == 0:
                            add_up(0, 0)
                        if not (isinstance(tt, int) and tt == TILES // N - 1 and i == N - 1):
                            add_up(tt + (i + 1) // N, (i + 1) % N)
                        finish(tt, i)

                loop(dve, TILES // N, body)


def attend(nc, L, w):
    l = L.index
    LEAD = 7
    UNITS = BATCH * GROUPS
    STEPS = UNITS * TPB
    PER_BATCH = GROUPS * TPB
    PARTS = L.products
    ROW = L.head_rows
    causal = l == 1
    with ExitStack() as ctx:
        sb, psum, sem = alloc(nc, ctx)
        S = lambda name: L.semaphore(f"d_{name}")
        q = [sb(f"d{l}_q{g}", [P, GH, SEQ], F32R) for g in range(GROUPS)]
        k = [sb(f"d{l}_k{g}", [P, GH, SEQ], F32R) for g in range(GROUPS)]
        v = sb(f"d{l}_v", [P, GROUPS, TPB, GH, VC])
        probs = sb(f"d{l}_probs", [P, 2, GH, SEQ])
        maxima = sb(f"d{l}_maxima", [P, GH, TPB])
        m_parts = sb(f"d{l}_m_parts", [P, 2, GH, TPB])
        mT = sb(f"d{l}_mT", [2 * GH * TPB, 2, P])
        o = sb(f"d{l}_o", [P, SEQ])
        inv = sb(f"d{l}_inv", [P, TPB, GH])
        out = sb(f"d{l}_out", [P, TPB, P])
        ps_s = [psum(f"d{l}_ps_s{i}", 2) for i in range(2)]
        ps_m = [psum(f"d{l}_ps_m{i}") for i in range(2)]
        ps_o = psum(f"d{l}_ps_o")
        ps_t = psum(f"d{l}_ps_t")

        qk_in = [S(f"qk_in{g}") for g in range(GROUPS)]
        m_in = [S(f"m_in{g}") for g in range(GROUPS)]
        out_out = S("out_out")
        cleared, m_mm, m_read, m_max, m_hi, m_split = (
            S("cleared"), S("m_mm"), S("m_read"), S("m_max"), S("m_hi"), S("m_split"))
        m_turned, mT_done = S("m_turned"), S("mT")
        s_mm, exps, pv, o_copied, o_turned, o_inv, o_done = (
            S("s_mm"), S("exps"), S("pv"), S("o_copied"), S("o_turned"), S("o_inv"), S("o_done"))
        minus_one, o_zero = S("minus_one"), S("o_zero")
        tile_rows = sb(f"d{l}_rows", [P, 2, P])
        index = sb(f"d{l}_index", [P, 2, 2], I32)
        row_in = [S(f"row_in{i}") for i in range(2)]
        row_out = [L.queue_semaphore(f"row_out{i}") for i in range(2)]
        index_done = S("index")
        xn_view = L.slots_in[SHARED_ROW:ROWS, :].rearrange("(t p) n -> t p n", p=P)
        LOADS = 2 * len(PARTS) + 1

        out_view = L.s.rearrange("(b t p) n -> b p t n", t=TPB, p=P)
        v_view = L.v.rearrange("(b p) (t h c) -> b p t h c", p=P, t=TPB, h=HEADS)

        def at(b, offset):
            turns, rest = divmod(offset, PER_BATCH)
            b = b + turns
            return b, rest // TPB, rest % TPB, PER_BATCH * b + rest, GROUPS * b + rest // TPB

        def all_steps(eng, step):
            for n in range(-LEAD, 0):
                step(0, n)
            def body(b):
                for n in range(PER_BATCH):
                    step(b, n)
            loop(eng, BATCH, body)
            for n in range(TPB):
                step(BATCH, n)

        def width(qb):
            return (qb + 1) * P if causal else SEQ

        def first(kb):
            return kb * P if causal else 0

        with nc.Block() as block:
            @block.sync
            def _(sp):
                def load(b, g):
                    u = GROUPS * b + g
                    wait(sp, pv, TPB * (u - GROUPS + 1))
                    tokens = bass.ds(b * SEQ, SEQ)
                    for i, pair in enumerate(PARTS):
                        for dst, src, part in ((q, L.q, pair[0]), (k, L.k, pair[1])):
                            rows = src[part, g * GH * ROW:(g + 1) * GH * ROW, tokens]
                            sp.dma_start(dst[g][i * ROW:(i + 1) * ROW, :, :].bitcast(F32),
                                         rows.rearrange("(h r) t -> r h t", h=GH)).then_inc(qk_in[g], 16)
                    sp.dma_start(v[:, g], v_view[bass.ds(b, 1), :, :, g * GH:(g + 1) * GH, :].rearrange(
                        "o p t h c -> (o p) t (h c)")).then_inc(qk_in[g], 16)

                def step(b, offset):
                    _, g, kb, _, u = at(b, offset)
                    if kb == 0 and inside(u, UNITS):
                        half = (GROUPS // 2) * at(b, offset)[0] + g // 2
                        wait(sp, row_out[g % 2], 32 * half)
                        sp.dma_start(tile_rows[:, g % 2], xn_view[bass.ds(u, 1)].rearrange("o p n -> (o p) n")
                                     ).then_inc(row_in[g % 2], 16)
                    if kb == 1 and inside(at(b, offset + 3 * TPB)[4], UNITS) and not (
                            isinstance(u, int) and u < 0):
                        load(*at(b, offset + 3 * TPB)[0:2])
                    if kb == 2 and inside(u + 1, UNITS):
                        nb, ng, _, _, nu = at(b, offset + TPB)
                        sp.wait_ge(mT_done, nu + 1)
                        for part in range(2):
                            rows = mT[part * GH * TPB:(part + 1) * GH * TPB, ng % 2, :]
                            dst = q[ng][M_ROW + part:M_ROW + part + 1, :, :].bitcast(F32)
                            sp.dma_start(dst.rearrange("o h (t n) -> o (h t) n", n=P), rows
                                           ).then_inc(m_in[ng], 16)
                    if kb == TPB - 1:
                        ob, og, _, _, ou = at(b, offset - TPB)
                        if og == GROUPS - 1 and inside(ou, UNITS):
                            sp.wait_ge(o_done, ou + 1)
                            sp.dma_start(out_view[bass.ds(ob, 1)].rearrange("o p t n -> (o p) t n"),
                                           out[:, :, :]).then_inc(out_out, 16)

                sp.wait_ge(cleared, 2 * GROUPS)
                for g in range(3):
                    load(0, g)
                all_steps(sp, step)
                sp.wait_ge(out_out, 16 * BATCH)

            @block.gpsimd
            def _(pool):
                for g in range(GROUPS):
                    pool.memset(q[g][:, :, :].bitcast(F32), 0.0).then_inc(cleared, 1)
                    pool.memset(k[g][:, :, :].bitcast(F32), 0.0).then_inc(cleared, 1)
                pool.wait_ge(cleared, 2 * GROUPS)
                for g in range(GROUPS):
                    pool.memset(k[g][M_ROW:M_ROW + 2, :, :].bitcast(F32), -1.0).then_inc(minus_one, 1)
                pool.wait_ge(minus_one, GROUPS)

                def body(bb):
                    for i in range(2):
                        t = 2 * bb + i
                        wait(pool, row_out[i], 32 * bb)
                        for c in range(2):
                            pool.tensor_copy(index[:, i, c:c + 1], w["slot"][:, c, bass.ds(t, 1)]
                                             ).then_inc(index_done, 1)
                        carried(pool, (index_done, 2), (index_done, 2 * t + 2), (row_in[i], 16 * (bb + 1)))
                        for c in range(2):
                            pool.indirect_dma_start(
                                L.slots_in, bass.IndirectOffsetOnAxis(ap=index[:, i, c:c + 1], axis=0),
                                tile_rows[:, i, :], None).then_inc(row_out[i], 16)

                loop(pool, TILES // 2, body)
                for i in range(2):
                    pool.wait_ge(row_out[i], 16 * TILES)

            @block.scalar
            def _(act):
                def step(b, offset):
                    _, _, kb, n, u = at(b, offset)
                    for pair in range(2):
                        if inside(n, STEPS):
                            act.wait_ge(s_mm, 2 * n + pair + 1)
                            wait(act, pv, n - 1)
                            wide = SEQ - first(kb)
                            act.activation(
                                probs[:, offset % 2, 2 * pair:2 * pair + 2, 0:wide],
                                ps_s[pair][:, :].rearrange("p (h n) -> p h n", h=2)[:, :, 0:wide],
                                ACT.Exp, scale=L.scale).then_inc(exps, 1)
                        if pair == 0 and kb == 1 and inside(u - 1, UNITS):
                            act.wait_ge(pv, TPB * u)
                            wait(act, o_turned, u - 1)
                            act.activation(o[:, :], ps_o[:, :], ACT.Copy).then_inc(o_copied, 1)

                all_steps(act, step)

            @block.vector
            def _(dve):
                dve.memset(ps_o[:, :], 0.0).then_inc(o_zero, 1)

                def step(b, offset):
                    _, g, kb, n, u = at(b, offset)
                    mb, mg, qb, m, mu = at(b, offset + LEAD)
                    for h in range(GH):
                        if inside(m, STEPS):
                            dve.wait_ge(m_mm, GH * m + h + 1)
                            if qb == 0 and h == 0:
                                wait(dve, m_split, mu)
                            dve.tensor_reduce(maxima[:, h, qb:qb + 1], ps_m[h % 2][:, 0:width(qb)],
                                              AX.X, ALU.max).then_inc(m_read, 1)
                        if h == 1 and kb == 2 and inside(u + 1, UNITS):
                            _, ng, _, _, nu = at(b, offset + TPB)
                            dve.wait_ge(m_turned, nu + 1)
                            before = at(b, offset - TPB)
                            if inside(before[4], UNITS):
                                dve.wait_ge(m_in[before[1]], 32 * (before[0] + 1))
                            dve.tensor_copy(mT[:, ng % 2, :], ps_t[0:2 * GH * TPB, 0:P]).then_inc(mT_done, 1)
                        if h == 1 and kb == 3 and inside(u - 1, UNITS):
                            ob, og, _, _, ou = at(b, offset - TPB)
                            dve.wait_ge(o_turned, ou + 1)
                            if og == 0:
                                wait(dve, out_out, 16 * ob)
                            ov = ps_t[:, :].rearrange("p (t h c) -> p t h c", t=TPB, h=GH)
                            dve.reciprocal(inv[:, :, :], ov[:, :, :, HD]).then_inc(o_inv, 1)
                            dve.wait_ge(o_inv, ou + 1)
                            for t in range(TPB):
                                ins = dve.tensor_tensor(
                                    out[:, t, og * GH * HD:(og + 1) * GH * HD].rearrange("p (h c) -> p h c", h=GH),
                                    ov[:, t, :, 0:HD],
                                    inv[:, t, :].unsqueeze(2).to_broadcast([P, GH, HD]), ALU.mult)
                            ins.then_inc(o_done, 1)
                    if qb == TPB - 1 and inside(m, STEPS):
                        dve.wait_ge(m_read, GH * (m + 1))
                        wait(dve, m_turned, mu)
                        dve.tensor_copy(m_parts[:, 0].bitcast(F32R), maxima[:, :, :]).then_inc(m_hi, 1)
                        dve.wait_ge(m_hi, mu + 1)
                        dve.tensor_tensor(m_parts[:, 1].bitcast(F32R), maxima[:, :, :], m_parts[:, 0],
                                          ALU.subtract).then_inc(m_split, 1)

                all_steps(dve, step)

            @block.tensor
            def _(pe):
                pe.wait_ge(minus_one, GROUPS)
                pe.wait_ge(o_zero, 1)

                def scores(b, offset, pair):
                    nb, g, kb, n, u = at(b, offset)
                    if not inside(n, STEPS):
                        return
                    if kb == 0 and pair == 0:
                        pe.wait_ge(m_in[g], 32 * (nb + 1))
                    wait(pe, exps, 2 * n + pair - 1)
                    for i in range(2):
                        h = 2 * pair + i
                        out_ps = ps_s[pair][:, i * SEQ:(i + 1) * SEQ - first(kb)]
                        mm = pe.matmul(out_ps, k[g][0:M_ROW + 2, h, kb * P:(kb + 1) * P],
                                       q[g][0:M_ROW + 2, h, first(kb):SEQ], start=True, stop=not causal)
                        if causal:
                            mm = pe.matmul(out_ps[:, 0:P], w["ident_bf"][:, :], w["mask_k"][:, :],
                                           start=False, stop=True)
                    mm.then_inc(s_mm, 1)

                def for_maxima(b, offset, h):
                    mb, g, qb, m, mu = at(b, offset)
                    if not inside(m, STEPS):
                        return
                    if qb == 0 and h == 0:
                        pe.wait_ge(qk_in[g], 16 * LOADS * (mb + 1))
                    wait(pe, m_read, GH * m + h - 1)
                    wide = width(qb)
                    mm = pe.matmul(ps_m[h % 2][:, 0:wide], q[g][0:M_ROW, h, qb * P:(qb + 1) * P],
                                   k[g][0:M_ROW, h, 0:wide], start=True, stop=not causal)
                    if causal:
                        mm = pe.matmul(ps_m[h % 2][:, qb * P:wide], w["ident_bf"][:, :], w["mask_q"][:, :],
                                       start=False, stop=True)
                    mm.then_inc(m_mm, 1)

                def with_v(b, offset):
                    _, g, kb, n, u = at(b, offset)
                    if not inside(n, STEPS):
                        return
                    pe.wait_ge(exps, 2 * n + 2)
                    if kb == 0:
                        wait(pe, o_copied, u)
                    for h in range(GH):
                        mm = pe.matmul(ps_o[32 * h:32 * h + VC, first(kb):SEQ], v[:, g, kb, h, :],
                                       probs[:, offset % 2, h, 0:SEQ - first(kb)],
                                       start=(kb == 0), stop=(kb == TPB - 1), tile_position=(0, 32 * h))
                    mm.then_inc(pv, 1)

                def step(b, offset):
                    _, g, kb, n, u = at(b, offset)
                    scores(b, offset, 0)
                    for_maxima(b, offset + LEAD, 0)
                    scores(b, offset, 1)
                    for_maxima(b, offset + LEAD, 1)
                    for_maxima(b, offset + LEAD, 2)
                    with_v(b, offset - 1)
                    for_maxima(b, offset + LEAD, 3)
                    if kb == 1 and inside(u + 1, UNITS):
                        nu = at(b, offset + TPB)[4]
                        pe.wait_ge(m_split, nu + 1)
                        wait(pe, o_done, nu - 2)
                        pe.transpose(ps_t[0:2 * GH * TPB, 0:P], m_parts[:, :, :, :].rearrange("p a h t -> p (a h t)"),
                                     w["ident"][:, :]).then_inc(m_turned, 1)
                    if kb == 2 and inside(u - 1, UNITS):
                        pe.wait_ge(o_copied, u)
                        wait(pe, o_done, u - 1)
                        wait(pe, mT_done, min(u + 2, UNITS) if isinstance(u, int) else u + 2)
                        for t in range(TPB):
                            mm = pe.transpose(ps_t[:, t * P:(t + 1) * P], o[:, t * P:(t + 1) * P], w["ident"][:, :])
                        mm.then_inc(o_turned, 1)

                all_steps(pe, step)


def build(nc, d, out):
    with ExitStack() as ctx:
        sb, _, _ = alloc(nc, ctx)
        w = {n: sb(n, [P, P]) for n in ("ident", "tri", "wq0", "wk0", "wv0", "wv1", "wqk", "cprojT", "ones")}
        for n in ("wr0", "wr1"):
            w[n] = sb(n, [P, E])
        for n in ("bq0", "bk0", "bqk", "eps"):
            w[n] = sb(n, [P, 1])
        for n in ("bv0", "bv1", "bs1"):
            w[n] = sb(n, [1, P])
        for n in ("waq", "wbq", "wak", "wbk", "cos", "sin"):
            w[n] = sb(n, [P, HEADS * LAT])
        for n in ("baq", "bbq", "bak", "bbk"):
            w[n] = sb(n, [P, GROUPS])
        for n in ("ident_bf", "mask_q", "mask_k"):
            w[n] = sb(n, [P, P], BF16)
        w["zeros"] = sb("zeros", [P, 16 * P])
        w["logits"] = sb("logits", [P, TILES, E])
        w["gate"] = sb("gate", [P, 2, TILES])
        w["slot"] = sb("slot", [P, 2, TILES], I32)
        w["tile_f"] = sb("tile_f", [P, ETILES])
        w["tile_expert"] = sb("tile_expert", [P, ETILES], I32)

        def scratch(name, shape):
            return nc.dram_tensor(name, shape, F32, kind="Internal").ap()

        layers, semaphores = [], {}
        for l in range(2):
            L = Layer(nc, semaphores)
            L.index = l
            rows = (HD, LAT)[l]
            L.head_rows = rows
            L.products = [(0, 0), (0, 1), (1, 0)] + [(1, 1)] * (l == 0)
            L.scale = float(rows) ** -0.5
            L.q, L.k = (scratch(f"{n}{l}", [2, HEADS * rows, TOKENS]) for n in "qk")
            L.v = scratch(f"v{l}", [BATCH * P, TPB * HEADS * VC])
            L.slots_in, L.slots_out = scratch(f"slots_in{l}", [ROWS, P]), scratch(f"slots_out{l}", [ROWS, P])
            L.s = scratch(f"s{l}", [TOKENS, P])
            L.x_in = d["x"] if l == 0 else layers[0].x_out
            L.x_out = scratch("x1", [TOKENS, P]) if l == 0 else out
            L.wr, L.wv, L.bv = w[f"wr{l}"], w[f"wv{l}"], w[f"bv{l}"]
            L.w1, L.w2, L.b2, L.up_width = d[f"up{l}"], d[f"down{l}"], d["b2"], (F, F + FB)[l]
            layers.append(L)

        load_constants(nc, d, w)
        for L in layers:
            if L.index > 0:
                clear(nc, semaphores)
            prepare(nc, L, d, w)
            dispatch(nc, L, w)
            attend(nc, L, w)
            experts(nc, L, w)
            combine(nc, L, w)


def layout(i):
    a = {n: np.ascontiguousarray(x) for n, x in i.items()}
    col = lambda x: x.reshape(-1, 1)
    row = lambda x: x.reshape(1, -1)
    d = {"x": a["L0_attn_x"].reshape(TOKENS, P)}
    d["wqT"], d["wkT"], d["wv0"] = a["L0_attn_Wq"].T, a["L0_attn_Wk"].T, a["L0_attn_Wv"]
    d["bq"], d["bk"], d["bv0"] = col(a["L0_attn_bq"]), col(a["L0_attn_bk"]), row(a["L0_attn_bv"])
    d["wpx"] = np.tile(a["L0_attn_Wp"], (HEADS, HEADS))
    d["wr0"], d["wr1"] = a["L0_ffn_router_w"], a["L1_ffn_Wg"]
    d["up0"] = np.concatenate([a["L0_ffn_routed_up"], a["L0_ffn_shared_up"]])
    d["down0"] = np.concatenate([a["L0_ffn_routed_down"], a["L0_ffn_shared_down"]])
    d["cq"], d["ck"], d["cv"] = a["L1_attn_c_attn_w"].reshape(3, P, P)
    d["cqb"], d["ckb"], d["cvb"] = a["L1_attn_c_attn_b"].reshape(3, P, 1)
    d["q2lx"] = np.tile(a["L1_attn_q2l_w"].T, (HEADS, HEADS))
    d["kv2lx"] = np.tile(a["L1_attn_kv2l_w"].T, (HEADS, HEADS))
    d["q2lbx"], d["kv2lbx"] = col(np.tile(a["L1_attn_q2l_b"], GH)), col(np.tile(a["L1_attn_kv2l_b"], GH))
    d["kv2lrep"] = np.tile(a["L1_attn_kv2l_w"], (1, HEADS))
    d["kv2lb"] = col(a["L1_attn_kv2l_b"])
    d["l2orep"] = np.tile(a["L1_attn_l2o_w"].T, (1, HEADS))
    d["l2obx"] = col(np.tile(a["L1_attn_l2o_b"], HEADS))
    d["wqkx"] = np.tile(a["L1_attn_wqk_w"].T, (GH, GH))
    d["bqk"] = col(np.tile(a["L1_attn_wqk_b"], GH))
    d["cprojT"], d["cprojb"] = a["L1_attn_cproj_w"].T, row(a["L1_attn_cproj_b"])
    b1 = np.concatenate([a["L1_ffn_b1"], row(a["L1_ffn_bs1"])]).reshape(E + 1, P, FB)
    d["up1"] = np.concatenate([np.concatenate([a["L1_ffn_W1"], a["L1_ffn_Ws1"][None]]), b1], axis=2)
    d["down1"] = np.concatenate([a["L1_ffn_W2"], a["L1_ffn_Ws2"][None]])
    d["b2"] = np.concatenate([a["L1_ffn_b2"], row(a["L1_ffn_bs2"])])

    n = np.arange(P)
    d["ident"] = np.eye(P)
    d["tri"] = n[:, None] < n[None, :]
    d["mask8"] = n[:, None] // HD == n[None, :] // HD
    d["mask32"] = n[:, None] // HD == np.arange(HEADS * LAT)[None, :] // LAT
    d["mask32x32"] = n[:, None] // LAT == n[None, :] // LAT
    d["rot"] = (n[:, None] == n[None, :] - 1) * (n[None, :] % 2) * 1.0 - (n[:, None] == n[None, :] + 1) * (1 - n[None, :] % 2)
    steps = np.arange(0, LAT, 2, dtype=np.float32) / np.float32(LAT)
    freq = np.float32(1.0) / np.power(np.float32(10000.0), steps)
    angle = np.repeat(np.outer(np.arange(SEQ, dtype=np.float32), freq), 2, axis=1).T
    d["cos"], d["sin"] = np.tile(np.cos(angle), (GH, 1)), np.tile(np.sin(angle), (GH, 1))
    return {name: np.ascontiguousarray(x, dtype=np.float32) for name, x in d.items()}


def kernel(**inputs):
    import concourse.bacc as bacc
    from concourse.bass_utils import run_bass_kernel_spmd

    nc = bacc.Bacc("TRN2", target_bir_lowering=False, num_devices=1)
    arrays = {f"in_{name}": x for name, x in layout(inputs).items()}
    d = {name: nc.dram_tensor(name, x.shape, F32, kind="ExternalInput").ap() for name, x in arrays.items()}
    out = nc.dram_tensor("out", [TOKENS, P], F32, kind="ExternalOutput").ap()
    build(nc, {name.removeprefix("in_"): ap for name, ap in d.items()}, out)
    r = run_bass_kernel_spmd(nc, [arrays], core_ids=[0])
    return r.results[0]["out"].reshape(BATCH, SEQ, P)
```

```python
from contextlib import ExitStack

import numpy as np

import concourse.bass as bass
from concourse import mybir

F32 = mybir.dt.float32
F32R = mybir.dt.float32r
I32 = mybir.dt.int32
ALU = mybir.AluOpType
ACT = mybir.ActivationFunctionType
AX = mybir.AxisListType

P = 128
BATCH, SEQ = 16, 512
TOKENS = BATCH * SEQ
TILES = TOKENS // P
TPB = SEQ // P
HEADS, HD = 16, 8
GH = 4
GROUPS = HEADS // GH
VC = HD + 1
LAT = 32
E, F = 8, 512
FB = F // P
SLOTS = 256
HALVES = SLOTS // P
ROUTED = (2 * TOKENS + E * (SLOTS - 1)) // SLOTS
ROUTED += ROUTED % 2
SHARED = TOKENS // SLOTS
ETILES = ROUTED + SHARED
ROUTED_ROWS = ROUTED * SLOTS
ROW_W = P + 4
FILLS = 9
M_ROW = 96
EPS = 1e-5
MASKED = -1e30


def wait(eng, sem, value):
    if not isinstance(value, int) or value > 0:
        eng.wait_ge(sem, value)


def carried(eng, first, *waits):
    for _, v in waits:
        if not isinstance(v, int):
            eng.compute_val(v)
    eng.wait_ge(*first)
    for sem, v in waits:
        eng.wait_ge(sem, v)


def inside(value, count):
    return not isinstance(value, int) or 0 <= value < count


def loop(eng, count, body):
    body(0)
    with eng.Fori(1, count - 1) as i:
        body(i)
    body(count - 1)


def part_runs(order):
    runs, at = [], 0
    while at < len(order):
        count = 2 if order[at:at + 2] == [0, 1] else 1
        runs.append((at, order[at], count))
        at += count
    return runs


class Layer:

    def __init__(self, nc, semaphores):
        self.nc, self.semaphores = nc, semaphores

    def semaphore(self, name):
        if name not in self.semaphores:
            self.semaphores[name] = self.nc.alloc_semaphore(name)
        return self.semaphores[name]

    def queue_semaphore(self, name):
        return self.nc.alloc_semaphore(f"{name}_{self.index}")


def clear(nc, semaphores):
    every = list(semaphores.values())
    with nc.Block() as block:
        @block.sync
        def _(sp):
            for s in every[0::4]:
                sp.sem_clear(s)

        @block.gpsimd
        def _(pool):
            for s in every[1::4]:
                pool.sem_clear(s)

        @block.scalar
        def _(act):
            for s in every[2::4]:
                act.sem_clear(s)

        @block.vector
        def _(dve):
            for s in every[3::4]:
                dve.sem_clear(s)


def alloc(nc, ctx):
    def sb(name, shape, dt=F32):
        return ctx.enter_context(nc.sbuf_tensor(name, shape, dt))

    def psum(name, banks=1):
        return ctx.enter_context(nc.psum_tensor(name, [P, banks * SEQ], F32))

    def sem(name):
        return nc.alloc_semaphore(name)

    return sb, psum, sem


def fill_slots(pool, L, pads, filled, zeroed, numbered):
    view = L.slots_in.rearrange("(z p r) n -> z p r n", z=FILLS, p=P)
    r = ROUTED_ROWS // FILLS // P
    pool.memset(pads[:, :, :, :], 0.0).then_inc(zeroed, 1)
    pool.wait_ge(zeroed, 1)
    for z in range(FILLS):
        wait(pool, filled[z % 2], 16 * (z // 2))
        pool.iota(pads[:, z % 2, :, P:P + 1].bitcast(I32), pattern=[[1, r], [0, 1]],
                  base=2 * TOKENS + z * P * r, channel_multiplier=r).then_inc(numbered, 1)
        pool.wait_ge(numbered, z + 1)
        pool.dma_start(view[z], pads[:, z % 2]).then_inc(filled[z % 2], 16)
    for i in range(2):
        pool.wait_ge(filled[i], 16 * ((FILLS + 1 - i) // 2))


def load_constants(nc, layer, d, w):
    with ExitStack() as ctx:
        sb, psum, sem = alloc(nc, ctx)
        loaded, folded, copied, ready = sem("w_loaded"), sem("w_folded"), sem("w_copied"), sem("w_ready")
        masks_zero, pads_zero, numbered = sem("w_masks_zero"), sem("w_pads_zero"), sem("w_numbered")
        pads = sb("w_pads", [P, 2, ROUTED_ROWS // FILLS // P, ROW_W])
        filled = [layer.queue_semaphore(f"w_filled{i}") for i in range(2)]
        ps = [psum(f"w_ps{i}") for i in range(2)]
        t = {}
        for name in ("wqT", "wkT", "wpx", "cq", "ck", "cv", "mask8", "mask32x32", "rot", "wqkx"):
            t[name] = sb("t_" + name, [P, P])
        for name in ("q2lx", "kv2lx", "mask32"):
            t[name] = sb("t_" + name, [P, HEADS * LAT])
        for name in ("kv2lrep", "l2orep"):
            t[name] = sb("t_" + name, [LAT, P])
        for name in ("bq", "bk", "cqb", "ckb", "cvb", "q2lbx", "kv2lbx", "l2obx"):
            t[name] = sb("t_" + name, [P, 1])
        kv2lb = sb("t_kv2lb", [LAT, 1])
        cprojb = sb("t_cprojb", [1, P])
        bd = {n: sb("bd_" + n, [P, P]) for n in ("wp", "v")}
        for n in ("q", "k"):
            bd[n] = sb("bd_" + n, [P, HEADS * LAT])

        loads = [(t[n], d[n]) for n in t] + [(kv2lb, d["kv2lb"]), (cprojb, d["cprojb"])]
        loads += [(w[n], d[n]) for n in ("ident", "tri", "cos", "sin", "wv0", "bv0", "wr0", "wr1",
                                         "bqk", "cprojT")]
        folds = []

        def fold(m, n, products, evacuate, chained=False):
            folds.append((m, n, products, evacuate, chained))

        def copy_to(out):
            return lambda eng, p: [eng.tensor_copy(out, p)]

        fold(P, P, [(t["wqT"], bd["wp"])], copy_to(w["wq0"][:, :]))
        fold(P, P, [(t["wkT"], bd["wp"])], copy_to(w["wk0"][:, :]))
        fold(P, 1, [(bd["wp"], t["bq"])], copy_to(w["bq0"][:, :]))
        fold(P, 1, [(bd["wp"], t["bk"])], copy_to(w["bk0"][:, :]))
        for s, c, x, lb in (("q", "cq", "cqb", "q2lbx"), ("k", "ck", "ckb", "kv2lbx")):
            def both(eng, p, s=s):
                if s == "q":
                    return [eng.tensor_copy(w["waq"][:, :], p)]
                turned = w["wbk"][:, :].rearrange("p (j two) -> p j two", two=2)
                plain = p.rearrange("p (j two) -> p j two", two=2)
                return [eng.tensor_copy(w["wa" + s][:, :], p),
                        eng.tensor_scalar(turned[:, :, 0], plain[:, :, 1], -1.0, None, ALU.mult),
                        eng.tensor_copy(turned[:, :, 1], plain[:, :, 0])]
            fold(P, HEADS * LAT, [(t[c], bd[s])], both)

            def bias(eng, p, s=s, lb=lb):
                return [eng.tensor_tensor(w["ba" + s][:, :], p, t[lb][:, :].to_broadcast([P, GROUPS]), ALU.add)]
            fold(P, GROUPS, [[(bd[s][:, g * P:(g + 1) * P], t[x])] for g in range(GROUPS)], bias)
        fold(P, GROUPS, [(t["rot"], w["bak"])], copy_to(w["bbk"][:, :]), chained=True)
        fold(P, P, [(t["rot"], w["wqk"])],
             lambda eng, p: [eng.tensor_scalar(w["wqkr"][:, :], p, -1.0, None, ALU.mult)])
        fold(P, P, [(t["kv2lrep"], t["l2orep"])],
             lambda eng, p: [eng.tensor_tensor(bd["v"][:, :], p, t["mask8"][:, :], ALU.mult)])
        fold(P, P, [(t["cv"], bd["v"])], copy_to(w["wv1"][:, :]), chained=True)
        fold(1, P, [(t["cvb"], bd["v"]), (kv2lb, t["l2orep"])], copy_to(w["bv1"][:, :]))
        fold(1, P, [(t["l2obx"], w["cprojT"])],
             lambda eng, p: [eng.tensor_tensor(w["bs1"][:, :], p, cprojb[:, :], ALU.add)])
        BUILT = 4

        with nc.Block() as block:
            @block.sync
            def _(sp):
                for out, src in loads:
                    sp.dma_start(out[:, :], src).then_inc(loaded, 16)

            @block.vector
            def _(dve):
                dve.memset(w["ones"][:, :], 1.0)
                dve.memset(w["eps"][:, :], EPS)
                dve.wait_ge(loaded, 16 * len(loads))
                dve.tensor_tensor(bd["wp"][:, :], t["wpx"][:, :], t["mask8"][:, :], ALU.mult).then_inc(ready, 1)
                dve.tensor_tensor(bd["q"][:, :], t["q2lx"][:, :], t["mask32"][:, :], ALU.mult).then_inc(ready, 1)
                dve.tensor_tensor(bd["k"][:, :], t["kv2lx"][:, :], t["mask32"][:, :], ALU.mult).then_inc(ready, 1)
                dve.tensor_tensor(w["wqk"][:, :], t["wqkx"][:, :], t["mask32x32"][:, :], ALU.mult).then_inc(ready, 1)
                for i, (m, n, _, evacuate, _) in enumerate(folds):
                    dve.wait_ge(folded, i + 1)
                    evacuate(dve, ps[i % 2][0:m, 0:n])[-1].then_inc(copied, 1)

            @block.tensor
            def _(pe):
                pe.wait_ge(ready, BUILT)
                for i, (m, n, products, _, chained) in enumerate(folds):
                    wait(pe, copied, i if chained else i - 1)
                    if isinstance(products[0], list):
                        for c, [(a, b)] in enumerate(products):
                            mm = pe.matmul(ps[i % 2][0:m, c:c + 1], a[:, :], b[:, :], start=True, stop=True)
                    else:
                        for j, (a, b) in enumerate(products):
                            mm = pe.matmul(ps[i % 2][0:m, 0:n], a[:, :], b[:, :],
                                           start=(j == 0), stop=(j == len(products) - 1))
                    mm.then_inc(folded, 1)

            @block.gpsimd
            def _(pool):
                pool.memset(w["mask"][:, :], 0.0).then_inc(masks_zero, 1)
                pool.wait_ge(masks_zero, 1)
                pool.affine_select(out=w["mask"][:, SEQ - P:SEQ], in_=w["mask"][:, SEQ - P:SEQ],
                                   compare_op=ALU.is_ge, fill=MASKED, base=0, pattern=[[-1, P]],
                                   channel_multiplier=1)
                fill_slots(pool, layer, pads, filled, pads_zero, numbered)


def prepare(nc, L, before, w):
    l = L.index
    PAIRS = GROUPS * BATCH
    heads = P // L.head_rows
    BUFS = 2 if l == 0 else GROUPS
    with ExitStack() as ctx:
        sb, psum, sem = alloc(nc, ctx)
        S = lambda name: L.semaphore(f"a_{name}")
        x = sb(f"a{l}_x", [P, 2, TPB, P])
        stats = sb(f"a{l}_stats", [P, 2, TPB, 6])
        mean_var = sb(f"a{l}_mv", [P, 2, TPB, 2])
        sd = sb(f"a{l}_sd", [P, 2, TPB])
        rstd = sb(f"a{l}_rstd", [P, 2, TPB])
        xn = sb(f"a{l}_xn", [P, 2, TPB, P])
        if l == 1:
            old = [sb(f"a{l}_{n}", [P, 2, TPB, P]) for n in ("x0", "xn0", "s0", "first0", "second0", "shared0")]
            x_old, xn_old, s_old, first, second, ffn = old
            silu = sb(f"a{l}_silu", [P, 2, TPB, P])
        xT = sb(f"a{l}_xT", [P, 2, SEQ])
        v = sb(f"a{l}_v", [P, 2, TPB, HEADS, VC])
        parts = sb(f"a{l}_parts", [P, 2, BUFS, 2, SEQ], F32R)
        ps_x = psum(f"a{l}_ps_x")
        ps_r = psum(f"a{l}_ps_r")[:, 0:TPB * E].rearrange("p (t e) -> p t e", e=E)
        ps_v = psum(f"a{l}_ps_v")[:, :].rearrange("p (t n) -> p t n", n=P)
        if l == 0:
            ps_j = [[psum(f"a{l}_ps_j{j}{s}") for s in range(2)] for j in range(2)]
        else:
            z_mixed = sb(f"a{l}_z_mixed", [P, 2, 2, SEQ])
            k_mixed = sb(f"a{l}_k_mixed", [P, 2, 3, SEQ])
            ps_z, ps_k = psum(f"a{l}_ps_z"), [psum(f"a{l}_ps_k{i}") for i in range(2)]
            ps_q = [psum(f"a{l}_ps_q{i}") for i in range(2)]

        x_in = [S(f"x_in{s}") for s in range(2)]
        xn_out = [S(f"xn_out{s}") for s in range(2)]
        v_out = [S(f"v_out{s}") for s in range(2)]
        x_out = [S(f"x_out{s}") for s in range(2)]
        xn_added, added, ffn_done, gated, product, joined = (
            S("xn_added"), S("added"), S("ffn"), S("gated"), S("product"), S("joined"))
        q_out = [S(f"q_out{i}") for i in range(BUFS)]
        k_out = [S(f"k_out{i}") for i in range(BUFS)]
        var_done, sd_done, normed, stat = S("var"), S("sd"), S("normed"), S("stat")
        turned, xT_done, rstd_done = S("turned"), S("xT"), S("rstd")
        routed, logits_done = S("routed"), S("logits")
        v_mm, v_done, v_ones = S("v_mm"), S("v_done"), S("v_ones")
        proj, hi_done, lo_done = S("proj"), S("hi"), S("lo")
        z_mm, z_done, q_mm, q_hi, q_lo = S("z_mm"), S("z"), S("q_mm"), S("q_hi"), S("q_lo")
        k_mm, k_done, summed, k_hi, k_lo = S("k_mm"), S("k"), S("summed"), S("k_hi"), S("k_lo")

        x_view = L.x_in.rearrange("(b t p) n -> b p t n", t=TPB, p=P)
        xn_view = L.xn.rearrange("(b t p) n -> b p t n", t=TPB, p=P)
        v_view = L.v.rearrange("(b p) n -> b p n", p=P)
        bias0 = (w["bq0"], w["bk0"])

        def view(rows):
            return rows.rearrange("(b t p) n -> b p t n", t=TPB, p=P)

        if l == 1:
            sources = (before.x_in, before.xn, before.s, before.routed[0:TOKENS, :],
                       before.routed[TOKENS:2 * TOKENS, :], before.shared)

        def pair(b, g, back):
            turns, g = divmod(g - back, GROUPS)
            return b + turns, g, GROUPS * (b + turns) + g

        def each_pair(b, *work, ahead=()):
            for g in range(GROUPS):
                for at, by, do in ahead:
                    if at == g and inside(b + by, BATCH):
                        do()
                for do, back in work:
                    pb, pg, m = pair(b, g, back)
                    if inside(m, PAIRS):
                        do(pb, pg, m)

        def rest(*work):
            for do, back in work:
                for g in range(GROUPS - back, GROUPS):
                    do(BATCH - 1, g, GROUPS * (BATCH - 1) + g)

        with nc.Block() as block:
            @block.sync
            def _(sp):
                def load_old(bb, s):
                    b = 2 * bb + s
                    wait(sp, joined, b - 1)
                    for dst, src in zip(old, sources):
                        sp.dma_start(dst[:, s], view(src)[bass.ds(b, 1)].rearrange("o p t n -> (o p) t n")
                                     ).then_inc(x_in[s], 16)

                def store_x(bb, s):
                    b = 2 * bb + s
                    sp.wait_ge(joined, b + 1)
                    sp.dma_start(x_view[bass.ds(b, 1)].rearrange("o p t n -> (o p) t n"), x[:, s]
                                 ).then_inc(x_out[s], 16)

                def load(bb, s):
                    b = 2 * bb + s
                    wait(sp, normed, TPB * (b - 1))
                    sp.dma_start(x[:, s], x_view[bass.ds(b, 1)].rearrange("o p t n -> (o p) t n")
                                 ).then_inc(x_in[s], 16)

                def store_parts(which, b, g, buf, done):
                    dst = (L.q, L.k)[which][g * heads:(g + 1) * heads, :, :, bass.ds(b * SEQ, SEQ)]
                    for part in range(2):
                        sp.dma_start(dst[:, part], parts[:, which, buf, part].bitcast(F32)).then_inc(done, 16)

                def store_k(b, g, m):
                    sp.wait_ge(k_hi, m + 1)
                    sp.wait_ge(k_lo, m + 1)
                    store_parts(1, b, g, g, k_out[g])

                def store_q(b, g, m):
                    sp.wait_ge(q_hi, m + 1)
                    sp.wait_ge(q_lo, m + 1)
                    store_parts(0, b, g, g, q_out[g])

                def body(bb):
                    for s in range(2):
                        b = 2 * bb + s
                        if isinstance(bb, int) and b == 0 and l == 0:
                            load(0, 0)
                            load(0, 1)
                        sp.wait_ge(normed, TPB * (b + 1))
                        sp.dma_start(xn_view[bass.ds(b, 1)].rearrange("o p t n -> (o p) t n"), xn[:, s]
                                     ).then_inc(xn_out[s], 16)
                        if l == 0 and inside(b + 2, BATCH):
                            load(bb + 1, s)
                        if l == 0:
                            for j in range(2):
                                sp.wait_ge(hi_done, 2 * b + j + 1)
                                sp.wait_ge(lo_done, 2 * b + j + 1)
                                store_parts(j, b, 0, s, (q_out, k_out)[j][s])
                        else:
                            each_pair(b, (store_k, 1), (store_q, 2))
                        sp.wait_ge(v_done, b + 1)
                        sp.dma_start(v_view[bass.ds(b, 1)].rearrange("o p n -> (o p) n"),
                                     v[:, s].rearrange("p t h c -> p (t h c)")).then_inc(v_out[s], 16)
                        if l == 1 and inside(b + 2, BATCH):
                            store_x(bb + 1, s)
                            if inside(b + 4, BATCH):
                                load_old(bb + 2, s)

                if l == 0:
                    loop(sp, BATCH // 2, body)
                else:
                    load_old(0, 0)
                    load_old(0, 1)
                    for s in range(2):
                        store_x(0, s)
                        load_old(1, s)
                    body(0)
                    with sp.Fori(1, BATCH // 2 - 2) as bb:
                        body(bb)
                    body(BATCH // 2 - 2)
                    body(BATCH // 2 - 1)
                    for s in range(2):
                        sp.wait_ge(x_out[s], 16 * (BATCH // 2))
                    rest((store_k, 1), (store_q, 2))
                for s in range(2):
                    sp.wait_ge(xn_out[s], 16 * (BATCH // 2))
                    sp.wait_ge(v_out[s], 16 * (BATCH // 2))
                for out in (*q_out, *k_out):
                    sp.wait_ge(out, 32 * (BATCH // 2 if l == 0 else BATCH))

            @block.vector
            def _(dve):
                dve.memset(v[:, :, :, :, HD:VC], 1.0).then_inc(v_ones, 1)

                def add_up(bb, s):
                    b = 2 * bb + s
                    for k, (chosen, done) in enumerate(((first, added), (second, ffn_done))):
                        if k == 0:
                            dve.wait_ge(xn_added, b + 1)
                        else:
                            dve.wait_ge(added, TPB * (b + 1))
                        for t in range(TPB):
                            gate = w["gate"][:, k, bass.ds(TPB * b + t, 1)]
                            dve.scalar_tensor_tensor(ffn[:, s, t], chosen[:, s, t], gate, ffn[:, s, t],
                                                     ALU.mult, ALU.add).then_inc(done, 1)

                def join(bb, s):
                    b = 2 * bb + s
                    dve.wait_ge(gated, b + 1)
                    dve.tensor_tensor(silu[:, s], s_old[:, s], silu[:, s], ALU.mult).then_inc(product, 1)
                    wait(dve, x_out[s], 16 * bb)
                    wait(dve, normed, TPB * (b - 1))
                    dve.wait_ge(product, b + 1)
                    dve.tensor_tensor(x[:, s], silu[:, s], x_old[:, s], ALU.add).then_inc(joined, 1)

                def measure(bb, s):
                    b = 2 * bb + s
                    if l == 0:
                        dve.wait_ge(x_in[s], 16 * (bb + 1))
                    else:
                        dve.wait_ge(joined, b + 1)
                    for t in range(TPB):
                        dve.bn_stats(stats[:, s, t, :], x[:, s, t, :]).then_inc(stat, 1)
                    carried(dve, (stat, 1), (stat, TPB * (b + 1)))
                    for t in range(TPB):
                        dve.bn_aggr(mean_var[:, s, t, :], stats[:, s, t, :]).then_inc(var_done, 1)

                def norm(bb, s):
                    b = 2 * bb + s
                    dve.wait_ge(sd_done, b + 1)
                    dve.reciprocal(rstd[:, s, :], sd[:, s, :]).then_inc(rstd_done, 1)
                    dve.wait_ge(rstd_done, b + 1)
                    wait(dve, xn_out[s], 16 * bb)
                    wait(dve, turned, b - 1)
                    for t in range(TPB):
                        dve.tensor_scalar(xn[:, s, t, :], x[:, s, t, :], mean_var[:, s, t, 0:1],
                                          rstd[:, s, t:t + 1], ALU.subtract, ALU.mult).then_inc(normed, 1)

                def mix_z(b, g, m):
                    dve.wait_ge(z_mm, m + 1)
                    wait(dve, q_mm, m - 1)
                    for i, angle in enumerate(("cos", "sin")):
                        dve.scalar_tensor_tensor(z_mixed[:, g % 2, i, :], ps_z[:, :], w["baq"][:, g:g + 1],
                                                 w[angle][:, :], ALU.add, ALU.mult).then_inc(z_done, 1)

                def mix_k(b, g, m):
                    dve.wait_ge(k_mm, m + 1)
                    wait(dve, summed, m - 1)
                    for i, (bias, angle) in enumerate((("bak", "cos"), ("bbk", "sin"))):
                        dve.scalar_tensor_tensor(k_mixed[:, g % 2, i, :], ps_k[i][:, :], w[bias][:, g:g + 1],
                                                 w[angle][:, :], ALU.add, ALU.mult).then_inc(k_done, 1)

                def split_q(b, g, m):
                    dve.wait_ge(q_hi, m + 1)
                    dve.scalar_tensor_tensor(parts[:, 0, g, 1, :], ps_q[g % 2][:, :], w["bqk"][:, 0:1],
                                             parts[:, 0, g, 0, :], ALU.add, ALU.subtract).then_inc(q_lo, 1)

                def body(bb):
                    for s in range(2):
                        b = 2 * bb + s
                        if isinstance(bb, int) and bb == 0 and s == 0:
                            if l == 1:
                                add_up(0, 0)
                                add_up(0, 1)
                                join(0, 0)
                            measure(0, 0)
                            norm(0, 0)
                            if l == 1:
                                join(0, 1)
                        if l == 0 and inside(b + 1, BATCH):
                            measure(bb + s, 1 - s)
                        dve.wait_ge(routed, b + 1)
                        dve.tensor_copy(w["logits"][:, bass.ds(b * TPB, TPB), :], ps_r[:, :, :]
                                        ).then_inc(logits_done, 1)
                        if l == 1:
                            each_pair(b, (mix_z, 0), (split_q, 2), (mix_k, 0),
                                      ahead=((0, 1, lambda: measure(bb + s, 1 - s)),
                                             (1, 2, lambda: add_up(bb + 1, s)),
                                             (2, 1, lambda: norm(bb + s, 1 - s)),
                                             (3, 2, lambda: join(bb + 1, s))))
                            continue
                        if inside(b + 1, BATCH):
                            norm(bb + s, 1 - s)
                        for j in range(2):
                            dve.wait_ge(hi_done, 2 * b + j + 1)
                            dve.scalar_tensor_tensor(parts[:, j, s, 1, :], ps_j[j][s][:, :], bias0[j][:, 0:1],
                                                     parts[:, j, s, 0, :], ALU.add, ALU.subtract
                                                     ).then_inc(lo_done, 1)

                loop(dve, BATCH // 2, body)
                if l == 1:
                    rest((split_q, 2))

            @block.gpsimd
            def _(pool):
                if l == 0:
                    return

                def add_k(b, g, m):
                    pool.wait_ge(k_done, 2 * m + 2)
                    wait(pool, k_lo, m - 1)
                    pool.tensor_tensor(k_mixed[:, g % 2, 2, :], k_mixed[:, g % 2, 0, :], k_mixed[:, g % 2, 1, :],
                                       ALU.add).then_inc(summed, 1)

                def split_k(b, g, m):
                    pool.wait_ge(k_hi, m + 1)
                    pool.tensor_tensor(parts[:, 1, g, 1, :], k_mixed[:, g % 2, 2, :], parts[:, 1, g, 0, :],
                                       ALU.subtract).then_inc(k_lo, 1)

                def add_xn(bb, s):
                    pool.wait_ge(x_in[s], 16 * len(old) * (bb + 1))
                    pool.tensor_tensor(ffn[:, s], ffn[:, s], xn_old[:, s], ALU.add).then_inc(xn_added, 1)

                def body(bb):
                    for s in range(2):
                        each_pair(2 * bb + s, (add_k, 0), (split_k, 1), ahead=((0, 2, lambda: add_xn(bb + 1, s)),))

                add_xn(0, 0)
                add_xn(0, 1)
                loop(pool, BATCH // 2, body)
                rest((split_k, 1))

            @block.scalar
            def _(act):
                def gate(bb, s):
                    b = 2 * bb + s
                    act.wait_ge(ffn_done, TPB * (b + 1))
                    wait(act, joined, b - 1)
                    act.activation(silu[:, s], ffn[:, s], ACT.Silu).then_inc(gated, 1)

                def sqrt(b, s):
                    act.wait_ge(var_done, TPB * (b + 1))
                    act.activation(sd[:, s, :], mean_var[:, s, :, 1], ACT.Sqrt, bias=w["eps"][:, 0:1]
                                   ).then_inc(sd_done, 1)

                def hi_of_q(b, g, m):
                    act.wait_ge(q_mm, m + 1)
                    wait(act, q_out[g], 32 * b)
                    act.activation(parts[:, 0, g, 0, :], ps_q[g % 2][:, :], ACT.Identity,
                                   bias=w["bqk"][:, 0:1]).then_inc(q_hi, 1)

                def hi_of_k(b, g, m):
                    act.wait_ge(summed, m + 1)
                    wait(act, k_out[g], 32 * b)
                    act.activation(parts[:, 1, g, 0, :], k_mixed[:, g % 2, 2, :], ACT.Copy).then_inc(k_hi, 1)

                def copy_xT(b, s):
                    act.wait_ge(turned, b + 1)
                    wait(act, proj if l == 0 else k_mm, (2 if l == 0 else GROUPS) * (b - 1))
                    act.activation(xT[:, s, :], ps_x[:, :], ACT.Copy).then_inc(xT_done, 1)

                def body(bb):
                    for s in range(2):
                        b = 2 * bb + s
                        if isinstance(bb, int) and bb == 0 and s == 0:
                            if l == 1:
                                gate(0, 0)
                                gate(0, 1)
                            sqrt(0, 0)
                            copy_xT(0, 0)
                        if l == 0 and inside(b + 1, BATCH):
                            sqrt(b + 1, 1 - s)
                        act.wait_ge(v_mm, b + 1)
                        act.wait_ge(v_ones, 1)
                        wait(act, v_out[s], 16 * bb)
                        act.activation(v[:, s, :, :, 0:HD],
                                       ps_v[:, :, :].rearrange("p t (h c) -> p t h c", h=HEADS),
                                       ACT.Copy).then_inc(v_done, 1)
                        if l == 1:
                            each_pair(b, (hi_of_q, 1), (hi_of_k, 0), ahead=(
                                (1, 1, lambda: sqrt(b + 1, 1 - s)), (2, 2, lambda: gate(bb + 1, s)),
                                (3, 1, lambda: copy_xT(b + 1, 1 - s))))
                            continue
                        for j in range(2):
                            act.wait_ge(proj, 2 * b + j + 1)
                            wait(act, (q_out, k_out)[j][s], 32 * bb)
                            act.activation(parts[:, j, s, 0, :], ps_j[j][s][:, :], ACT.Identity,
                                           bias=bias0[j][:, 0:1]).then_inc(hi_done, 1)
                            if j == 0 and inside(b + 1, BATCH):
                                copy_xT(b + 1, 1 - s)

                loop(act, BATCH // 2, body)
                if l == 1:
                    rest((hi_of_q, 1))

            @block.tensor
            def _(pe):
                def turn(b, s):
                    pe.wait_ge(normed, TPB * (b + 1))
                    wait(pe, xT_done, b)
                    for t in range(TPB):
                        mm = pe.transpose(ps_x[:, t * P:(t + 1) * P], xn[:, s, t, :], w["ident"][:, :])
                    mm.then_inc(turned, 1)

                def make_q(b, g, m):
                    wait(pe, q_lo, m - 1)
                    pe.wait_ge(z_done, 2 * m + 2)
                    pe.matmul(ps_q[g % 2][:, :], w["wqk"][:, :], z_mixed[:, g % 2, 0, :], start=True, stop=False)
                    pe.matmul(ps_q[g % 2][:, :], w["wqkr"][:, :], z_mixed[:, g % 2, 1, :],
                              start=False, stop=True).then_inc(q_mm, 1)

                def body(bb):
                    for s in range(2):
                        b = 2 * bb + s
                        if isinstance(bb, int) and bb == 0 and s == 0:
                            turn(0, 0)
                        pe.wait_ge(xT_done, b + 1)
                        wait(pe, logits_done, b)
                        for t in range(TPB):
                            mm = pe.matmul(ps_r[:, t, :], xT[:, s, t * P:(t + 1) * P], L.wr[:, :],
                                           start=True, stop=True)
                        mm.then_inc(routed, 1)
                        wait(pe, v_done, b)
                        for t in range(TPB):
                            pe.matmul(ps_v[:, t, :], xT[:, s, t * P:(t + 1) * P], L.wv[:, :],
                                      start=True, stop=False)
                            mm = pe.matmul(ps_v[:, t, :], w["ones"][0:1, :], L.bv[:, :],
                                           start=False, stop=True)
                        mm.then_inc(v_mm, 1)

                        def make_z(b, g, m, s=s):
                            wait(pe, z_done, 2 * m)
                            pe.matmul(ps_z[:, :], w["waq"][:, g * P:(g + 1) * P], xT[:, s, :],
                                      start=True, stop=True).then_inc(z_mm, 1)

                        def make_k(b, g, m, s=s):
                            wait(pe, k_done, 2 * m)
                            for i, form in enumerate(("wak", "wbk")):
                                mm = pe.matmul(ps_k[i][:, :], w[form][:, g * P:(g + 1) * P], xT[:, s, :],
                                               start=True, stop=True)
                            mm.then_inc(k_mm, 1)

                        if l == 1:
                            each_pair(b, (make_z, 0), (make_k, 0), (make_q, 1),
                                      ahead=((3, 1, lambda: turn(b + 1, 1 - s)),))
                        else:
                            for j in range(2):
                                wait(pe, lo_done, 2 * (b - 2) + j + 1)
                                pe.matmul(ps_j[j][s][:, :], (w["wq0"], w["wk0"])[j][:, :], xT[:, s, :],
                                          start=True, stop=True).then_inc(proj, 1)
                                if j == 0 and inside(b + 1, BATCH):
                                    turn(b + 1, 1 - s)

                loop(pe, BATCH // 2, body)
                if l == 1:
                    rest((make_q, 1))


def dispatch(L, w, sb, ps_in, ps_all, dispatched):
    l = L.index
    TE = [P, TILES, E]
    S = lambda name: L.semaphore(f"b_{name}")
    big = {n: sb(f"b{l}_{n}", TE) for n in ("ex", "pick", "oh1", "oh2", "oh", "total", "sum0", "sum1", "pos")}
    small = {n: sb(f"b{l}_{n}", [P, TILES]) for n in ("top", "all", "first", "p1", "p2")}
    iota_e = sb(f"b{l}_iota_e", [P, E])
    iota_c = sb(f"b{l}_iota_c", [P, E, TOKENS // SLOTS])
    iota_t = sb(f"b{l}_iota_t", [P, ROUTED, E])
    over = sb(f"b{l}_over", [P, E, TOKENS // SLOTS])
    before = sb(f"b{l}_before", [P, ROUTED, E])
    tiles = sb(f"b{l}_tiles", [P, 4, E])
    chain, iotas, shifted, exps = S("chain"), S("iotas"), S("shifted"), S("exps")
    onehot, counted = S("onehot"), S("counted")

    def over_e(x):
        return x[:, :].unsqueeze(2).to_broadcast(TE)

    def over_t(x):
        return x.unsqueeze(1).to_broadcast(TE)

    def on_gpsimd(pool):
        pool.iota(iota_e[:, :], pattern=[[1, E]], base=-E, channel_multiplier=0,
                  allow_small_or_imprecise_dtypes=True).then_inc(iotas, 1)
        pool.iota(iota_c[:, :, :], pattern=[[0, E], [SLOTS, TOKENS // SLOTS]], base=0,
                  channel_multiplier=0, allow_small_or_imprecise_dtypes=True).then_inc(iotas, 1)
        pool.iota(iota_t[:, :, :], pattern=[[1, ROUTED], [0, E]], base=0,
                  channel_multiplier=0, allow_small_or_imprecise_dtypes=True).then_inc(iotas, 1)

    def on_scalar(act):
        act.wait_ge(shifted, 1)
        act.activation(big["ex"][:, :, :], big["ex"][:, :, :], ACT.Exp).then_inc(exps, 1)

    def on_tensor(pe):
        pe.wait_ge(onehot, 1)
        flat = big["oh"][:, :, :].rearrange("p t e -> p (t e)")
        pe.matmul(ps_in[:, :], w["tri"][:, :], flat, start=True, stop=True)
        pe.matmul(ps_all[:, :], w["ones"][:, :], flat, start=True, stop=True).then_inc(counted, 1)

    def on_vector(dve):
        done = [0]

        def step(ins):
            done[0] += 1
            ins.then_inc(chain, 1)
            dve.wait_ge(chain, done[0])

        ex, pick, pos = big["ex"], big["pick"], big["pos"]
        step(dve.tensor_reduce(small["top"][:, :], w["logits"][:, :, :], AX.X, ALU.max))
        dve.tensor_tensor(ex[:, :, :], w["logits"][:, :, :], over_e(small["top"]), ALU.subtract
                          ).then_inc(shifted, 1)
        dve.wait_ge(exps, 1)
        dve.wait_ge(iotas, 3)
        step(dve.tensor_reduce(small["all"][:, :], ex[:, :, :], AX.X, ALU.add))
        step(dve.reciprocal(small["all"][:, :], small["all"][:, :]))
        for k, (oh, p) in enumerate(((big["oh1"], small["p1"]), (big["oh2"], small["p2"]))):
            step(dve.tensor_reduce(small["top"][:, :], ex[:, :, :], AX.X, ALU.max))
            step(dve.tensor_tensor(pick[:, :, :], ex[:, :, :], over_e(small["top"]), ALU.is_equal))
            step(dve.tensor_tensor(pick[:, :, :], pick[:, :, :], over_t(iota_e[:, :]), ALU.mult))
            step(dve.tensor_reduce(small["first"][:, :], pick[:, :, :], AX.X, ALU.min))
            step(dve.tensor_tensor(oh[:, :, :], over_t(iota_e[:, :]), over_e(small["first"]), ALU.is_equal))
            step(dve.tensor_tensor(p[:, :], small["top"][:, :], small["all"][:, :], ALU.mult))
            if k == 0:
                step(dve.scalar_tensor_tensor(ex[:, :, :], oh[:, :, :], -2.0, ex[:, :, :],
                                              ALU.mult, ALU.add))
        dve.tensor_tensor(big["oh"][:, :, :], big["oh1"][:, :, :], big["oh2"][:, :, :], ALU.add
                          ).then_inc(onehot, 1)
        if l == 0:
            step(dve.tensor_copy(w["gate"][:, 0, :], small["p1"][:, :]))
            step(dve.tensor_copy(w["gate"][:, 1, :], small["p2"][:, :]))
        else:
            step(dve.tensor_tensor(small["first"][:, :], small["p1"][:, :], small["p2"][:, :], ALU.add))
            step(dve.tensor_scalar(small["first"][:, :], small["first"][:, :], 1e-9, None, ALU.add))
            step(dve.reciprocal(small["first"][:, :], small["first"][:, :]))
            step(dve.tensor_tensor(w["gate"][:, 0, :], small["p1"][:, :], small["first"][:, :], ALU.mult))
            step(dve.tensor_tensor(w["gate"][:, 1, :], small["p2"][:, :], small["first"][:, :], ALU.mult))
        dve.wait_ge(counted, 1)
        flat = lambda x: x[:, :, :].rearrange("p t e -> p (t e)")
        dve.tensor_copy(flat(big["total"]), ps_all[:, :])
        step(dve.tensor_copy(flat(big["sum0"]), ps_all[:, :]))
        a, b = big["sum0"], big["sum1"]
        reach = 1
        while reach < TILES:
            dve.tensor_copy(b[:, 0:reach, :], a[:, 0:reach, :])
            step(dve.tensor_tensor(b[:, reach:TILES, :], a[:, reach:TILES, :],
                                   a[:, 0:TILES - reach, :], ALU.add))
            a, b = b, a
            reach *= 2
        counts = a[:, TILES - 1, :]
        step(dve.tensor_tensor(over[:, :, :], counts.unsqueeze(2).to_broadcast([P, E, TOKENS // SLOTS]),
                               iota_c[:, :, :], ALU.is_gt))
        step(dve.tensor_reduce(tiles[:, 0, :], over[:, :, :], AX.X, ALU.add))
        step(dve.tensor_copy(tiles[:, 1, :], tiles[:, 0, :]))
        e, f, reach = 1, 2, 1
        while reach < E:
            dve.tensor_copy(tiles[:, f, 0:reach], tiles[:, e, 0:reach])
            step(dve.tensor_tensor(tiles[:, f, reach:E], tiles[:, e, reach:E],
                                   tiles[:, e, 0:E - reach], ALU.add))
            e, f, reach = f, e, 2 * reach
        step(dve.tensor_tensor(before[:, :, :], tiles[:, e, :].unsqueeze(1).to_broadcast([P, ROUTED, E]),
                               iota_t[:, :, :], ALU.is_le))
        step(dve.tensor_reduce(w["tile_f"][:, :], before[:, :, :], AX.X, ALU.add))
        step(dve.tensor_copy(w["tile_expert"][:, :], w["tile_f"][:, :]))
        step(dve.tensor_tensor(tiles[:, 3, :], tiles[:, e, :], tiles[:, 0, :], ALU.subtract))
        step(dve.tensor_scalar(tiles[:, 3, :], tiles[:, 3, :], float(SLOTS), None, ALU.mult))
        step(dve.tensor_tensor(pos[:, :, :], a[:, :, :], big["total"][:, :, :], ALU.subtract))
        step(dve.tensor_tensor(pos[:, :, :], pos[:, :, :], over_t(tiles[:, 3, :]), ALU.add))
        step(dve.tensor_tensor(flat(pos), flat(pos), ps_in[:, :], ALU.add))
        for k, oh in enumerate((big["oh1"], big["oh2"])):
            step(dve.tensor_tensor(pick[:, :, :], oh[:, :, :], pos[:, :, :], ALU.mult))
            step(dve.tensor_reduce(small["first"][:, :], pick[:, :, :], AX.X, ALU.add))
            if k == 0:
                step(dve.tensor_copy(w["slot"][:, k, :], small["first"][:, :]))
            else:
                dve.tensor_copy(w["slot"][:, k, :], small["first"][:, :]).then_inc(dispatched, 1)

    return on_gpsimd, on_scalar, on_tensor, on_vector


def experts(nc, L, next_layer, w):
    l = L.index
    N = 4
    TURNS, ROUTED_TURNS = ETILES // N, ROUTED // N
    with ExitStack() as ctx:
        sb, psum, sem = alloc(nc, ctx)
        S = lambda name: L.semaphore(f"c_{name}")
        up = sb(f"c{l}_up", [P, N, F + FB])
        down = sb(f"c{l}_down", [P, N, FB, P])
        b2 = sb(f"c{l}_b2", [1, N, P])
        rows = sb(f"c{l}_rows", [P, N, HALVES, ROW_W])
        targets = sb(f"c{l}_targets", [P, N, HALVES], I32)
        targets_done = S("targets")
        xT = sb(f"c{l}_xT", [P, 2, SLOTS])
        hT = sb(f"c{l}_hT", [P, 2, FB, SLOTS])
        y = sb(f"c{l}_y", [P, N, HALVES, P])
        ps_x = psum(f"c{l}_ps_x")
        ps_h = [psum(f"c{l}_ps_h{s}", 2) for s in range(2)]
        ps_y = [psum(f"c{l}_ps_y{s}") for s in range(2)]
        rows_in = [S(f"rows_in{i}") for i in range(N)]
        weights_in = [S(f"weights_in{i}") for i in range(N)]
        routed_out = [L.queue_semaphore(f"routed_out{i}") for i in range(N)]
        shared_out = [S(f"shared_out{i}") for i in range(N)]
        turned, xT_done, h_mm, h_done, y_mm, y_done = (
            S("turned"), S("xT"), S("h_mm"), S("h"), S("y_mm"), S("y"))
        if next_layer:
            pads = sb(f"c{l}_pads", [P, 2, ROUTED_ROWS // FILLS // P, ROW_W])
            pads_zero, numbered = S("pads_zero"), S("numbered")
            pads_out = [L.queue_semaphore(f"pads_out{i}") for i in range(2)]
        WEIGHT_DMAS = 2 if l == 0 else 3
        H_STEPS = 1 if l == 0 else FB

        routed_in = L.slots_in.rearrange("(t a p) n -> t p a n", a=HALVES, p=P)
        shared_in = L.xn.rearrange("(t a p) n -> t p a n", a=HALVES, p=P)
        shared_view = L.shared.rearrange("(t a p) n -> t p a n", a=HALVES, p=P)

        def follow(tt, i, by):
            return tt + (i + by) // N, (i + by) % N

        def each_tile(eng, step):
            def turn(shared):
                def body(tt):
                    for i in range(N):
                        step(tt, i, shared)
                return body
            turn(False)(0)
            with eng.Fori(1, ROUTED_TURNS) as tt:
                turn(False)(tt)
            turn(True)(ROUTED_TURNS)
            turn(True)(ROUTED_TURNS + 1)
            with eng.Fori(ROUTED_TURNS + 2, TURNS - 1) as tt:
                turn(True)(tt)
            turn(True)(TURNS - 1)

        def weights_of(tt, shared):
            return 16 * WEIGHT_DMAS * (ROUTED_TURNS + 1 if shared else tt + 1)

        def wait_for_output(eng, tt, i, shared):
            if shared:
                eng.wait_ge(shared_out[i], 16 * (tt - ROUTED_TURNS + 1))
            else:
                eng.wait_ge(routed_out[i], 32 * (tt + 1))

        with nc.Block() as block:
            @block.sync
            def _(sp):
                def step(tt, i, shared):
                    t = N * tt + i
                    expert = E
                    if not shared:
                        expert = sp.value_load(w["tile_expert"][0:1, bass.ds(t, 1)], min_val=0, max_val=E)
                    wait(sp, turned, t - N + 1)
                    first_shared = isinstance(tt, int) and tt == ROUTED_TURNS
                    if not shared or first_shared:
                        wait(sp, targets_done, t - N + 1)
                    if shared:
                        src = shared_in[bass.ds(t - ROUTED, 1)]
                        sp.dma_start(rows[:, i, :, 0:P], src.rearrange("o p a n -> (o p) a n")
                                     ).then_inc(rows_in[i], 16)
                        if not first_shared:
                            return
                    else:
                        sp.dma_start(rows[:, i], routed_in[bass.ds(t, 1)].rearrange("o p a n -> (o p) a n")
                                     ).then_inc(rows_in[i], 16)
                    wait(sp, y_mm, t - N + 1)
                    sp.dma_start(up[:, i, 0:L.up_width], L.w1[bass.ds(expert, 1)].rearrange("o p n -> (o p) n")
                                 ).then_inc(weights_in[i], 16)
                    sp.dma_start(down[:, i], L.w2[bass.ds(expert, 1)].rearrange(
                        "o (p j) n -> (o p) j n", j=FB)).then_inc(weights_in[i], 16)
                    if l == 1:
                        sp.dma_start(b2[:, i, :], L.b2[bass.ds(expert, 1), :]).then_inc(weights_in[i], 16)

                each_tile(sp, step)

            @block.tensor
            def _(pe):
                def turn(tt, i):
                    t = N * tt + i
                    pe.wait_ge(rows_in[i], 16 * (tt + 1))
                    wait(pe, xT_done, t)
                    for a in range(HALVES):
                        mm = pe.transpose(ps_x[:, a * P:(a + 1) * P], rows[:, i, a, 0:P], w["ident"][:, :])
                    mm.then_inc(turned, 1)

                def go_up(tt, i, shared):
                    t, s = N * tt + i, i % 2
                    pe.wait_ge(xT_done, t + 1)
                    pe.wait_ge(weights_in[i], weights_of(tt, shared))
                    wait(pe, h_done, H_STEPS * (t - 1))
                    for j in range(FB):
                        mm = pe.matmul(ps_h[s][:, j * SLOTS:(j + 1) * SLOTS], up[:, i, j:F:FB], xT[:, s, :],
                                       start=True, stop=True)
                    mm.then_inc(h_mm, 1)

                def go_down(tt, i):
                    t, s = N * tt + i, i % 2
                    pe.wait_ge(h_done, H_STEPS * (t + 1))
                    wait(pe, y_done, t - 1)
                    for a in range(HALVES):
                        out = ps_y[s][:, a * P:(a + 1) * P]
                        for j in range(FB):
                            mm = pe.matmul(out, hT[:, s, j, a * P:(a + 1) * P], down[:, i, j, :],
                                           start=(j == 0), stop=(l == 0 and j == FB - 1))
                        if l == 1:
                            mm = pe.matmul(out, w["ones"][0:1, :], b2[:, i, :], start=False, stop=True)
                    mm.then_inc(y_mm, 1)

                def step(tt, i, shared):
                    nt, ni = follow(tt, i, 1)
                    if inside(N * nt + ni, ETILES):
                        turn(nt, ni)
                    go_up(tt, i, shared)
                    before = follow(tt, i, -1)
                    if inside(N * before[0] + before[1], ETILES):
                        go_down(*before)

                turn(0, 0)
                each_tile(pe, step)
                go_down(TURNS - 1, N - 1)

            @block.gpsimd
            def _(pool):
                def body(tt):
                    for i in range(N):
                        carried(pool, (y_done, 1), (y_done, N * tt + i + 1), (targets_done, N * tt + i + 1))
                        for a in range(HALVES):
                            pool.indirect_dma_start(
                                L.routed, bass.IndirectOffsetOnAxis(ap=targets[:, i, a:a + 1], axis=0),
                                y[:, i, a, :], None).then_inc(routed_out[i], 16)

                if next_layer:
                    fill_slots(pool, next_layer, pads, pads_out, pads_zero, numbered)
                loop(pool, ROUTED_TURNS, body)
                for i in range(N):
                    pool.wait_ge(routed_out[i], 32 * ROUTED_TURNS)

            @block.scalar
            def _(act):
                def store(tt, i):
                    act.wait_ge(y_done, N * tt + i + 1)
                    act.dma_start(shared_view[bass.ds(N * (tt - ROUTED_TURNS) + i, 1)].rearrange(
                        "o p a n -> (o p) a n"), y[:, i]).then_inc(shared_out[i], 16)

                def step(tt, i, shared):
                    t, s = N * tt + i, i % 2
                    act.wait_ge(h_mm, t + 1)
                    wait(act, y_mm, t - 1)
                    if l == 0:
                        act.activation(hT[:, s].rearrange("p j n -> p (j n)"), ps_h[s][:, :], ACT.Gelu
                                       ).then_inc(h_done, 1)
                    else:
                        act.wait_ge(weights_in[i], weights_of(tt, shared))
                        for j in range(FB):
                            act.activation(hT[:, s, j, :], ps_h[s][:, j * SLOTS:(j + 1) * SLOTS], ACT.Silu,
                                           bias=up[:, i, F + j:F + j + 1]).then_inc(h_done, 1)
                    before = follow(tt, i, -1)
                    if shared and not (isinstance(tt, int) and N * before[0] + before[1] < ROUTED):
                        store(*before)

                each_tile(act, step)
                store(TURNS - 1, N - 1)
                for i in range(N):
                    act.wait_ge(shared_out[i], 16 * (SHARED // N))

            @block.vector
            def _(dve):
                def turn(tt, i, shared):
                    t = N * tt + i
                    dve.wait_ge(turned, t + 1)
                    if not shared:
                        if not (isinstance(tt, int) and tt == 0):
                            dve.wait_ge(routed_out[i], 32 * tt)
                        dve.tensor_copy(targets[:, i, :], rows[:, i, :, P].bitcast(I32)).then_inc(targets_done, 1)
                    wait(dve, h_mm, t - 1)
                    dve.tensor_copy(xT[:, i % 2, :], ps_x[:, 0:SLOTS]).then_inc(xT_done, 1)

                def leave(tt, i, before):
                    t, s = N * tt + i, i % 2
                    dve.wait_ge(y_mm, t + 1)
                    if before is not None:
                        wait_for_output(dve, tt - 1, i, before)
                    dve.tensor_copy(y[:, i].rearrange("p a n -> p (a n)"), ps_y[s][:, 0:SLOTS]
                                    ).then_inc(y_done, 1)

                def step(tt, i, shared):
                    nt, ni = follow(tt, i, 1)
                    if inside(N * nt + ni, ETILES):
                        turn(nt, ni, shared)
                    before = follow(tt, i, -1)
                    if inside(N * before[0] + before[1], ETILES):
                        if not shared or (isinstance(tt, int) and N * before[0] + before[1] < ROUTED):
                            leave(*before, None)
                        else:
                            leave(*before, not isinstance(before[0], int) or before[0] - 1 >= ROUTED_TURNS)

                turn(0, 0, False)
                each_tile(dve, step)
                leave(TURNS - 1, N - 1, True)


def combine(nc, L, w):
    with ExitStack() as ctx:
        sb, psum, sem = alloc(nc, ctx)
        S = lambda name: L.semaphore(f"e_{name}")
        N = 4
        TURNS = BATCH // N
        x, s_in, shared, first, second = (
            sb(f"e_{n}", [P, N, TPB, P]) for n in ("x", "s", "shared", "first", "second"))
        ffn, silu, out, sT = (sb(f"e_{n}", [P, N, TPB, P]) for n in ("ffn", "silu", "out", "sT"))
        ps_t = [psum(f"e_ps_t{i}") for i in range(N)]
        ps_s = [psum(f"e_ps_s{i}") for i in range(N)]
        batch_in = [S(f"batch_in{i}") for i in range(N)]
        out_out = [S(f"out_out{i}") for i in range(N)]
        summed, gated, stored, partial, product = (
            S("summed"), S("gated"), S("stored"), S("partial"), S("product"))
        turned, sT_done, s_mm = S("turned"), S("sT"), S("s_mm")
        view = lambda a: a.rearrange("(b t p) n -> b p t n", t=TPB, p=P)
        loads = [(x, L.x_in), (s_in, L.s), (shared, L.shared), (first, L.routed[0:TOKENS, :]),
                 (second, L.routed[TOKENS:2 * TOKENS, :])]
        LOADS = len(loads)

        def each_batch(eng, step):
            def body(bb):
                for i in range(N):
                    step(bb, i)
            loop(eng, TURNS, body)

        with nc.Block() as block:
            @block.sync
            def _(sp):
                def step(bb, i):
                    b = N * bb + i
                    wait(sp, stored, b - N + 1)
                    wait(sp, turned, b - N + 1)
                    for dst, src in loads:
                        sp.dma_start(dst[:, i], view(src)[bass.ds(b, 1)].rearrange("o p t n -> (o p) t n")
                                     ).then_inc(batch_in[i], 16)

                each_batch(sp, step)

            @block.scalar
            def _(act):
                def step(bb, i):
                    b = N * bb + i
                    act.wait_ge(summed, b + 1)
                    wait(act, stored, b - N + 1)
                    act.activation(silu[:, i], ffn[:, i], ACT.Silu).then_inc(gated, 1)
                    act.wait_ge(stored, b + 1)
                    act.dma_start(view(L.x_out)[bass.ds(b, 1)].rearrange("o p t n -> (o p) t n"), out[:, i]
                                  ).then_inc(out_out[i], 16)

                each_batch(act, step)
                for i in range(N):
                    act.wait_ge(out_out[i], 16 * TURNS)

            @block.tensor
            def _(pe):
                def turn(bb, i):
                    b = N * bb + i
                    pe.wait_ge(batch_in[i], 16 * LOADS * (bb + 1))
                    wait(pe, sT_done, b - N + 1)
                    for t in range(TPB):
                        mm = pe.transpose(ps_t[i][:, t * P:(t + 1) * P], s_in[:, i, t], w["ident"][:, :])
                    mm.then_inc(turned, 1)

                def step(bb, i):
                    b = N * bb + i
                    if isinstance(bb, int) and bb == 0 and i == 0:
                        turn(0, 0)
                    if not (isinstance(bb, int) and bb == TURNS - 1 and i == N - 1):
                        turn(bb + (i + 1) // N, (i + 1) % N)
                    pe.wait_ge(sT_done, b + 1)
                    wait(pe, stored, b - N + 1)
                    for t in range(TPB):
                        columns = ps_s[i][:, t * P:(t + 1) * P]
                        pe.matmul(columns, sT[:, i, t], w["cprojT"][:, :], start=True, stop=False)
                        mm = pe.matmul(columns, w["ones"][0:1, :], w["bs1"][:, :], start=False, stop=True)
                    mm.then_inc(s_mm, 1)

                each_batch(pe, step)

            @block.vector
            def _(dve):
                def add_up(bb, i):
                    b = N * bb + i
                    dve.wait_ge(batch_in[i], 16 * LOADS * (bb + 1))
                    wait(dve, gated, b - N + 1)
                    dve.tensor_scalar(ffn[:, i], shared[:, i], 0.1, None, ALU.mult).then_inc(partial, 1)
                    PARTIALS = 1 + TPB
                    for k, (chosen, done) in enumerate(((first, partial), (second, summed))):
                        dve.wait_ge(partial, PARTIALS * b + (1, PARTIALS)[k])
                        for t in range(TPB):
                            gate = w["gate"][:, k, bass.ds(TPB * b + t, 1)]
                            ins = dve.scalar_tensor_tensor(ffn[:, i, t], chosen[:, i, t], gate, ffn[:, i, t],
                                                           ALU.mult, ALU.add)
                            if k == 0 or t == TPB - 1:
                                ins.then_inc(done, 1)
                    dve.wait_ge(turned, b + 1)
                    wait(dve, s_mm, b - N + 1)
                    dve.tensor_copy(sT[:, i].rearrange("p t n -> p (t n)"), ps_t[i][:, :]).then_inc(sT_done, 1)

                def finish(bb, i):
                    b = N * bb + i
                    dve.wait_ge(gated, b + 1)
                    wait(dve, out_out[i], 16 * bb)
                    dve.wait_ge(s_mm, b + 1)
                    s = ps_s[i][:, :].rearrange("p (t n) -> p t n", n=P)
                    dve.tensor_tensor(out[:, i], s, silu[:, i], ALU.mult).then_inc(product, 1)
                    dve.wait_ge(product, b + 1)
                    dve.tensor_tensor(out[:, i], out[:, i], x[:, i], ALU.add).then_inc(stored, 1)

                def step(bb, i):
                    if isinstance(bb, int) and bb == 0 and i == 0:
                        add_up(0, 0)
                    if not (isinstance(bb, int) and bb == TURNS - 1 and i == N - 1):
                        add_up(bb + (i + 1) // N, (i + 1) % N)
                    finish(bb, i)

                each_batch(dve, step)


def attend(nc, L, w):
    l = L.index
    UNITS = BATCH * GROUPS
    STEPS = UNITS * TPB
    PER_BATCH = GROUPS * TPB
    ROW = L.head_rows
    RUNS = [part_runs([pair[i] for pair in L.products]) for i in range(2)]
    USED = len(L.products) * ROW
    causal = l == 1
    LEAD = 2 * TPB if causal else 2 * TPB - 1
    BANKS = 3
    TURN = GH
    TURN_AT, LOAD_AT = (0, 0) if causal else (1, 2)
    LAG = 2 if causal else 1
    PROBS = 4
    with ExitStack() as ctx:
        sb, psum, sem = alloc(nc, ctx)
        S = lambda name: L.semaphore(f"d_{name}")
        q = [sb(f"d{l}_q{g}", [P, GH, SEQ], F32R) for g in range(GROUPS)]
        k = [sb(f"d{l}_k{g}", [P, GH, SEQ], F32R) for g in range(GROUPS)]
        v = sb(f"d{l}_v", [P, GROUPS, TPB, GH, VC])
        probs = sb(f"d{l}_probs", [P, PROBS, GH, SEQ])
        masked_scores = sb(f"d{l}_masked", [P, BANKS, SEQ])
        maxima = sb(f"d{l}_maxima", [P, GH, TPB])
        m_parts = sb(f"d{l}_m_parts", [P, 2, GH, TPB])
        mT = sb(f"d{l}_mT", [2 * GH * TPB, 2, P])
        o = sb(f"d{l}_o", [P, SEQ])
        inv = sb(f"d{l}_inv", [P, 2, TPB, GH])
        out = sb(f"d{l}_out", [P, TPB, P])
        ps_s = psum(f"d{l}_ps_s", 4)
        ps_m = [psum(f"d{l}_ps_m{i}") for i in range(BANKS)]
        ps_o = psum(f"d{l}_ps_o")

        qk_in = [S(f"qk_in{g}") for g in range(GROUPS)]
        m_in = [S(f"m_in{g}") for g in range(GROUPS)]
        out_out = S("out_out")
        cleared, filled, drained, m_hi, m_split = (
            S("cleared"), S("filled"), S("drained"), S("m_hi"), S("m_split"))
        s_mm, exps, pv, o_copied, o_inv = S("s_mm"), S("exps"), S("pv"), S("o_copied"), S("o_inv")
        minus_one, o_zero, selected = S("minus_one"), S("o_zero"), S("selected")
        tile_rows = sb(f"d{l}_rows", [P, 2, 2, ROW_W])
        targets = sb(f"d{l}_targets", [P, 2, TILES], I32)
        index = sb(f"d{l}_index", [P, 2, 2], I32)
        row_in = [S(f"row_in{i}") for i in range(2)]
        row_out = [L.queue_semaphore(f"row_out{i}") for i in range(2)]
        index_done = S("index")
        xn_view = L.xn.rearrange("(t p) n -> t p n", p=P)
        numbered, rows_zero, targeted = S("numbered"), S("rows_zero"), S("targeted")
        dispatched = S("dispatched")
        dispatch_pool, dispatch_act, dispatch_pe, dispatch_dve = dispatch(L, w, sb, ps_m[0], ps_m[1], dispatched)
        LOADS = len(RUNS[0]) + len(RUNS[1]) + 1

        out_view = L.s.rearrange("(b t p) n -> b p t n", t=TPB, p=P)
        v_view = L.v.rearrange("(b p) (t h c) -> b p t h c", p=P, t=TPB, h=HEADS)

        def at(b, offset):
            turns, rest = divmod(offset, PER_BATCH)
            b = b + turns
            return b, rest // TPB, rest % TPB, PER_BATCH * b + rest, GROUPS * b + rest // TPB

        def all_steps(eng, step):
            for n in range(-LEAD, 0):
                step(0, n)
            def body(b):
                for n in range(PER_BATCH):
                    step(b, n)
            loop(eng, BATCH, body)
            for n in range(TPB):
                step(BATCH, n)

        items = {}
        for n in range(-LEAD, STEPS + TPB):
            for h in range(GH):
                if 0 <= n + LEAD < STEPS:
                    items[n, h] = len(items)
            if (n % TPB == TURN_AT and 0 <= n // TPB + 1 < UNITS) or (n % TPB == LAG + 1 and 0 <= n // TPB - 1 < UNITS):
                items[n, TURN] = len(items)
        PER_LOOP = items[2 * PER_BATCH, 0] - items[PER_BATCH, 0]
        assert PER_LOOP % BANKS == 0

        def item(b, offset, j):
            if isinstance(b, int):
                number = items[PER_BATCH * b + offset, j]
                return number, number % BANKS
            number = items[PER_BATCH + offset, j]
            return PER_LOOP * (b - 1) + number, number % BANKS

        def narrow(kb):
            return causal and kb >= TPB // 2

        def pair_scores(kb, pair):
            at, apart = 2 * pair * SEQ, SEQ
            if narrow(kb):
                at, apart = (2 * (kb % 2) + pair) * SEQ, SEQ // 2
            return ps_s[:, at:at + 2 * apart].rearrange("p (h n) -> p h n", h=2)[:, :, 0:SEQ - first(kb)]

        def exps_before(kb, n, pair):
            if not causal:
                return 2 * n + pair - 1
            return 2 * n + {0: (-2, 0), 1: (-1, 0), 2: (-1, -1), 3: (-2, -2)}[kb][pair]

        def width(qb):
            return (qb + 1) * P if causal else SEQ

        def first(kb):
            return kb * P if causal else 0

        with nc.Block() as block:
            @block.sync
            def _(sp):
                def load(b, g):
                    u = GROUPS * b + g
                    wait(sp, pv, TPB * (u - GROUPS + 1))
                    tokens = bass.ds(b * SEQ, SEQ)
                    for dst, src, runs in ((q, L.q, RUNS[0]), (k, L.k, RUNS[1])):
                        for at, part, count in runs:
                            rows = src[g * GH:(g + 1) * GH, part:part + count, :, tokens]
                            sp.dma_start(dst[g][at * ROW:(at + count) * ROW, :, :].bitcast(F32),
                                         rows.rearrange("h i r t -> (i r) h t")).then_inc(qk_in[g], 16)
                    sp.dma_start(v[:, g], v_view[bass.ds(b, 1), :, :, g * GH:(g + 1) * GH, :].rearrange(
                        "o p t h c -> (o p) t (h c)")).then_inc(qk_in[g], 16)

                def step(b, offset):
                    _, g, kb, _, u = at(b, offset)
                    if kb == 0 and inside(u, UNITS):
                        if isinstance(u, int) and u == 0:
                            sp.wait_ge(rows_zero, 1)
                        half = (GROUPS // 2) * at(b, offset)[0] + g // 2
                        wait(sp, row_out[g % 2], 32 * half)
                        for c in range(2):
                            sp.dma_start(tile_rows[:, g % 2, c, 0:P],
                                         xn_view[bass.ds(u, 1)].rearrange("o p n -> (o p) n")
                                         ).then_inc(row_in[g % 2], 16)
                    if kb == TURN_AT and inside(u + 1, UNITS):
                        nb, ng, _, _, nu = at(b, offset + TPB)
                        sp.wait_ge(drained, item(b, offset, TURN)[0] + 1)
                        dst = q[ng][M_ROW:M_ROW + 2, :, :].bitcast(F32)
                        sp.dma_start(dst.rearrange("part h (t n) -> part (h t) n", n=P), mT[:, ng % 2, :]
                                     ).then_inc(m_in[ng], 16)
                    if kb == LOAD_AT and inside(at(b, offset + 3 * TPB)[4], UNITS) and not (
                            isinstance(u, int) and u < 0):
                        load(*at(b, offset + 3 * TPB)[0:2])
                    if kb == TPB - 1:
                        ob, og, _, _, ou = at(b, offset - TPB)
                        if og == GROUPS - 1 and inside(ou, UNITS):
                            sp.wait_ge(drained, item(b, offset - TPB + LAG + 2, TURN)[0] + 1)
                            sp.dma_start(out_view[bass.ds(ob, 1)].rearrange("o p t n -> (o p) t n"),
                                         out[:, :, :]).then_inc(out_out, 16)

                for g in range(3):
                    if USED < M_ROW:
                        sp.wait_ge(cleared, 2 * (1, 2, GROUPS)[g])
                    load(0, g)
                all_steps(sp, step)
                sp.wait_ge(out_out, 16 * BATCH)

            @block.gpsimd
            def _(pool):
                dispatch_pool(pool)
                if USED < M_ROW:
                    for g in range(GROUPS):
                        pool.memset(k[g][0:M_ROW, :, :].bitcast(F32), 0.0).then_inc(cleared, 1)
                        pool.memset(q[g][0:M_ROW, :, :].bitcast(F32), 0.0).then_inc(cleared, 1)
                pool.memset(tile_rows[:, :, :, :], 0.0).then_inc(rows_zero, 1)
                pool.iota(targets[:, :, :], pattern=[[TOKENS, 2], [P, TILES]], base=0, channel_multiplier=1
                          ).then_inc(numbered, 1)
                pool.wait_ge(rows_zero, 1)
                pool.wait_ge(numbered, 1)
                for g in range(GROUPS):
                    pool.memset(k[g][M_ROW:M_ROW + 2, :, :].bitcast(F32), -1.0).then_inc(minus_one, 1)
                pool.wait_ge(minus_one, GROUPS)
                pool.wait_ge(dispatched, 1)

                def scatter(b, g, choice):
                    t, i = GROUPS * b + g, g % 2
                    turn = (GROUPS // 2) * b + g // 2
                    if choice == 0:
                        wait(pool, row_out[i], 32 * turn)
                    pool.tensor_copy(index[:, i, choice:choice + 1], w["slot"][:, choice, bass.ds(t, 1)]
                                     ).then_inc(index_done, 1)
                    pool.tensor_copy(tile_rows[:, i, choice, P:P + 1].bitcast(I32),
                                     targets[:, choice, bass.ds(t, 1)]).then_inc(targeted, 1)
                    carried(pool, (index_done, 1), (index_done, 2 * t + choice + 1),
                            (targeted, 2 * t + choice + 1), (row_in[i], 32 * (turn + 1)))
                    pool.indirect_dma_start(
                        L.slots_in, bass.IndirectOffsetOnAxis(ap=index[:, i, choice:choice + 1], axis=0),
                        tile_rows[:, i, choice, :], None).then_inc(row_out[i], 16)

                def step(b, offset):
                    nb, g, kb, n, u = at(b, offset)
                    if causal and inside(n, STEPS):
                        carried(pool, (exps, 2), (exps, 2 * n + 2))
                        diagonal = probs[:, offset % PROBS, :, 0:P]
                        pool.affine_select(out=diagonal, in_=diagonal, compare_op=ALU.is_ge, fill=0.0,
                                           base=0, pattern=[[0, GH], [1, P]], channel_multiplier=-1
                                           ).then_inc(selected, 1)
                    if kb >= TPB - 2 and inside(u, UNITS):
                        scatter(nb, g, kb - (TPB - 2))

                all_steps(pool, step)
                for i in range(2):
                    pool.wait_ge(row_out[i], 16 * TILES)

            @block.scalar
            def _(act):
                dispatch_act(act)

                def step(b, offset):
                    _, _, kb, n, u = at(b, offset)
                    for pair in range(2):
                        if inside(n, STEPS):
                            act.wait_ge(s_mm, 2 * n + pair + 1)
                            wait(act, pv, n - PROBS + 1)
                            wide = SEQ - first(kb)
                            act.activation(
                                probs[:, offset % PROBS, 2 * pair:2 * pair + 2, 0:wide],
                                pair_scores(kb, pair),
                                ACT.Exp, scale=L.scale).then_inc(exps, 1)
                        if pair == 0 and kb == LAG and inside(u - 1, UNITS):
                            act.wait_ge(pv, TPB * u)
                            if inside(u - 2, UNITS):
                                act.wait_ge(filled, item(b, offset + 1 - TPB, TURN)[0] + 1)
                            act.activation(o[:, :], ps_o[:, :], ACT.Copy).then_inc(o_copied, 1)

                all_steps(act, step)

            @block.vector
            def _(dve):
                dispatch_dve(dve)
                dve.memset(ps_o[:, :], 0.0).then_inc(o_zero, 1)

                def step(b, offset):
                    _, g, kb, n, u = at(b, offset)
                    mb, mg, qb, m, mu = at(b, offset + LEAD)
                    for h in range(GH):
                        if inside(m, STEPS):
                            number, r = item(b, offset, h)
                            if qb == 0 and h == 0:
                                wait(dve, m_split, mu)
                            if causal:
                                carried(dve, (filled, 1), (filled, number + 1))
                                dve.tensor_tensor_reduce(
                                    masked_scores[:, r, 0:width(qb)], ps_m[r][:, 0:width(qb)],
                                    w["mask"][:, SEQ - width(qb):SEQ], 1.0, MASKED,
                                    ALU.add, ALU.max, maxima[:, h, qb:qb + 1]).then_inc(drained, 1)
                            else:
                                dve.wait_ge(filled, number + 1)
                                dve.tensor_reduce(maxima[:, h, qb:qb + 1], ps_m[r][:, :], AX.X, ALU.max
                                                  ).then_inc(drained, 1)
                    if qb == TPB - 1 and inside(m, STEPS):
                        dve.wait_ge(drained, item(b, offset, GH - 1)[0] + 1)
                        dve.tensor_copy(m_parts[:, 0].bitcast(F32R), maxima[:, :, :]).then_inc(m_hi, 1)
                        dve.wait_ge(m_hi, mu + 1)
                        dve.tensor_tensor(m_parts[:, 1].bitcast(F32R), maxima[:, :, :], m_parts[:, 0],
                                          ALU.subtract).then_inc(m_split, 1)
                    if kb == TURN_AT and inside(u + 1, UNITS):
                        ng = at(b, offset + TPB)[1]
                        number, r = item(b, offset, TURN)
                        dve.wait_ge(filled, number + 1)
                        before = at(b, offset - TPB)
                        if inside(before[4], UNITS):
                            dve.wait_ge(m_in[before[1]], 16 * (before[0] + 1))
                        dve.tensor_copy(mT[:, ng % 2, :], ps_m[r][0:2 * GH * TPB, 0:P]).then_inc(drained, 1)
                    if kb == LAG + 1 and inside(u - 1, UNITS):
                        ob, og, _, _, ou = at(b, offset - TPB)
                        number, r = item(b, offset, TURN)
                        dve.wait_ge(filled, number + 1)
                        ov = ps_m[r][:, :].rearrange("p (t h c) -> p t h c", t=TPB, h=GH)
                        dve.reciprocal(inv[:, og % 2], ov[:, :, :, HD]).then_inc(o_inv, 1)
                        if og == 0:
                            wait(dve, out_out, 16 * ob)
                        dve.wait_ge(o_inv, ou + 1)
                        dve.tensor_tensor(
                            out[:, :, og * GH * HD:(og + 1) * GH * HD].rearrange("p t (h c) -> p t h c", h=GH),
                            ov[:, :, :, 0:HD], inv[:, og % 2].unsqueeze(3).to_broadcast([P, TPB, GH, HD]),
                            ALU.mult).then_inc(drained, 1)

                all_steps(dve, step)

            @block.tensor
            def _(pe):
                dispatch_pe(pe)
                pe.wait_ge(minus_one, GROUPS)
                pe.wait_ge(o_zero, 1)
                pe.wait_ge(dispatched, 1)

                def scores(b, offset, pair):
                    nb, g, kb, n, u = at(b, offset)
                    if not inside(n, STEPS):
                        return
                    if kb == 0 and pair == 0:
                        pe.wait_ge(m_in[g], 16 * (nb + 1))
                    wait(pe, exps, exps_before(kb, n, pair))
                    for i in range(2):
                        h = 2 * pair + i
                        out_ps = pair_scores(kb, pair)[:, i]
                        mm = pe.matmul(out_ps, k[g][0:M_ROW + 2, h, kb * P:(kb + 1) * P],
                                       q[g][0:M_ROW + 2, h, first(kb):SEQ], start=True, stop=True)
                    mm.then_inc(s_mm, 1)

                def next_bank(b, offset, j):
                    number, r = item(b, offset, j)
                    wait(pe, drained, number - BANKS + 1)
                    return ps_m[r]

                def for_maxima(b, offset, h):
                    mb, g, qb, m, mu = at(b, offset + LEAD)
                    if not inside(m, STEPS):
                        return
                    if qb == 0 and h == 0:
                        pe.wait_ge(qk_in[g], 16 * LOADS * (mb + 1))
                    bank = next_bank(b, offset, h)
                    wide = width(qb)
                    mm = pe.matmul(bank[:, 0:wide], q[g][0:M_ROW, h, qb * P:(qb + 1) * P],
                                   k[g][0:M_ROW, h, 0:wide], start=True, stop=True)
                    mm.then_inc(filled, 1)

                def with_v(b, offset):
                    _, g, kb, n, u = at(b, offset)
                    if not inside(n, STEPS):
                        return
                    if causal:
                        pe.wait_ge(selected, n + 1)
                    else:
                        pe.wait_ge(exps, 2 * n + 2)
                    if kb == 0:
                        wait(pe, o_copied, u)
                    for h in range(GH):
                        mm = pe.matmul(ps_o[32 * h:32 * h + VC, first(kb):SEQ], v[:, g, kb, h, :],
                                       probs[:, offset % PROBS, h, 0:SEQ - first(kb)],
                                       start=(kb == 0), stop=(kb == TPB - 1), tile_position=(0, 32 * h))
                    mm.then_inc(pv, 1)

                def step(b, offset):
                    _, g, kb, n, u = at(b, offset)
                    scores(b, offset, 0)
                    for_maxima(b, offset, 0)
                    scores(b, offset, 1)
                    for_maxima(b, offset, 1)
                    for_maxima(b, offset, 2)
                    with_v(b, offset - LAG)
                    for_maxima(b, offset, 3)
                    if kb == TURN_AT and inside(u + 1, UNITS):
                        pe.wait_ge(m_split, u + 2)
                        pe.transpose(next_bank(b, offset, TURN)[0:2 * GH * TPB, 0:P],
                                     m_parts[:, :, :, :].rearrange("p a h t -> p (a h t)"),
                                     w["ident"][:, :]).then_inc(filled, 1)
                    if kb == LAG + 1 and inside(u - 1, UNITS):
                        pe.wait_ge(o_copied, u)
                        bank = next_bank(b, offset, TURN)
                        for t in range(TPB):
                            mm = pe.transpose(bank[:, t * P:(t + 1) * P], o[:, t * P:(t + 1) * P], w["ident"][:, :])
                        mm.then_inc(filled, 1)

                all_steps(pe, step)


def build(nc, d, out):
    with ExitStack() as ctx:
        sb, _, _ = alloc(nc, ctx)
        w = {n: sb(n, [P, P]) for n in ("ident", "tri", "wq0", "wk0", "wv0", "wv1", "wqk", "wqkr", "cprojT", "ones")}
        for n in ("wr0", "wr1"):
            w[n] = sb(n, [P, E])
        for n in ("bq0", "bk0", "bqk", "eps"):
            w[n] = sb(n, [P, 1])
        for n in ("bv0", "bv1", "bs1"):
            w[n] = sb(n, [1, P])
        for n in ("waq", "wak", "wbk", "cos", "sin"):
            w[n] = sb(n, [P, HEADS * LAT])
        for n in ("baq", "bak", "bbk"):
            w[n] = sb(n, [P, GROUPS])
        w["mask"] = sb("mask", [P, SEQ])
        w["logits"] = sb("logits", [P, TILES, E])
        w["gate"] = sb("gate", [P, 2, TILES])
        w["slot"] = sb("slot", [P, 2, TILES], I32)
        w["tile_f"] = sb("tile_f", [P, ROUTED])
        w["tile_expert"] = sb("tile_expert", [P, ROUTED], I32)

        def scratch(name, shape):
            return nc.dram_tensor(name, shape, F32, kind="Internal").ap()

        layers, semaphores = [], {}
        for l in range(2):
            L = Layer(nc, semaphores)
            L.index = l
            rows = (HD, LAT)[l]
            L.head_rows = rows
            L.products = ([(0, 0), (1, 0), (0, 1), (1, 1)], [(0, 0), (1, 0), (0, 1)])[l]
            L.scale = float(rows) ** -0.5
            L.q, L.k = (scratch(f"{n}{l}", [HEADS, 2, rows, TOKENS]) for n in "qk")
            L.v = scratch(f"v{l}", [BATCH * P, TPB * HEADS * VC])
            L.slots_in, L.routed = (scratch(f"slots_in{l}", [ROUTED_ROWS, ROW_W]),
                                    scratch(f"routed{l}", [2 * TOKENS + ROUTED_ROWS, P]))
            L.xn, L.shared = scratch(f"xn{l}", [TOKENS, P]), scratch(f"shared{l}", [TOKENS, P])
            L.s = scratch(f"s{l}", [TOKENS, P])
            L.x_in = d["x"] if l == 0 else layers[0].x_out
            L.x_out = scratch("x1", [TOKENS, P]) if l == 0 else out
            L.wr, L.wv, L.bv = w[f"wr{l}"], w[f"wv{l}"], w[f"bv{l}"]
            L.w1, L.w2, L.b2, L.up_width = d[f"up{l}"], d[f"down{l}"], d["b2"], (F, F + FB)[l]
            layers.append(L)

        load_constants(nc, layers[0], d, w)
        for L in layers:
            if L.index > 0:
                clear(nc, semaphores)
            prepare(nc, L, layers[L.index - 1] if L.index > 0 else None, w)
            attend(nc, L, w)
            experts(nc, L, layers[1] if L.index == 0 else None, w)
        combine(nc, layers[-1], w)


def layout(i):
    a = {n: np.ascontiguousarray(x) for n, x in i.items()}
    col = lambda x: x.reshape(-1, 1)
    row = lambda x: x.reshape(1, -1)
    d = {"x": a["L0_attn_x"].reshape(TOKENS, P)}
    d["wqT"], d["wkT"], d["wv0"] = a["L0_attn_Wq"].T, a["L0_attn_Wk"].T, a["L0_attn_Wv"]
    d["bq"], d["bk"], d["bv0"] = col(a["L0_attn_bq"]), col(a["L0_attn_bk"]), row(a["L0_attn_bv"])
    d["wpx"] = np.tile(a["L0_attn_Wp"], (HEADS, HEADS))
    d["wr0"], d["wr1"] = a["L0_ffn_router_w"], a["L1_ffn_Wg"]
    d["up0"] = np.concatenate([a["L0_ffn_routed_up"], a["L0_ffn_shared_up"]])
    d["down0"] = np.concatenate([a["L0_ffn_routed_down"], a["L0_ffn_shared_down"]])
    d["cq"], d["ck"], d["cv"] = a["L1_attn_c_attn_w"].reshape(3, P, P)
    d["cqb"], d["ckb"], d["cvb"] = a["L1_attn_c_attn_b"].reshape(3, P, 1)
    d["q2lx"] = np.tile(a["L1_attn_q2l_w"].T, (HEADS, HEADS))
    d["kv2lx"] = np.tile(a["L1_attn_kv2l_w"].T, (HEADS, HEADS))
    d["q2lbx"], d["kv2lbx"] = col(np.tile(a["L1_attn_q2l_b"], GH)), col(np.tile(a["L1_attn_kv2l_b"], GH))
    d["kv2lrep"] = np.tile(a["L1_attn_kv2l_w"], (1, HEADS))
    d["kv2lb"] = col(a["L1_attn_kv2l_b"])
    d["l2orep"] = np.tile(a["L1_attn_l2o_w"].T, (1, HEADS))
    d["l2obx"] = col(np.tile(a["L1_attn_l2o_b"], HEADS))
    d["wqkx"] = np.tile(a["L1_attn_wqk_w"].T, (GH, GH))
    d["bqk"] = col(np.tile(a["L1_attn_wqk_b"], GH))
    d["cprojT"], d["cprojb"] = a["L1_attn_cproj_w"].T, row(a["L1_attn_cproj_b"])
    b1 = np.concatenate([a["L1_ffn_b1"], row(a["L1_ffn_bs1"])]).reshape(E + 1, P, FB)
    d["up1"] = np.concatenate([np.concatenate([a["L1_ffn_W1"], a["L1_ffn_Ws1"][None]]), b1], axis=2)
    d["down1"] = np.concatenate([a["L1_ffn_W2"], a["L1_ffn_Ws2"][None]])
    d["b2"] = np.concatenate([a["L1_ffn_b2"], row(a["L1_ffn_bs2"])])

    n = np.arange(P)
    d["ident"] = np.eye(P)
    d["tri"] = n[:, None] < n[None, :]
    d["mask8"] = n[:, None] // HD == n[None, :] // HD
    d["mask32"] = n[:, None] // HD == np.arange(HEADS * LAT)[None, :] // LAT
    d["mask32x32"] = n[:, None] // LAT == n[None, :] // LAT
    d["rot"] = ((n[:, None] == n[None, :] - 1) * (n[None, :] % 2) * 1.0
                - (n[:, None] == n[None, :] + 1) * (1 - n[None, :] % 2))
    steps = np.arange(0, LAT, 2, dtype=np.float32) / np.float32(LAT)
    freq = np.float32(1.0) / np.power(np.float32(10000.0), steps)
    angle = np.repeat(np.outer(np.arange(SEQ, dtype=np.float32), freq), 2, axis=1).T
    d["cos"], d["sin"] = np.tile(np.cos(angle), (GH, 1)), np.tile(np.sin(angle), (GH, 1))
    return {name: np.ascontiguousarray(x, dtype=np.float32) for name, x in d.items()}


def kernel(**inputs):
    import concourse.bacc as bacc
    from concourse.bass_utils import run_bass_kernel_spmd

    nc = bacc.Bacc("TRN2", target_bir_lowering=False, num_devices=1)
    arrays = {f"in_{name}": x for name, x in layout(inputs).items()}
    d = {name: nc.dram_tensor(name, x.shape, F32, kind="ExternalInput").ap() for name, x in arrays.items()}
    out = nc.dram_tensor("out", [TOKENS, P], F32, kind="ExternalOutput").ap()
    build(nc, {name.removeprefix("in_"): ap for name, ap in d.items()}, out)
    r = run_bass_kernel_spmd(nc, [arrays], core_ids=[0])
    return r.results[0]["out"].reshape(BATCH, SEQ, P)
```
